# Optimizing a Trainium2 kernel written in Bass

```python
import numpy as np
import jax
import jax.numpy as jnp

def _softmax(x, axis=-1):
    return jax.nn.softmax(x, axis=axis)
def _gelu(x):
    return jax.nn.gelu(x, approximate=True)
def _silu(x):
    return jax.nn.silu(x)
def _sigmoid(x):
    return jax.nn.sigmoid(x)
def _layernorm(x, axis=-1, eps=1e-5):
    m = jnp.mean(x, axis=axis, keepdims=True)
    v = jnp.var(x, axis=axis, keepdims=True)
    return (x - m) / jnp.sqrt(v + eps)
def _scatter_add(tgt, idx, src, axis=0):
    return tgt.at[idx].add(src)
def _segment_sum(src, seg, n):
    return jax.ops.segment_sum(src, seg, n)

kernel_name = 'mk_conv_preact_d2_conv_nchw384_ef7619'

def setup_inputs(seed: int = 0):
    np.random.seed(seed)
    _w = jnp.asarray
    def _rec_inputs():
        import jax
        import jax.numpy as jnp
        _gk = jax.random.key(seed)
        x = -0.0005963 + 1.001 * jax.random.normal(jax.random.fold_in(_gk, 1), (8, 384, 32, 32), jnp.float32)
        return x
    x = _rec_inputs()
    def _L0_conv_setup():
        import jax, jax.numpy as jnp
        import numpy as np
        B, C, H, W = (8, 384, 32, 32)
        D_STATE, D_CONV, EXPAND = (16, 3, 2)
        D_INNER = EXPAND * C
        DT_RANK = -(-C // 16)
        key = jax.random.key(seed)
        ks = jax.random.split(key, 12)

        def n(k, shape, s=0.02):
            return jax.random.normal(k, shape, jnp.float32) * s
        inp = {'x': jax.random.normal(ks[0], (B, C, H, W), jnp.float32), 'ln_w': jnp.ones((C,), jnp.float32), 'ln_b': jnp.zeros((C,), jnp.float32), 'in_proj_w': n(ks[1], (2 * D_INNER, C)), 'conv_w': n(ks[2], (D_INNER, D_CONV), 0.1), 'conv_b': jnp.zeros((D_INNER,), jnp.float32), 'x_proj_w': n(ks[3], (DT_RANK + 2 * D_STATE, D_INNER)), 'dt_proj_w': n(ks[4], (D_INNER, DT_RANK), 0.1), 'dt_proj_b': jnp.full((D_INNER,), float(np.log(np.expm1(0.01))), jnp.float32), 'A_log': jnp.log(jnp.tile(jnp.arange(1, D_STATE + 1, dtype=jnp.float32), (D_INNER, 1))), 'D': jnp.ones((D_INNER,), jnp.float32), 'out_proj_w': n(ks[5], (C, D_INNER)), 'mlp_w1': n(ks[6], (4 * C, C)), 'mlp_b1': jnp.zeros((4 * C,), jnp.float32), 'mlp_w2': n(ks[7], (C, 4 * C)), 'mlp_b2': jnp.zeros((C,), jnp.float32)}
        return inp
    _L0_conv_all = _L0_conv_setup()
    _L0_conv_in = {k: v for k, v in _L0_conv_all.items() if k in ('ln_w', 'ln_b', 'in_proj_w', 'conv_w', 'conv_b', 'x_proj_w', 'dt_proj_w', 'dt_proj_b', 'A_log', 'D', 'out_proj_w', 'mlp_w1', 'mlp_b1', 'mlp_w2', 'mlp_b2', )}
    del _L0_conv_all

    def _L1_conv_setup():
        import jax, jax.numpy as jnp
        import numpy as np
        B, C, H, W = (32, 384, 28, 28)
        E, HID, K = (4, 384, 2)
        key = jax.random.key(seed)
        ks = jax.random.split(key, 5)
        x = jax.random.normal(ks[0], (B, C, H, W), jnp.float32)
        gate_w = jax.random.normal(ks[1], (C, E), jnp.float32) * 0.02
        gate_b = jnp.zeros((E,), jnp.float32)
        w1 = jax.random.normal(ks[2], (E, HID, C), jnp.float32) * 0.02
        b1 = jnp.zeros((E, HID), jnp.float32)
        w2 = jax.random.normal(ks[3], (E, C, HID), jnp.float32) * 0.02
        b2 = jnp.zeros((E, C), jnp.float32)
        return {'x': x, 'gate_w': gate_w, 'gate_b': gate_b, 'w1': w1, 'b1': b1, 'w2': w2, 'b2': b2}
    _L1_conv_all = _L1_conv_setup()
    _L1_conv_in = {k: v for k, v in _L1_conv_all.items() if k in ('gate_w', 'gate_b', 'w1', 'b1', 'w2', 'b2', )}
    del _L1_conv_all

    return {
        "x": x,
        "L0_conv_ln_w": _L0_conv_in["ln_w"],
        "L0_conv_ln_b": _L0_conv_in["ln_b"],
        "L0_conv_in_proj_w": _L0_conv_in["in_proj_w"],
        "L0_conv_conv_w": _L0_conv_in["conv_w"],
        "L0_conv_conv_b": _L0_conv_in["conv_b"],
        "L0_conv_x_proj_w": _L0_conv_in["x_proj_w"],
        "L0_conv_dt_proj_w": _L0_conv_in["dt_proj_w"],
        "L0_conv_dt_proj_b": _L0_conv_in["dt_proj_b"],
        "L0_conv_A_log": _L0_conv_in["A_log"],
        "L0_conv_D": _L0_conv_in["D"],
        "L0_conv_out_proj_w": _L0_conv_in["out_proj_w"],
        "L0_conv_mlp_w1": _L0_conv_in["mlp_w1"],
        "L0_conv_mlp_b1": _L0_conv_in["mlp_b1"],
        "L0_conv_mlp_w2": _L0_conv_in["mlp_w2"],
        "L0_conv_mlp_b2": _L0_conv_in["mlp_b2"],
        "L1_conv_gate_w": _L1_conv_in["gate_w"],
        "L1_conv_gate_b": _L1_conv_in["gate_b"],
        "L1_conv_w1": _L1_conv_in["w1"],
        "L1_conv_b1": _L1_conv_in["b1"],
        "L1_conv_w2": _L1_conv_in["w2"],
        "L1_conv_b2": _L1_conv_in["b2"],
    }

def reference(x, L0_conv_ln_w, L0_conv_ln_b, L0_conv_in_proj_w, L0_conv_conv_w, L0_conv_conv_b, L0_conv_x_proj_w, L0_conv_dt_proj_w, L0_conv_dt_proj_b, L0_conv_A_log, L0_conv_D, L0_conv_out_proj_w, L0_conv_mlp_w1, L0_conv_mlp_b1, L0_conv_mlp_w2, L0_conv_mlp_b2, L1_conv_gate_w, L1_conv_gate_b, L1_conv_w1, L1_conv_b1, L1_conv_w2, L1_conv_b2):
    import jax
    import jax.numpy as jnp
    def _L0_conv_ref(x, ln_w, ln_b, in_proj_w, conv_w, conv_b, x_proj_w, dt_proj_w, dt_proj_b, A_log, D, out_proj_w, mlp_w1, mlp_b1, mlp_w2, mlp_b2):
        import jax, jax.numpy as jnp
        import numpy as np
        B, C, H, W = (8, 384, 32, 32)
        D_STATE, D_CONV, EXPAND = (16, 3, 2)
        D_INNER = EXPAND * C
        DT_RANK = -(-C // 16)
        b, c, h, w = x.shape
        L = h * w
        t = x.transpose(0, 2, 3, 1).reshape(b, L, c)
        mu = t.mean(-1, keepdims=True)
        var = t.var(-1, keepdims=True)
        t = (t - mu) * jax.lax.rsqrt(var + 1e-05) * ln_w + ln_b
        xz = t @ in_proj_w.T
        xm, z = jnp.split(xz, 2, axis=-1)
        K = conv_w.shape[-1]
        xp = jnp.pad(xm, ((0, 0), (K - 1, 0), (0, 0)))
        xc = sum((xp[:, k:k + L, :] * conv_w[:, k] for k in range(K))) + conv_b
        xc = jax.nn.silu(xc)
        dbc = xc @ x_proj_w.T
        dt_rank = dt_proj_w.shape[1]
        d_state = A_log.shape[1]
        dt, Bm, Cm = jnp.split(dbc, [dt_rank, dt_rank + d_state], axis=-1)
        dt = jax.nn.softplus(dt @ dt_proj_w.T + dt_proj_b)
        A = -jnp.exp(A_log)
        dA = jnp.exp(jnp.einsum('bld,dn->bldn', dt, A))
        dBu = jnp.einsum('bld,bln->bldn', dt * xc, Bm)

        def step(hst, inp):
            dA_t, dBu_t, C_t = inp
            hst = dA_t * hst + dBu_t
            return (hst, jnp.einsum('bdn,bn->bd', hst, C_t))
        h0 = jnp.zeros((b, dA.shape[2], d_state), x.dtype)
        _, ys = jax.lax.scan(step, h0, (dA.transpose(1, 0, 2, 3), dBu.transpose(1, 0, 2, 3), Cm.transpose(1, 0, 2)))
        y = ys.transpose(1, 0, 2) + xc * D
        y = y * jax.nn.silu(z)
        t = y @ out_proj_w.T
        t = jax.nn.gelu(t @ mlp_w1.T + mlp_b1, approximate=False) @ mlp_w2.T + mlp_b2
        return t.reshape(b, h, w, c).transpose(0, 3, 1, 2)

    def _L1_conv_ref(x, gate_w, gate_b, w1, b1, w2, b2):
        import jax, jax.numpy as jnp
        import numpy as np
        B, C, H, W = (32, 384, 28, 28)
        E, HID, K = (4, 384, 2)
        b, c, h, w = x.shape
        e = gate_b.shape[0]
        x_flat = x.transpose(0, 2, 3, 1).reshape(-1, c)
        scores = jax.nn.softmax(x_flat @ gate_w + gate_b, -1)
        top_v, top_i = jax.lax.top_k(scores, K)
        top_w = jax.nn.softmax(top_v, -1)
        wmap = top_w.T.reshape(K, b, h, w)
        present = (top_i[:, :, None] == jnp.arange(e)[None, None, :]).any(0)
        coef = jnp.einsum('ke,kbhw->ebhw', present.astype(x.dtype), wmap)
        hdn = jax.nn.relu(jnp.einsum('bchw,edc->ebdhw', x, w1) + b1[:, None, :, None, None])
        y = jnp.einsum('ebdhw,eod->ebohw', hdn, w2) + b2[:, None, :, None, None]
        out = jnp.einsum('ebohw,ebhw->bohw', y, coef)
        return out

    def _gn(v, G=32, eps=1e-5):
        B_, C_, H_, W_ = v.shape
        g = v.reshape(B_, G, C_ // G, H_, W_)
        m = jnp.mean(g, axis=(2, 3, 4), keepdims=True)
        s = jnp.var(g, axis=(2, 3, 4), keepdims=True)
        return ((g - m) / jnp.sqrt(s + eps)).reshape(v.shape)

    def _ln_c(v, eps=1e-6):
        m = jnp.mean(v, axis=1, keepdims=True)
        s = jnp.var(v, axis=1, keepdims=True)
        return (v - m) / jnp.sqrt(s + eps)

    def _ln_t(v, eps=1e-5):
        m = jnp.mean(v, axis=-1, keepdims=True)
        s = jnp.var(v, axis=-1, keepdims=True)
        return (v - m) / jnp.sqrt(s + eps)

    def _to_tokens(v):
        B_, C_, H_, W_ = v.shape
        return v.reshape(B_, C_, H_ * W_).transpose(0, 2, 1)
    def _from_tokens(t, like):
        B_, C_, H_, W_ = like.shape
        return t.transpose(0, 2, 1).reshape(B_, C_, H_, W_)

    x = x + _L0_conv_ref(_gn(x), L0_conv_ln_w, L0_conv_ln_b, L0_conv_in_proj_w, L0_conv_conv_w, L0_conv_conv_b, L0_conv_x_proj_w, L0_conv_dt_proj_w, L0_conv_dt_proj_b, L0_conv_A_log, L0_conv_D, L0_conv_out_proj_w, L0_conv_mlp_w1, L0_conv_mlp_b1, L0_conv_mlp_w2, L0_conv_mlp_b2)
    x = x + _L1_conv_ref(_gn(x), L1_conv_gate_w, L1_conv_gate_b, L1_conv_w1, L1_conv_b1, L1_conv_w2, L1_conv_b2)
    return x


_drawn_inputs = setup_inputs


def setup_inputs(seed=0):
    import zlib

    import numpy as np

    out = dict(_drawn_inputs(seed))
    spreads = {'L0_conv_ln_w': (1.0, 0.2),
     'L0_conv_ln_b': (0.0, 0.1),
     'L0_conv_conv_b': (0.0, 0.1),
     'L0_conv_dt_proj_b': (-4.600165843963623, 0.2),
     'L0_conv_D': (1.0, 0.2),
     'L0_conv_mlp_b1': (0.0, 0.1),
     'L0_conv_mlp_b2': (0.0, 0.1),
     'L1_conv_gate_b': (0.0, 0.1),
     'L1_conv_b1': (0.0, 0.1),
     'L1_conv_b2': (0.0, 0.1)}
    factors = {}
    for name, (base, spread) in spreads.items():
        noise = np.random.default_rng([zlib.crc32(name.encode()), seed]).standard_normal(out[name].shape)
        drawn = base * np.exp(spread * noise) if base else spread * noise
        out[name] = jnp.asarray(drawn.astype(out[name].dtype))
    for name, factor in factors.items():
        out[name] = (out[name] * factor).astype(out[name].dtype)
    return out
```

```python
from contextlib import ExitStack

import numpy as np

import concourse.bass as bass
from concourse import mybir

F32 = mybir.dt.float32
ALU = mybir.AluOpType
ACT = mybir.ActivationFunctionType
AX = mybir.AxisListType

P = 128
NB, C, L = 8, 384, 1024
T = 512
HALVES = L // T
NU = NB * HALVES
DI, NS, RANK = 768, 16, 24
NX = RANK + 2 * NS
HID = 4 * C
E, KTOP = 4, 2
KC, KD, KH = C // P, DI // P, HID // P
CH = T // P
G3 = 3
NG = KD // G3
SLOTS = NS * NG
GN_EPS, LN_EPS = 1e-5, 1e-5
GN_CH = C // 32
BANK = 512


class Unit:

    def __init__(self, b, half):
        self.b, self.half, self.n = b, half, b * HALVES + half
        self.static = isinstance(b, int)

    def ds(self):
        return bass.ds(self.b, 1)


class Event:

    def __init__(self, sem, per_unit, step=1, primed=False):
        self.sem, self.per_unit, self.step = sem, per_unit, step
        self.base = per_unit * step if primed else 0

    def prime(self, eng):
        eng.sem_inc(self.sem, self.base)

    def inc_by(self, instruction):
        instruction.then_inc(self.sem, self.step)

    def wait(self, eng, unit, i=None, back=0):
        i = self.per_unit - 1 if i is None else i
        if unit.static and unit.n < back:
            return
        eng.wait_ge(self.sem, unit.n * (self.per_unit * self.step)
                    + (self.base + (i + 1 - back * self.per_unit) * self.step))


def build(nc, a, out):
    with ExitStack() as ctx:
        def sem(name):
            return ctx.enter_context(nc.semaphore(name))

        x_d = a["x"].rearrange("b (k p) l -> b p k l", p=P)
        out_d = out.rearrange("b (k p) l -> b p k l", p=P)
        x1_t = nc.dram_tensor("x1_scratch", (NB, C, L), F32).ap()
        x1_d = x1_t.rearrange("b (k p) l -> b p k l", p=P)
        b_d = nc.dram_tensor("b_rows", (2, NS, T), F32).ap()
        w_d = nc.dram_tensor("top_weights", (KTOP, NB, L), F32).ap()

        def keep(name, shape):
            return ctx.enter_context(nc.sbuf_tensor(name, shape, F32))
        ident = keep("ident", [P, P])
        st1 = keep("st1", [P, NB, HALVES, KC, 6])
        gn0 = keep("gn0", [P, KC, NB, 2])
        eps = keep("eps", [P, 1])
        psum = [ctx.enter_context(nc.psum_tensor(f"bank{i}", [P, BANK], F32)) for i in range(8)]

        layer0(nc, ctx, a, sem, psum, ident, st1, gn0, eps, x_d, x1_d, b_d)
        layer1(nc, ctx, a, sem, psum, ident, st1, eps, x1_d, w_d, out_d)


class Chain:

    def __init__(self, sem):
        self.sem, self.n, self.at = sem, 0, {}

    def add(self, instruction, mark=None):
        instruction.then_inc(self.sem, 1)
        self.n += 1
        if mark is not None:
            self.at[mark] = self.n

    def own(self, eng):
        eng.wait_ge(self.sem, self.n)


def group_stats(dve, act, pe, dv, ac, pc, mv, group, bank, tmp, gn, eps, tag):
    mean_ps = bank[:, 0:KC * NB].rearrange("p (k b) -> p k b", k=KC)
    var_ps = bank[:, KC * NB:2 * KC * NB].rearrange("p (k b) -> p k b", k=KC)
    if pe is not None:
        for src, dst, mark in ((mv[:, :, :, 0], mean_ps, "mean"), (tmp, var_ps, "var")):
            pe.wait_ge(*dv[tag + (" mv" if mark == "mean" else " sq")])
            for m in range(KC):
                for k in range(KC):
                    mm = pe.matmul(dst[:, m, :], group[:, k, m * P:(m + 1) * P], src[:, k, :],
                                   start=(k == 0), stop=(k == KC - 1))
            mm.then_inc(pc[0], 1)
    if dve is not None:
        dve.wait_ge(pc[0], pc[1] + 1)
        dv.add(dve.tensor_copy(gn[:, :, :, 0], mean_ps))
        dv.own(dve)
        dv.add(dve.tensor_tensor(tmp, mv[:, :, :, 0], gn[:, :, :, 0], ALU.subtract))
        dv.own(dve)
        dv.add(dve.tensor_tensor(tmp, tmp, tmp, ALU.mult))
        dv.own(dve)
        dv.add(dve.tensor_tensor(tmp, tmp, mv[:, :, :, 1], ALU.add), tag + " sq")
        dve.wait_ge(ac[0], ac[1] + 1)
        dv.add(dve.reciprocal(gn[:, :, :, 1], gn[:, :, :, 1]), tag + " done")
    if act is not None:
        act.wait_ge(pc[0], pc[1] + 2)
        act.activation(gn[:, :, :, 1], var_ps, ACT.Sqrt, bias=eps[:, 0:1]).then_inc(ac[0], 1)


def layer0(nc, outer, a, sem, psum, ident, st1, gn0, eps, x_d, x1_d, b_d):
    with ExitStack() as ctx:
        def sb(name, shape):
            return ctx.enter_context(nc.sbuf_tensor(name, shape, F32))

        w_in = sb("w_in", [P, KC, 2 * DI])
        w_xp = sb("w_xp", [P, KD, NX])
        w_dt = sb("w_dt", [P, DI])
        w_out = sb("w_out", [P, KD, C])
        conv_w = sb("conv_w", [P, KD, 3])
        conv_b = sb("conv_b", [P, KD])
        dt_b = sb("dt_b", [P, KD])
        d_sk = sb("d_sk", [P, KD])
        a_neg = sb("a_neg", [P, KD, NS])
        ln_w = sb("ln_w", [P, KC])
        ln_b = sb("ln_b", [P, KC])
        b_in = sb("b_in", [P, 2 * KD])
        b1 = sb("b1", [P, KH])
        b2 = sb("b2", [P, KC])
        mean_w = sb("mean_w", [P, P])
        wring = sb("wring", [P, 3, 768])
        xn = sb("xn", [P, 2, KC, T])
        xc = sb("xc", [P, 2, KD, T])
        hr = sb("hr", [P, 3, T])
        tt = sb("tt", [P, KC, T])
        xr = sb("xr", [P, KC, T])
        xm = sb("xm", [P, 3, T + 2])
        halo = sb("halo", [P, KD, 2])
        rstd = sb("rstd", [P, T])
        dbc = sb("dbc", [P, T])
        spa = sb("spa", [P, 2, T])
        spb = sb("spb", [P, 2, T])
        dt = sb("dt", [P, KD, T])
        wu = sb("wu", [P, KD, T])
        ct = sb("ct", [P, 2, CH, NS])
        bb = sb("bb", [P, 4, T])
        da = sb("da", [P, 2, G3, T])
        vv = sb("vv", [P, 2, G3, T])
        hh = sb("hh", [P, 2, G3, T])
        hl = sb("hl", [P, NS, KD])
        yy = sb("yy", [P, CH, DI])
        group = vv[:, :, :, :].rearrange("p a g t -> p (a g t)")[:, 0:KC * C].rearrange(
            "p (k c) -> p k c", k=KC)
        st0 = da[:, 0, 0, 0:KC * NB * HALVES * 6].rearrange(
            "p (k b h s) -> p k b h s", k=KC, b=NB, h=HALVES)
        mv0 = da[:, 1, 0, 0:KC * NB * 2].rearrange("p (k b s) -> p k b s", k=KC, b=NB)
        tmp0 = da[:, 1, 1, 0:KC * NB].rearrange("p (k b) -> p k b", k=KC)
        xs = [xn[:, 0, :, :], xn[:, 1, :, :], tt[:, :, :], xr[:, :, :]]

        small = [(conv_w, "conv_w"), (conv_b, "conv_b"), (dt_b, "dt_b"), (d_sk, "D"),
                 (a_neg, "A_log"), (ln_w, "ln_w"), (ln_b, "ln_b"), (b1, "mlp_b1"),
                 (b2, "mlp_b2")]

        s_small, s_group, s_big = sem("small"), sem("group"), sem("big")
        s_xs = [sem(f"stat_x{i}") for i in range(4)]
        s_in = sem("w_in_loaded")
        dv = Chain(sem("b1_dve"))
        s_bact, s_bpe = sem("b1_act"), sem("b1_pe")
        with nc.Block() as block:
            @block.vector
            def _(eng):
                dv.add(eng.memset(w_dt[:, :], 0.0), "w_dt zero")
                dv.add(eng.memset(dbc[:, :], 0.0))
                dv.add(eng.memset(eps[:, :], GN_EPS), "eps")
                for n in range(NU):
                    eng.wait_ge(s_xs[n % 4], 16 * (n // 4 + 1))
                    for k in range(KC):
                        dv.add(eng.bn_stats(st0[:, k, n // 2, n % 2, :], xs[n % 4][:, k, :]),
                               ("stats", n))
                dv.own(eng)
                for k in range(KC):
                    for b in range(NB):
                        dv.add(eng.bn_aggr(mv0[:, k, b, :], st0[:, k, b, :, :].rearrange(
                            "p h s -> p (h s)")), "gn0 mv")
                eng.wait_ge(s_small, 16 * len(small))
                eng.wait_ge(s_bact, 1)
                dv.add(eng.tensor_scalar(a_neg[:, :, :], a_neg[:, :, :], -1.0, None, ALU.mult))
                eng.wait_ge(s_bpe, 1)
                dv.add(eng.tensor_copy(b_in[:, :], psum[1][:, 0:2 * KD]))
                for k in range(KC):
                    dv.add(eng.tensor_scalar(w_in[:, k, :], w_in[:, k, :], ln_w[:, k:k + 1],
                                             None, ALU.mult))
                group_stats(eng, None, None, dv, (s_bact, 1), (s_bpe, 1), mv0, group, psum[0],
                            tmp0, gn0, eps, "gn0")

            marks = {k: (dv.sem, v) for k, v in dv.at.items()}

            @block.sync
            def _(eng):
                for n in range(NU):
                    if n >= 4:
                        eng.wait_ge(*marks[("stats", n - 4)])
                    eng.dma_start(xs[n % 4], x_d[n // 2, :, :, n % 2 * T:(n % 2 + 1) * T])\
                       .then_inc(s_xs[n % 4], 16)

            @block.scalar
            def _(eng):
                for tile, name in small:
                    view = tile[:, :, :] if len(tile.shape) == 3 else tile[:, :]
                    eng.dma_start(view, a[name]).then_inc(s_small, 16)
                eng.dma_start(w_in[:, :, :], a["w_in"]).then_inc(s_in, 16)
                eng.dma_start(group, a["group"]).then_inc(s_group, 16)
                eng.dma_start(ident[:, :], a["ident"]).then_inc(s_big, 16)
                eng.dma_start(mean_w[:, :], a["mean_w"]).then_inc(s_big, 16)
                eng.dma_start(w_xp[:, :, :], a["w_xp"]).then_inc(s_big, 16)
                eng.dma_start(w_out[:, :, :], a["w_out"]).then_inc(s_big, 16)
                eng.wait_ge(*marks["w_dt zero"])
                eng.dma_start(w_dt[0:RANK, :], a["w_dt"]).then_inc(s_big, 16)
                eng.wait_ge(s_small, 16 * len(small))
                eng.activation(a_neg[:, :, :], a_neg[:, :, :], ACT.Exp).then_inc(s_bact, 1)
                eng.wait_ge(*marks["eps"])
                group_stats(None, eng, None, marks, (s_bact, 1), (s_bpe, 1), mv0, group,
                            psum[0], tmp0, gn0, eps, "gn0")
                eng.wait_ge(s_big, 16 * 5)

            @block.tensor
            def _(eng):
                eng.wait_ge(s_in, 16)
                eng.wait_ge(s_small, 16 * len(small))
                for m in range(2 * KD):
                    for k in range(KC):
                        mm = eng.matmul(psum[1][:, m:m + 1], w_in[:, k, m * P:(m + 1) * P],
                                        ln_b[:, k:k + 1], start=(k == 0), stop=(k == KC - 1))
                mm.then_inc(s_bpe, 1)
                eng.wait_ge(s_group, 16)
                group_stats(None, None, eng, marks, None, (s_bpe, 1), mv0, group, psum[0],
                            tmp0, gn0, eps, "gn0")

        def ev(name, per_unit, step=1, primed=False):
            return Event(sem(name), per_unit, step, primed)
        e_bb = [ev(f"b_row{i}", NS // 4, 16) for i in range(4)]
        e_da, e_v, e_scan = ev("dA", SLOTS), ev("v", SLOTS), ev("scanned", SLOTS)
        e_ht, e_mac, e_hl = ev("hT", SLOTS * CH), ev("mac", SLOTS * CH), ev("h_last", SLOTS)
        e_yt, e_yz = ev("yT", KD), ev("y_skip", KD)
        e_zp, e_sz, e_gt = ev("z_proj", KD), ev("silu_z", KD), ev("gated", KD)
        e_op, e_t = ev("out_proj", KC), ev("t_copied", KC)
        e_m1, e_ge, e_m2 = (
            ev("mlp1", KH, primed=True), ev("gelu", KH), ev("mlp2", 2 * KC, primed=True))
        e_x1, e_bn = ev("x1", KC), ev("x1_stats", KC, primed=True)
        e_xr, e_st = ev("xr_loaded", 1, 16), ev("x1_stored", 1, 16, primed=True)
        e_ws = [ev(f"mlp_w{i}", 4, 16) for i in range(3)]
        e_xin = ev("x_loaded", 1, 16)
        e_gn, e_mu, e_ce = ev("gn_applied", KC), ev("ln_mean", 1), ev("centred", KC)
        e_sq, e_var, e_rs = ev("squares", KC), ev("ln_var", 1), ev("ln_rstd", 2)
        e_xh = ev("xhat", KC)
        e_xm, e_xe, e_hi = ev("xm_proj", KD), ev("xm_copied", KD), ev("halo_in", 2)
        e_cv, e_hs, e_xc = ev("conv", 3 * KD), ev("halo_saved", 2), ev("xc", KD)
        e_xp, e_db, e_bw = ev("x_proj", 1), ev("dbc", 1), ev("b_stored", 1, 16)
        e_ct, e_cc = ev("C_T", 1), ev("C_copied", 1)
        e_dp, e_sp = ev("dt_proj", KD), ev("softplus", 4 * KD)
        e_dt, e_w = ev("dt", KD), ev("dt_x", KD)

        post_list = ([("Y", j, (e_yz, j)) for j in range(KD)]
                     + [("Z", j, (e_sz, j)) for j in range(KD)]
                     + [("O", m, (e_t, m)) for m in range(KC)]
                     + [("M1", m, (e_ge, m)) for m in range(KH)]
                     + [("M2", m, (e_x1, m)) for m in range(KC)])
        pre_list = ([("MU", 0, (e_ce, KC - 1)), ("VAR", 0, (e_rs, 0))]
                    + [("XM", j, (e_xe, j)) for j in range(KD)]
                    + [("XP", 0, (e_db, 0)), ("CT", 0, (e_cc, 0))]
                    + [("DT", j, (e_sp, 4 * j + 1)) for j in range(KD)])
        post_pos = {(s[0], s[1]): i for i, s in enumerate(post_list)}
        pre_pos = {(s[0], s[1]): i for i, s in enumerate(pre_list)}
        NDB = 4
        dense = psum[4:8]
        ht = psum[0:4]

        def bank(name, i):
            pos = post_pos.get((name, i), pre_pos.get((name, i)))
            return dense[pos % NDB]

        def bank_free(eng, unit, name, i):
            if (name, i) in post_pos:
                pos, own, other, back = post_pos[(name, i)], post_list, pre_list, -1
                if unit.static and unit.n >= NU - 1:
                    other, back = post_list, 1
            else:
                pos, own, other, back = pre_pos[(name, i)], pre_list, post_list, 2
                if unit.static and unit.n < 2:
                    other, back = pre_list, 1
            if pos >= NDB:
                event, at = own[pos - NDB][2]
                event.wait(eng, unit, at)
                return
            before = [s for q, s in enumerate(other) if q % NDB == pos % NDB]
            event, at = before[-1][2]
            event.wait(eng, unit, at, back=back)

        scan_w = {}

        def scan_sync(eng, u, k):
            if k % NG:
                return
            n = k // NG
            if n == 0:
                e_bw.wait(eng, u)
            if n >= 4:
                e_v.wait(eng, u, NG * (n - 4) + NG - 1)
            else:
                e_v.wait(eng, u, NG * (n + NS - 4) + NG - 1, back=1)
            e_bb[n % 4].inc_by(eng.dma_start(
                bb[:, n % 4, :], b_d[u.half, n:n + 1, :].to_broadcast([P, T])))

        def scan_pool(eng, u, k):
            n, g = k // NG, k % NG
            if n == 0:
                e_w.wait(eng, u, G3 * g + G3 - 1)
            if g == 0:
                e_bb[n % 4].wait(eng, u, n // 4)
            if k >= 2:
                e_scan.wait(eng, u, k - 2)
            else:
                e_scan.wait(eng, u, SLOTS - 2 + k, back=1)
            e_v.inc_by(eng.tensor_tensor(
                vv[:, k % 2, :, :], wu[:, G3 * g:G3 * g + G3, :],
                bb[:, n % 4:n % 4 + 1, :].to_broadcast([P, G3, T]), ALU.mult))

        def scan_act(eng, u, k):
            n, g = k // NG, k % NG
            if n == 0:
                e_dt.wait(eng, u, G3 * g + G3 - 1)
            if k >= 2:
                e_scan.wait(eng, u, k - 2)
            else:
                e_scan.wait(eng, u, SLOTS - 2 + k, back=1)
            for i in range(G3):
                j = G3 * g + i
                ins = eng.activation(da[:, k % 2, i, :], dt[:, j, :], ACT.Exp,
                                     scale=a_neg[:, j, n:n + 1])
            e_da.inc_by(ins)

        def scan_dve(eng, u, k):
            n, g = k // NG, k % NG
            e_da.wait(eng, u, k)
            e_v.wait(eng, u, k)
            if k >= 2:
                e_ht.wait(eng, u, CH * (k - 2) + CH - 1)
                e_hl.wait(eng, u, k - 2)
            else:
                e_ht.wait(eng, u, CH * (SLOTS - 2 + k) + CH - 1, back=1)
                e_hl.wait(eng, u, SLOTS - 2 + k, back=1)
            for i in range(G3):
                j = G3 * g + i
                start = hl[:, n, j:j + 1] if u.half else 0.0
                ins = eng.tensor_tensor_scan(hh[:, k % 2, i, :], da[:, k % 2, i, :],
                                             vv[:, k % 2, i, :], start, ALU.mult, ALU.add)
            e_scan.inc_by(ins)

        def mac_dve(eng, u, k):
            n, g = k // NG, k % NG
            if k == 0:
                e_cc.wait(eng, u)
                e_yt.wait(eng, u, back=1)
            if k >= NG:
                e_mac.wait(eng, u, CH * (k - NG) + CH - 1)
            for c in range(CH):
                e_ht.wait(eng, u, CH * k + c)
                y = yy[:, c, G3 * P * g:G3 * P * (g + 1)]
                scale = ct[:, u.half, c, n:n + 1]
                if n == 0:
                    ins = eng.tensor_scalar(y, ht[c][:, 0:G3 * P], scale, None, ALU.mult)
                else:
                    ins = eng.scalar_tensor_tensor(out=y, in0=ht[c][:, 0:G3 * P], scalar=scale,
                                                   in1=y, op0=ALU.mult, op1=ALU.add)
                e_mac.inc_by(ins)

        def last_dve(eng, u, k):
            n, g = k // NG, k % NG
            e_scan.wait(eng, u, k)
            e_hl.inc_by(eng.tensor_copy(hl[:, n, G3 * g:G3 * g + G3], hh[:, k % 2, :, T - 1]))

        def scan_pe(eng, u, k):
            e_scan.wait(eng, u, k)
            for c in range(CH):
                if k >= 1:
                    e_mac.wait(eng, u, CH * (k - 1) + c)
                else:
                    e_mac.wait(eng, u, CH * (SLOTS - 1) + c, back=1)
                for i in range(G3):
                    ins = eng.transpose(ht[c][:, i * P:(i + 1) * P],
                                        hh[:, k % 2, i, c * P:(c + 1) * P], ident[:, :])
                e_ht.inc_by(ins)

        def hid(u, m):
            if m < KD:
                return xc[:, u.half, m, :]
            if m < KD + KC:
                return xn[:, u.half, m - KD, :]
            return hr[:, m - KD - KC, :]

        def stream(q):
            return a["w_m1"][q] if q < KH // 2 else a["w_m2"][q - KH // 2]

        def stream_sync(eng, u, q):
            if q < 3:
                e_m2.wait(eng, u, 2 * KC - 3 + q, back=1)
            elif q < KH // 2 + 3:
                e_m1.wait(eng, u, 2 * (q - 3) + 1)
            else:
                e_m2.wait(eng, u, q - 3 - KH // 2)
            e_ws[q % 3].inc_by(eng.dma_start(wring[:, q % 3, :], stream(q)))

        def post(u):
            st = []

            def y_stage(j):
                def pe(eng):
                    if j == 0:
                        e_mac.wait(eng, u)
                    bank_free(eng, u, "Y", j)
                    for c in range(CH):
                        ins = eng.transpose(bank("Y", j)[:, c * P:(c + 1) * P],
                                            yy[:, c, j * P:(j + 1) * P], ident[:, :])
                    e_yt.inc_by(ins)

                def dve(eng):
                    e_yt.wait(eng, u, j)
                    e_yz.inc_by(eng.scalar_tensor_tensor(
                        out=xc[:, u.half, j, :], in0=xc[:, u.half, j, :],
                        scalar=d_sk[:, j:j + 1], in1=bank("Y", j)[:, :],
                        op0=ALU.mult, op1=ALU.add))
                return (0.5, {"pe": pe, "dve": dve})

            def z_stage(j):
                def pe(eng):
                    bank_free(eng, u, "Z", j)
                    for k in range(KC):
                        ins = eng.matmul(bank("Z", j)[:, :], w_in[:, k, DI + j * P:DI + (j + 1) * P],
                                         xn[:, u.half, k, :], start=(k == 0), stop=(k == KC - 1))
                    e_zp.inc_by(ins)

                def act(eng):
                    for q in range(j - 2, j + 1):
                        if q >= 3:
                            e_gt.wait(eng, u, q - 3)
                        e_zp.wait(eng, u, q)
                        e_sz.inc_by(eng.activation(hr[:, q % 3, :], bank("Z", q)[:, :], ACT.Silu,
                                                   bias=b_in[:, KD + q:KD + q + 1]))

                def dve(eng):
                    for q in range(j - 2, j + 1):
                        e_sz.wait(eng, u, q)
                        e_yz.wait(eng, u, q)
                        e_gt.inc_by(eng.tensor_tensor(xc[:, u.half, q, :], xc[:, u.half, q, :],
                                                      hr[:, q % 3, :], ALU.mult))
                return (3, {"pe": pe} | ({"act": act, "dve": dve} if j % 3 == 2 else {}))

            def o_stage(m):
                def pe(eng):
                    bank_free(eng, u, "O", m)
                    e_gt.wait(eng, u)
                    for k in range(KD):
                        ins = eng.matmul(bank("O", m)[:, :], w_out[:, k, m * P:(m + 1) * P],
                                         xc[:, u.half, k, :], start=(k == 0), stop=(k == KD - 1))
                    e_op.inc_by(ins)

                def act(eng):
                    if m == 0:
                        e_m1.wait(eng, u, back=1)
                    e_op.wait(eng, u, m)
                    e_t.inc_by(eng.activation(tt[:, m, :], bank("O", m)[:, :], ACT.Copy))
                return (6, {"pe": pe, "act": act})

            def m1_stage(m):
                def pe(eng):
                    bank_free(eng, u, "M1", m)
                    if m == 0:
                        e_t.wait(eng, u)
                    if m % 2 == 0:
                        e_ws[m // 2 % 3].wait(eng, u, m // 2 // 3)
                    w = wring[:, m // 2 % 3, :].rearrange("p (m k c) -> p m k c", m=2, k=KC)
                    for k in range(KC):
                        ins = eng.matmul(bank("M1", m)[:, :], w[:, m % 2, k, :], tt[:, k, :],
                                         start=(k == 0), stop=(k == KC - 1))
                    e_m1.inc_by(ins)

                def act(eng):
                    for q in range(m - 3, m + 1):
                        e_m1.wait(eng, u, q)
                        e_ge.inc_by(eng.activation(hid(u, q), bank("M1", q)[:, :], ACT.Gelu,
                                                   bias=b1[:, q:q + 1]))
                return (3, {"pe": pe} | ({"act": act} if m % 4 == 3 else {}))

            def m2_stage(m):
                def pe(eng):
                    bank_free(eng, u, "M2", m)
                    for h in range(2):
                        q = KH // 2 + 2 * m + h
                        e_ws[q % 3].wait(eng, u, q // 3)
                        if m == 0:
                            e_ge.wait(eng, u, 6 * h + 5)
                        w = wring[:, q % 3, :].rearrange("p (k c) -> p k c", k=6)
                        for k in range(6):
                            ins = eng.matmul(bank("M2", m)[:, :], w[:, k, :], hid(u, 6 * h + k),
                                             start=(h + k == 0), stop=(h == 1 and k == 5))
                        e_m2.inc_by(ins)

                def dve(eng):
                    if m == 0:
                        e_xr.wait(eng, u)
                    e_m2.wait(eng, u, 2 * m + 1)
                    e_x1.inc_by(eng.scalar_tensor_tensor(
                        out=xr[:, m, :], in0=bank("M2", m)[:, :], scalar=b2[:, m:m + 1],
                        in1=xr[:, m, :], op0=ALU.add, op1=ALU.add))
                    e_x1.wait(eng, u, m)
                    e_bn.inc_by(eng.bn_stats(
                        st1[:, u.ds(), u.half, m, :].rearrange("p o s -> p (o s)"), xr[:, m, :]))
                return (12, {"pe": pe, "dve": dve})

            def dma_stage(q):
                def sync(eng):
                    stream_sync(eng, u, q)
                return (0, {"sync": sync})

            def load_xr():
                def sync(eng):
                    e_st.wait(eng, u, back=1)
                    e_bn.wait(eng, u, back=1)
                    e_xr.inc_by(eng.dma_start(xr[:, :, :], x_half(x_d, u)))
                return (0, {"sync": sync})

            def store_x1():
                def sync(eng):
                    e_x1.wait(eng, u)
                    e_st.inc_by(eng.dma_start(x_half(x1_d, u), xr[:, :, :]))
                return (0, {"sync": sync})

            st.append(load_xr())
            st += [y_stage(j) for j in range(KD)]
            st += [dma_stage(q) for q in range(3)]
            st += [z_stage(j) for j in range(KD)]
            st += [o_stage(m) for m in range(KC)]
            for m in range(KH):
                st.append(m1_stage(m))
                if m % 2:
                    st.append(dma_stage(m // 2 + 3))
            for m in range(KC):
                st.append(m2_stage(m))
                if m == 0:
                    st += [dma_stage(9), dma_stage(10)]
                if m == 1:
                    st += [dma_stage(11)]
            st.append(store_x1())
            return st

        def x_half(d, u):
            s = slice(u.half * T, (u.half + 1) * T)
            if u.static:
                return d[u.b, :, :, s]
            return d[u.ds(), :, :, s].rearrange("o p k l -> (o p) k l")

        def pre_front(u):
            st = []

            def load():
                def sync(eng):
                    e_m2.wait(eng, u, back=2)
                    e_xin.inc_by(eng.dma_start(xn[:, u.half, :, :], x_half(x_d, u)))

                def dve(eng):
                    e_xin.wait(eng, u)
                    for k in range(KC):
                        s = [gn0[:, k, u.ds(), i] for i in range(2)]
                        e_gn.inc_by(eng.tensor_scalar(
                            xn[:, u.half, k, :], xn[:, u.half, k, :], s[0], s[1],
                            ALU.subtract, ALU.mult))
                return (0, {"sync": sync, "dve": dve})

            def mu_stage():
                def pe(eng):
                    bank_free(eng, u, "MU", 0)
                    e_gn.wait(eng, u)
                    for k in range(KC):
                        ins = eng.matmul(bank("MU", 0)[:, :], mean_w[:, :], xn[:, u.half, k, :],
                                         start=(k == 0), stop=(k == KC - 1))
                    e_mu.inc_by(ins)

                def dve(eng):
                    e_mu.wait(eng, u)
                    for k in range(KC):
                        e_ce.inc_by(eng.tensor_tensor(xn[:, u.half, k, :], xn[:, u.half, k, :],
                                                      bank("MU", 0)[:, :], ALU.subtract))

                def act(eng):
                    for k in range(KC):
                        e_ce.wait(eng, u, k)
                        e_sq.inc_by(eng.activation(hr[:, k, :], xn[:, u.half, k, :], ACT.Square))
                return (3, {"pe": pe, "dve": dve, "act": act})

            def var_stage():
                def pe(eng):
                    bank_free(eng, u, "VAR", 0)
                    for k in range(KC):
                        e_sq.wait(eng, u, k)
                        ins = eng.matmul(bank("VAR", 0)[:, :], mean_w[:, :], hr[:, k, :],
                                         start=(k == 0), stop=(k == KC - 1))
                    e_var.inc_by(ins)

                def act(eng):
                    e_xh.wait(eng, u, back=1)
                    e_var.wait(eng, u)
                    e_rs.inc_by(eng.activation(rstd[:, :], bank("VAR", 0)[:, :], ACT.Ln,
                                               bias=eps[:, 0:1]))
                    e_rs.wait(eng, u, 0)
                    e_rs.inc_by(eng.activation(rstd[:, :], rstd[:, :], ACT.Exp, scale=-0.5))

                def dve(eng):
                    e_rs.wait(eng, u)
                    for k in range(KC):
                        e_xh.inc_by(eng.tensor_tensor(xn[:, u.half, k, :], xn[:, u.half, k, :],
                                                      rstd[:, :], ALU.mult))
                return (3, {"pe": pe, "act": act, "dve": dve})

            def xm_stage(j):
                q = j // 3

                def pe(eng):
                    bank_free(eng, u, "XM", j)
                    e_xh.wait(eng, u)
                    for k in range(KC):
                        ins = eng.matmul(bank("XM", j)[:, :], w_in[:, k, j * P:(j + 1) * P],
                                         xn[:, u.half, k, :], start=(k == 0), stop=(k == KC - 1))
                    e_xm.inc_by(ins)

                def act(eng):
                    if q:
                        e_hs.wait(eng, u, 0)
                        e_cv.wait(eng, u, 8)
                    else:
                        e_hs.wait(eng, u, back=1)
                        e_cv.wait(eng, u, back=1)
                    e_xm.wait(eng, u, j)
                    e_xe.inc_by(eng.activation(xm[:, j % 3, 2:T + 2], bank("XM", j)[:, :],
                                               ACT.Identity, bias=b_in[:, j:j + 1]))

                def dve(eng):
                    edge = xm[:, :, 0:2]
                    js = range(3 * q, 3 * q + 3)
                    if q:
                        e_cv.wait(eng, u, 8)
                    else:
                        e_cv.wait(eng, u, back=1)
                    if u.half:
                        e_hs.wait(eng, u, q, back=1)
                        ins = eng.tensor_copy(edge, halo[:, 3 * q:3 * q + 3, :])
                    else:
                        ins = eng.memset(edge, 0.0)
                    e_hi.inc_by(ins)
                    e_xe.wait(eng, u, j)
                    e_hi.wait(eng, u, q)
                    e_hs.inc_by(eng.tensor_copy(halo[:, 3 * q:3 * q + 3, :], xm[:, :, T:T + 2]))
                    if q:
                        e_xc.wait(eng, u, 2)
                    for tap in range(3):
                        for i in js:
                            src = xm[:, i % 3, 2 - tap:T + 2 - tap]
                            w = conv_w[:, i, 2 - tap:3 - tap]
                            if tap == 0:
                                ins = eng.tensor_scalar(hr[:, i % 3, :], src, w, None, ALU.mult)
                            else:
                                e_cv.wait(eng, u, 9 * q + 3 * (tap - 1) + i % 3)
                                ins = eng.scalar_tensor_tensor(
                                    out=hr[:, i % 3, :], in0=src, scalar=w, in1=hr[:, i % 3, :],
                                    op0=ALU.mult, op1=ALU.add)
                            e_cv.inc_by(ins)

                def act_silu(eng):
                    for i in range(3 * q, 3 * q + 3):
                        e_cv.wait(eng, u, 9 * q + 6 + i % 3)
                        e_xc.inc_by(eng.activation(xc[:, u.half, i, :], hr[:, i % 3, :], ACT.Silu,
                                                   bias=conv_b[:, i:i + 1]))
                return (3, {"pe": pe, "act": act}
                        | ({"dve": dve, "act2": act_silu} if j % 3 == 2 else {}))

            st.append(load())
            st.append((0, {"gap": 1}))
            st.append(mu_stage())
            st.append((0, {"gap": 2}))
            st.append(var_stage())
            st.append((0, {"gap": 2}))
            st += [xm_stage(j) for j in range(KD)]
            return st

        def pre_back(u):
            def pe(eng):
                bank_free(eng, u, "XP", 0)
                for k in range(KD):
                    e_xc.wait(eng, u, k)
                    ins = eng.matmul(bank("XP", 0)[0:NX, :], w_xp[:, k, :], xc[:, u.half, k, :],
                                     start=(k == 0), stop=(k == KD - 1))
                e_xp.inc_by(ins)
                e_db.wait(eng, u)
                for j in range(KD):
                    if j == 1:
                        bank_free(eng, u, "CT", 0)
                        for c in range(CH):
                            ins = eng.transpose(bank("CT", 0)[:, c * P:(c + 1) * P],
                                                dbc[:, c * P:(c + 1) * P], ident[:, :])
                        e_ct.inc_by(ins)
                    bank_free(eng, u, "DT", j)
                    e_dp.inc_by(eng.matmul(bank("DT", j)[:, :], w_dt[:, j * P:(j + 1) * P],
                                           dbc[:, :], start=True, stop=True))

            def act(eng):
                e_bw.wait(eng, u, back=1)
                e_dp.wait(eng, u, back=1)
                e_ct.wait(eng, u, back=1)
                e_xp.wait(eng, u)
                e_db.inc_by(eng.activation(dbc[0:NX, :], bank("XP", 0)[0:NX, :], ACT.Copy))
                for j in range(KD):
                    if j >= 2:
                        e_dt.wait(eng, u, j - 2)
                    else:
                        e_dt.wait(eng, u, KD - 2 + j, back=1)
                    e_dp.wait(eng, u, j)
                    ps, sa, sb_ = bank("DT", j)[:, :], spa[:, j % 2, :], spb[:, j % 2, :]
                    e_sp.inc_by(eng.activation(sb_, ps, ACT.Abs, bias=dt_b[:, j:j + 1]))
                    e_sp.inc_by(eng.activation(sa, ps, ACT.Identity, bias=dt_b[:, j:j + 1]))
                    e_sp.wait(eng, u, 4 * j)
                    e_sp.inc_by(eng.activation(sb_, sb_, ACT.Exp, scale=-1.0))
                    e_sp.wait(eng, u, 4 * j + 2)
                    e_sp.inc_by(eng.activation(sb_, sb_, ACT.Ln, bias=1.0))

            def dve(eng):
                e_da.wait(eng, u, back=1)
                e_v.wait(eng, u, back=1)
                for j in range(KD):
                    e_sp.wait(eng, u, 4 * j + 3)
                    e_dt.inc_by(eng.scalar_tensor_tensor(
                        out=dt[:, j, :], in0=spa[:, j % 2, :], scalar=0.0, in1=spb[:, j % 2, :],
                        op0=ALU.max, op1=ALU.add))
                    if j >= 1:
                        times_x(eng, j - 1)
                    if j == 2:
                        e_ct.wait(eng, u)
                        c_t = bank("CT", 0)[:, :].rearrange("p (c r) -> p c r", c=CH)
                        e_cc.inc_by(eng.tensor_copy(ct[:, u.half, :, :], c_t[:, :, RANK + NS:NX]))
                times_x(eng, KD - 1)

            def times_x(eng, j):
                e_dt.wait(eng, u, j)
                e_w.inc_by(eng.tensor_tensor(wu[:, j, :], dt[:, j, :], xc[:, u.half, j, :],
                                             ALU.mult))

            def sync(eng):
                e_db.wait(eng, u)
                e_bw.inc_by(eng.dma_start(b_d[u.half, :, :], dbc[RANK:RANK + NS, :]))
            return {"pe": pe, "act": act, "dve": dve, "sync": sync}

        def plan(stages):
            gaps = sum(s[1]["gap"] for s in stages if "gap" in s[1])
            total = sum(s[0] for s in stages)
            per = total / max(SLOTS - 3 - gaps, 1)
            at = {e: [[] for _ in range(SLOTS + 4)] for e in ("pe", "act", "dve", "sync")}
            done, extra = 0.0, 0
            for work, parts in stages:
                if "gap" in parts:
                    extra += parts["gap"]
                    continue
                slot = int(done / per) + extra
                done += work
                for e, f in parts.items():
                    if e == "pe" or e == "sync":
                        at[e][slot].append(f)
                    elif e == "act2":
                        at["act"][slot + 2].append(f)
                    else:
                        at[e][slot + 1].append(f)
            return at

        def step(eng, name, scan=None, posts=None, pres=None):
            stages = (post(posts) if posts else []) + (pre_front(pres) if pres else [])
            at = plan(stages)[name] if name != "pool" else None
            tables = name == "act"
            for k in range(SLOTS + 4):
                if scan and k < SLOTS:
                    if name == "sync":
                        if k == 0:
                            for q in range(0, 2 * NG, NG):
                                scan_sync(eng, scan, q)
                        if k + 2 * NG < SLOTS and k % NG == 0:
                            scan_sync(eng, scan, k + 2 * NG)
                    if name == "pool":
                        scan_pool(eng, scan, k)
                    if name == "act":
                        scan_act(eng, scan, k)
                    if name == "dve":
                        scan_dve(eng, scan, k)
                    if name == "pe":
                        scan_pe(eng, scan, k)
                if at:
                    for f in at[k]:
                        f(eng)
                if scan and name == "dve" and k < SLOTS:
                    if k >= 1:
                        mac_dve(eng, scan, k - 1)
                    last_dve(eng, scan, k)
                    if k == SLOTS - 1:
                        mac_dve(eng, scan, k)
            if pres and name != "pool":
                pre_back(pres)[name](eng)

        def program(eng, name):
            step(eng, name, pres=Unit(0, 0))
            step(eng, name, scan=Unit(0, 0), pres=Unit(0, 1))
            with eng.Fori(0, NB - 1) as i:
                step(eng, name, scan=Unit(i, 1), posts=Unit(i, 0), pres=Unit(i + 1, 0))
                step(eng, name, scan=Unit(i + 1, 0), posts=Unit(i, 1), pres=Unit(i + 1, 1))
            step(eng, name, scan=Unit(NB - 1, 1), posts=Unit(NB - 1, 0))
            step(eng, name, posts=Unit(NB - 1, 1))

        with nc.Block() as block:
            @block.sync
            def _(eng):
                for event in (e_m1, e_m2, e_bn, e_st):
                    event.prime(eng)
                program(eng, "sync")
                e_st.wait(eng, Unit(NB - 1, 1))

            @block.gpsimd
            def _(eng):
                program(eng, "pool")

            @block.scalar
            def _(eng):
                program(eng, "act")

            @block.vector
            def _(eng):
                program(eng, "dve")

            @block.tensor
            def _(eng):
                program(eng, "pe")


def layer1(nc, outer, a, sem, psum, ident, st1, eps, x1_d, w_d, out_d):
    with ExitStack() as ctx:
        def sb(name, shape):
            return ctx.enter_context(nc.sbuf_tensor(name, shape, F32))

        w1 = sb("w1e", [P, E, KC, C])
        w2 = sb("w2e", [P, E, KC, C])
        b1 = sb("b1e", [P, E, KC])
        gn1 = sb("gn1", [P, KC, NB, 2])
        sel = sb("sel", [P, E, P])
        b2r = sb("b2r", [P, C])
        xb = sb("xb", [P, 2, KC, T])
        xg = sb("xg", [P, 2, KC, T])
        cw = sb("cw", [P, 2, T])
        cf = sb("cf", [P, E, T])
        hb = sb("hb", [P, 2, KC, T])
        ob = sb("ob", [P, 2, KC, T])
        group = sb("group1", [P, KC, C])
        mv = sb("mv1", [P, KC, NB, 2])
        tmp = sb("tmp1", [P, KC, NB])
        gate_w = sb("gate_w", [P, KC, E])
        gate_b = sb("gate_b", [P, E])
        rows = sb("rows", [P, KTOP])
        ones = sb("ones", [P, P])
        gs = sb("gs", [P, KC, NB, E])
        gm = sb("gm", [P, KC, NB, E])
        b2b = sb("b2b", [P, E, C])
        NT = NB * L // P
        lg = sb("lg", [P, NT, E])
        off = sb("off", [P, NB, E])
        mx = sb("mx", [P, NT])
        sm = sb("sm", [P, NT])
        ge = sb("ge", [P, 6, NT])
        rk = sb("rk", [P, NT, E])
        top = sb("top", [P, KTOP, NT, E])
        pf = sb("pf", [P, KTOP, E])
        pres = sb("pres", [P, KTOP, E])
        tw = sb("tw", [P, KTOP, NT])
        twt = sb("twt", [P, P])
        se = sb("se", [P, E])

        s_c, s_w = sem("b3_small"), sem("b3_weights")
        s_x = [sem(f"gate_x{i}") for i in range(HALVES)]
        s_pe, s_act, s_tw = sem("b3_pe"), sem("b3_act"), sem("b3_tw")
        s_lg = sem("b3_logits")
        dv = Chain(sem("b3_dve"))
        small = [(group, "group"), (gate_w, "gate_w"), (rows, "rows"), (ones, "ones"), (b1, "b1e")]
        n_small = len(small) + 2
        pairs = [(i, j) for i in range(E) for j in range(i + 1, E)]
        with nc.Block() as block:
            @block.vector
            def _(eng):
                for h in range(2):
                    dv.add(eng.memset(cw[:, h, :], 0.0))
                for k in range(KC):
                    for b in range(NB):
                        dv.add(eng.bn_aggr(mv[:, k, b, :], st1[:, b, :, k, :]), "gn1 mv")
                group_stats(eng, None, None, dv, (s_act, 0), (s_pe, 0), mv, group, psum[0], tmp[:, :, :],
                            gn1, eps, "gn1")
                dv.own(eng)
                eng.wait_ge(s_c, 16 * n_small)
                for k in range(KC):
                    dv.add(eng.tensor_tensor(
                        gs[:, k, :, :], gate_w[:, k:k + 1, :].to_broadcast([P, NB, E]),
                        gn1[:, k, :, 1:2].to_broadcast([P, NB, E]), ALU.mult))
                dv.own(eng)
                dv.at["gs"] = dv.n
                for k in range(KC):
                    dv.add(eng.tensor_tensor(gm[:, k, :, :], gs[:, k, :, :],
                                             gn1[:, k, :, 0:1].to_broadcast([P, NB, E]),
                                             ALU.mult), "gm")
                eng.wait_ge(s_pe, 3)
                offp = psum[2][:, 0:NB * E].rearrange("p (b e) -> p b e", b=NB)
                dv.add(eng.tensor_tensor(off[:, :, :], gate_b[:, None, :].to_broadcast([P, NB, E]),
                                         offp, ALU.subtract))
                dv.own(eng)
                eng.wait_ge(s_lg, NB + 1)
                lgp = psum[1][:, 0:NT * E].rearrange("p (b t e) -> p b t e", b=NB, e=E)
                dv.add(eng.tensor_tensor(
                    lg[:, :, :].rearrange("p (b t) e -> p b t e", b=NB), lgp,
                    off[:, :, None, :].to_broadcast([P, NB, NT // NB, E]), ALU.add))
                dv.own(eng)
                dv.add(eng.tensor_reduce(mx[:, :], lg[:, :, :], AX.X, ALU.max))
                dv.own(eng)
                dv.add(eng.tensor_tensor(lg[:, :, :], lg[:, :, :],
                                         mx[:, :, None].to_broadcast([P, NT, E]), ALU.subtract),
                       "shifted")
                eng.wait_ge(s_act, 2)
                dv.add(eng.tensor_reduce(sm[:, :], lg[:, :, :], AX.X, ALU.add))
                dv.own(eng)
                dv.add(eng.reciprocal(sm[:, :], sm[:, :]))
                dv.own(eng)
                dv.add(eng.tensor_tensor(lg[:, :, :], lg[:, :, :],
                                         sm[:, :, None].to_broadcast([P, NT, E]), ALU.mult))
                dv.own(eng)
                for q, (i, j) in enumerate(pairs):
                    dv.add(eng.tensor_tensor(ge[:, q, :], lg[:, :, i], lg[:, :, j], ALU.is_ge))
                for i in range(E):
                    dv.add(eng.memset(rk[:, :, i], float(E - 1 - i)))
                dv.own(eng)
                for q, (i, j) in enumerate(pairs):
                    dv.add(eng.tensor_tensor(rk[:, :, i], rk[:, :, i], ge[:, q, :], ALU.subtract))
                    dv.own(eng)
                    dv.add(eng.tensor_tensor(rk[:, :, j], rk[:, :, j], ge[:, q, :], ALU.add))
                    dv.own(eng)
                for k in range(KTOP):
                    dv.add(eng.tensor_scalar(top[:, k, :, :], rk[:, :, :], float(k), None,
                                             ALU.is_equal))
                dv.own(eng)
                for k in range(KTOP):
                    dv.add(eng.tensor_reduce(pf[:, k, :], top[:, k, :, :].rearrange(
                        "p t e -> p e t"), AX.X, ALU.max), "chosen")
                dv.own(eng)
                for k in range(KTOP):
                    dv.add(eng.tensor_tensor(top[:, k, :, :], top[:, k, :, :], lg[:, :, :],
                                             ALU.mult))
                dv.own(eng)
                for k in range(KTOP):
                    dv.add(eng.tensor_reduce(tw[:, k, :], top[:, k, :, :], AX.X, ALU.add))
                dv.own(eng)
                dv.add(eng.tensor_tensor(tw[:, 1, :], tw[:, 1, :], tw[:, 0, :], ALU.subtract),
                       "second - first")
                eng.wait_ge(s_act, 3)
                dv.add(eng.tensor_scalar(tw[:, 0, :], tw[:, 1, :], 1.0, None, ALU.add))
                dv.own(eng)
                dv.add(eng.reciprocal(tw[:, 0, :], tw[:, 0, :]))
                dv.own(eng)
                dv.add(eng.tensor_tensor(tw[:, 1, :], tw[:, 1, :], tw[:, 0, :], ALU.mult),
                       "weights")
                eng.wait_ge(s_pe, 4)
                dv.add(eng.tensor_scalar(
                    pres[:, :, :], psum[3][:, 0:KTOP * E].rearrange("p (k e) -> p k e", k=KTOP),
                    0.0, None, ALU.is_gt))
                dv.own(eng)
                dv.add(eng.tensor_scalar(se[:, :], pres[:, 0, :], rows[:, 0:1], None, ALU.mult))
                dv.own(eng)
                dv.add(eng.scalar_tensor_tensor(out=se[:, :], in0=pres[:, 1, :],
                                                scalar=rows[:, 1:2], in1=se[:, :],
                                                op0=ALU.mult, op1=ALU.add))
                dv.own(eng)
                for e in range(E):
                    dv.add(eng.tensor_scalar(sel[:, e, :], ones[:, :], se[:, e:e + 1], None,
                                             ALU.mult))
                    if e == 0:
                        ins = eng.tensor_scalar(b2r[:, :], b2b[:, e, :], se[:, e:e + 1], None,
                                                ALU.mult)
                    else:
                        ins = eng.scalar_tensor_tensor(out=b2r[:, :], in0=b2b[:, e, :],
                                                       scalar=se[:, e:e + 1], in1=b2r[:, :],
                                                       op0=ALU.mult, op1=ALU.add)
                    dv.add(ins)
                    dv.own(eng)
                eng.wait_ge(s_pe, 5)
                dv.add(eng.tensor_copy(twt[:, :], psum[4][:, 0:P]), "twt")

            marks = {k: (dv.sem, v) for k, v in dv.at.items()}

            @block.sync
            def _(eng):
                for tile, name in small:
                    view = tile[:, :, :] if len(tile.shape) == 3 else tile[:, :]
                    eng.dma_start(view, a[name]).then_inc(s_c, 16)
                eng.dma_start(gate_b[:, :], a["gate_b"].to_broadcast([P, E])).then_inc(s_c, 16)
                eng.dma_start(b2b[:, :, :], a["b2e"].to_broadcast([P, E, C])).then_inc(s_c, 16)
                eng.sem_inc(s_lg, 1)
                with eng.Fori(0, NB) as b:
                    for h in range(HALVES):
                        eng.wait_ge(s_lg, b + 1)
                        eng.dma_start(xb[:, h, :, :],
                                      x1_d[bass.ds(b, 1), :, :, h * T:(h + 1) * T].rearrange(
                                          "o p k l -> (o p) k l")).then_inc(s_x[h], 16)
                eng.wait_ge(*marks["twt"])
                eng.dma_start(w_d.rearrange("k b (c l) -> (k b c) l", l=P), twt[:, :])\
                   .then_inc(s_tw, 16)
                eng.wait_ge(s_tw, 16)

            @block.scalar
            def _(eng):
                eng.dma_start(w1[:, :, :, :], a["w1e"]).then_inc(s_w, 16)
                eng.dma_start(w2[:, :, :, :], a["w2e"]).then_inc(s_w, 16)
                group_stats(None, eng, None, marks, (s_act, 0), (s_pe, 0), mv, group, psum[0],
                            tmp[:, :, :], gn1, eps, "gn1")
                eng.wait_ge(*marks["shifted"])
                eng.activation(lg[:, :, :], lg[:, :, :], ACT.Exp).then_inc(s_act, 1)
                eng.wait_ge(*marks["second - first"])
                eng.activation(tw[:, 1, :], tw[:, 1, :], ACT.Exp).then_inc(s_act, 1)
                eng.wait_ge(s_w, 32)

            @block.tensor
            def _(eng):
                eng.wait_ge(s_c, 16 * n_small)
                group_stats(None, None, eng, marks, None, (s_pe, 0), mv, group, psum[0], tmp[:, :, :],
                            gn1, eps, "gn1")
                eng.wait_ge(*marks["gm"])
                for k in range(KC):
                    mm = eng.matmul(psum[2][:, 0:NB * E], ones[:, :], gm[:, k, :, :].rearrange(
                        "p b e -> p (b e)"), start=(k == 0), stop=(k == KC - 1))
                mm.then_inc(s_pe, 1)
                with eng.Fori(0, NB) as b:
                    for h in range(HALVES):
                        eng.wait_ge(s_x[h], 16 * b + 16)
                        for c in range(CH):
                            at = (h * CH + c) * E
                            for k in range(KC):
                                mm = eng.matmul(
                                    psum[1][:, bass.ds(b * (HALVES * CH * E) + at, E)],
                                    xb[:, h, k, c * P:(c + 1) * P],
                                    gs[:, k, bass.ds(b, 1), :].rearrange("p o e -> p (o e)"),
                                    start=(k == 0), stop=(k == KC - 1))
                    mm.then_inc(s_lg, 1)
                eng.wait_ge(*marks["chosen"])
                eng.matmul(psum[3][:, 0:KTOP * E], ones[:, :], pf[:, :, :].rearrange(
                    "p k e -> p (k e)"), start=True, stop=True).then_inc(s_pe, 1)
                eng.wait_ge(*marks["weights"])
                eng.transpose(psum[4][:, 0:P], tw[:, :, :].rearrange("p k t -> p (k t)"),
                              ident[:, :]).then_inc(s_pe, 1)

        def ev(name, per_unit, step=1):
            return Event(sem(name), per_unit, step)
        e_lx = [ev(f"x1_load{h}", 1, 16) for h in range(2)]
        e_lw = [ev(f"tw_load{h}", 1, 16) for h in range(2)]
        e_so = [ev(f"out_store{h}", 1, 16) for h in range(2)]
        e_ng, e_cp, e_cf = ev("normed", KC), ev("coef_mm", E), ev("coef", E)
        e_w1, e_rl, e_hc = ev("w1_mm", E * KC), ev("relu", E * KC), ev("h_coef", E * KC)
        e_w2, e_o = ev("w2_mm", E), ev("result", KC)
        hbank, cbank, acc = psum[0:3], psum[3:5], psum[5:8]

        class Image:
            def __init__(self, b):
                self.n, self.static = b, isinstance(b, int)

        def wait_image(event, eng, b, back=0):
            eng.wait_ge(event.sem, b * 16 + (16 - 16 * back))

        def body(eng, name, b, first):
            for h in range(HALVES):
                u = Unit(b, h)
                u.static = False
                begin = first and h == 0
                if name == "sync":
                    if not first:
                        e_o_b(eng, b, h)
                    src = slice(h * T, (h + 1) * T)
                    e_lx[h].inc_by(eng.dma_start(xb[:, h, :, :], x1_d[bass.ds(b, 1), :, :, src]
                                                 .rearrange("o p k l -> (o p) k l")))
                    e_lw[h].inc_by(eng.dma_start(cw[0:KTOP, h, :],
                                                 w_d[:, bass.ds(b, 1), src].rearrange(
                                                     "k o l -> k (o l)")))
                if name == "pe":
                    wait_image(e_lw[h], eng, b)
                    for e in range(E):
                        if e >= 2:
                            e_cf.wait(eng, u, e - 2)
                        elif not begin:
                            e_cf.wait(eng, u, E - 2 + e, back=1)
                        e_cp.inc_by(eng.matmul(cbank[e % 2][:, :], sel[:, e, :], cw[:, h, :],
                                               start=True, stop=True))
                    e_ng.wait(eng, u)
                    for e in range(E + 1):
                        if e < E:
                            for m in range(KC):
                                q = KC * e + m
                                if e:
                                    e_rl.wait(eng, u, q - KC)
                                elif not begin:
                                    e_rl.wait(eng, u, (E - 1) * KC + m, back=1)
                                for k in range(KC):
                                    mm = eng.matmul(hbank[m][:, :], w1[:, e, k, m * P:(m + 1) * P],
                                                    xg[:, h, k, :], start=(k == 0),
                                                    stop=(k == KC - 1))
                                e_w1.inc_by(mm)
                        if e == 0:
                            if not begin:
                                e_o.wait(eng, u, back=1)
                            for o in range(KC):
                                eng.matmul(acc[o][:, :], b2r[:, o * P:(o + 1) * P], cw[:, h, :],
                                           start=True, stop=False)
                        if e >= 1:
                            for k in range(KC):
                                e_hc.wait(eng, u, KC * (e - 1) + k)
                                for o in range(KC):
                                    mm = eng.matmul(acc[o][:, :],
                                                    w2[:, e - 1, k, o * P:(o + 1) * P],
                                                    hb[:, (e - 1) % 2, k, :], start=False,
                                                    stop=(e == E and k == KC - 1))
                            e_w2.inc_by(mm)
                if name == "act":
                    for e in range(E):
                        if not begin:
                            e_hc.wait(eng, u, KC * e + KC - 1, back=1)
                        e_cp.wait(eng, u, e)
                        e_cf.inc_by(eng.activation(cf[:, e, :], cbank[e % 2][:, :], ACT.Copy))
                    for e in range(E):
                        if e >= 2:
                            e_w2.wait(eng, u, e - 2)
                        elif not begin:
                            e_w2.wait(eng, u, E - 2 + e, back=1)
                        for m in range(KC):
                            e_w1.wait(eng, u, KC * e + m)
                            e_rl.inc_by(eng.activation(hb[:, e % 2, m, :], hbank[m][:, :],
                                                       ACT.Relu, bias=b1[:, e, m:m + 1]))
                if name == "dve":
                    wait_image(e_lx[h], eng, b)
                    if not first:
                        e_w1.wait(eng, u, back=2)
                    for k in range(KC):
                        s = [gn1[:, k, bass.ds(b, 1), i] for i in range(2)]
                        e_ng.inc_by(eng.tensor_scalar(xg[:, h, k, :], xb[:, h, k, :], s[0], s[1],
                                                      ALU.subtract, ALU.mult))
                    for e in range(E):
                        e_cf.wait(eng, u, e)
                        for m in range(KC):
                            e_rl.wait(eng, u, KC * e + m)
                            e_hc.inc_by(eng.tensor_tensor(hb[:, e % 2, m, :], hb[:, e % 2, m, :],
                                                          cf[:, e, :], ALU.mult))
                    if not first:
                        wait_image(e_so[h], eng, b, back=1)
                    e_w2.wait(eng, u)
                    for k in range(KC):
                        e_o.inc_by(eng.tensor_tensor(ob[:, h, k, :], xb[:, h, k, :], acc[k][:, :],
                                                     ALU.add))
                if name == "store":
                    e_o.wait(eng, u)
                    dst = slice(h * T, (h + 1) * T)
                    e_so[h].inc_by(eng.dma_start(out_d[bass.ds(b, 1), :, :, dst].rearrange(
                        "o p k l -> (o p) k l"), ob[:, h, :, :]))

        def e_o_b(eng, b, h):
            u = Unit(b, h)
            u.static = False
            e_o.wait(eng, u, back=2)

        def program(eng, name):
            body(eng, name, 0, True)
            with eng.Fori(1, NB) as b:
                body(eng, name, b, False)

        with nc.Block() as block:
            @block.sync
            def _(eng):
                program(eng, "sync")

            @block.gpsimd
            def _(eng):
                program(eng, "store")
                for h in range(HALVES):
                    eng.wait_ge(e_so[h].sem, 16 * NB)

            @block.scalar
            def _(eng):
                program(eng, "act")

            @block.vector
            def _(eng):
                program(eng, "dve")

            @block.tensor
            def _(eng):
                program(eng, "pe")


def constants():
    c = np.arange(C)
    group = (c[:, None] // GN_CH == c[None, :] // GN_CH).astype(np.float32) / np.float32(GN_CH)
    rows = np.zeros((P, KTOP), np.float32)
    rows[np.arange(KTOP), np.arange(KTOP)] = 1
    return {
        "ident": np.eye(P, dtype=np.float32),
        "mean_w": np.full((P, P), 1.0 / C, np.float32),
        "ones": np.ones((P, P), np.float32),
        "group": group.reshape(KC, P, C).transpose(1, 0, 2),
        "rows": rows,
    }


def kernel(**inputs):
    import numpy as _np
    import concourse.bacc as _bacc
    from concourse.bass_utils import run_bass_kernel_spmd as _run

    v = {k: _np.asarray(x) for k, x in inputs.items()}

    def l0(name):
        return v["L0_conv_" + name]

    def l1(name):
        return v["L1_conv_" + name]

    def cols(x, k):
        return x.reshape(k, P, *x.shape[1:]).swapaxes(0, 1)
    w_m1 = l0("mlp_w1").reshape(KH // 2, 2, P, KC, P).transpose(0, 4, 1, 3, 2)
    w_m2 = l0("mlp_w2").reshape(KC, P, 2, KH // 2, P).transpose(0, 2, 4, 3, 1)
    arrays = {
        "x": v["x"].reshape(NB, C, L),
        "w_in": cols(l0("in_proj_w").T, KC),
        "w_xp": cols(l0("x_proj_w").T, KD),
        "w_dt": l0("dt_proj_w").T,
        "w_out": cols(l0("out_proj_w").T, KD),
        "w_m1": w_m1.reshape(KH // 2, P, 2 * KC * P),
        "w_m2": w_m2.reshape(2 * KC, P, KH // 2 * P),
        "conv_w": cols(l0("conv_w"), KD),
        "conv_b": cols(l0("conv_b"), KD),
        "dt_b": cols(l0("dt_proj_b"), KD),
        "D": cols(l0("D"), KD),
        "A_log": cols(l0("A_log"), KD),
        "ln_w": cols(l0("ln_w"), KC),
        "ln_b": cols(l0("ln_b"), KC),
        "mlp_b1": cols(l0("mlp_b1"), KH),
        "mlp_b2": cols(l0("mlp_b2"), KC),
        "w1e": l1("w1").reshape(E, C, KC, P).transpose(3, 0, 2, 1),
        "w2e": l1("w2").reshape(E, C, KC, P).transpose(3, 0, 2, 1),
        "b1e": l1("b1").reshape(E, KC, P).transpose(2, 0, 1),
        "b2e": l1("b2").reshape(1, E, C),
        "gate_w": cols(l1("gate_w"), KC),
        "gate_b": l1("gate_b").reshape(1, E),
    }
    arrays.update(constants())
    nc = _bacc.Bacc("TRN2", target_bir_lowering=False, num_devices=1)
    feed, args = {}, {}
    for name, x in arrays.items():
        x = _np.ascontiguousarray(x)
        feed[f"in_{name}"] = x
        args[name] = nc.dram_tensor(f"in_{name}", x.shape, F32, kind="ExternalInput").ap()
    out = nc.dram_tensor("out_0", (NB, C, L), F32, kind="ExternalOutput").ap()
    build(nc, args, out)
    r = _run(nc, [feed], core_ids=[0])
    return r.results[0]["out_0"].reshape(v["x"].shape)
```

```python
from contextlib import ExitStack

import numpy as np

import concourse.bass as bass
from concourse import mybir

F32 = mybir.dt.float32
ALU = mybir.AluOpType
ACT = mybir.ActivationFunctionType
AX = mybir.AxisListType

P = 128
NB, C, L = 8, 384, 1024
T = 512
HALVES = L // T
NU = NB * HALVES
DI, NS, RANK = 768, 16, 24
NX = RANK + 2 * NS
HID = 4 * C
E, KTOP = 4, 2
KC, KD, KH = C // P, DI // P, HID // P
CH = T // P
G3 = 3
NG = KD // G3
SLOTS = NS * NG
GN_EPS, LN_EPS = 1e-5, 1e-5
GN_CH = C // 32
HH = KH // 2
DENSE_SLOTS = SLOTS - 1
BANK = 512


class Unit:

    def __init__(self, b, half):
        self.b, self.half, self.n = b, half, b * HALVES + half
        self.static = isinstance(b, int)

    def ds(self):
        return bass.ds(self.b, 1)


class Event:

    def __init__(self, sem, per_unit, step=1, primed=False):
        self.sem, self.per_unit, self.step = sem, per_unit, step
        self.base = per_unit * step if primed else 0

    def prime(self, eng):
        eng.sem_inc(self.sem, self.base)

    def inc_by(self, instruction):
        instruction.then_inc(self.sem, self.step)

    def wait(self, eng, unit, i=None, back=0):
        i = self.per_unit - 1 if i is None else i
        if unit.static and unit.n < back:
            return
        eng.wait_ge(self.sem, unit.n * (self.per_unit * self.step)
                    + (self.base + (i + 1 - back * self.per_unit) * self.step))


def build(nc, a, out):
    with ExitStack() as ctx:
        def sem(name):
            return ctx.enter_context(nc.semaphore(name))

        x_d = a["x"].rearrange("b (k p) l -> b p k l", p=P)
        out_d = out.rearrange("b (k p) l -> b p k l", p=P)
        x1_t = nc.dram_tensor("x1_scratch", (NB, C, L), F32).ap()
        x1_d = x1_t.rearrange("b (k p) l -> b p k l", p=P)
        b_d = nc.dram_tensor("b_rows", (2, NS, T), F32).ap()
        w_d = nc.dram_tensor("top_weights", (KTOP, NB, L), F32).ap()

        def keep(name, shape):
            return ctx.enter_context(nc.sbuf_tensor(name, shape, F32))
        ident = keep("ident", [P, P])
        st1 = keep("st1", [P, NB, HALVES, KC, 6])
        gn0 = keep("gn0", [P, KC, NB, 2])
        eps = keep("eps", [P, 1])
        psum = [ctx.enter_context(nc.psum_tensor(f"bank{i}", [P, BANK], F32)) for i in range(8)]

        layer0(nc, ctx, a, sem, psum, ident, st1, gn0, eps, x_d, x1_d, b_d)
        layer1(nc, ctx, a, sem, psum, ident, st1, eps, x1_d, w_d, out_d)


class Chain:

    def __init__(self, sem):
        self.sem, self.n, self.at = sem, 0, {}

    def add(self, instruction, mark=None):
        instruction.then_inc(self.sem, 1)
        self.n += 1
        if mark is not None:
            self.at[mark] = self.n

    def own(self, eng):
        eng.wait_ge(self.sem, self.n)


def group_stats(dve, act, pe, dv, ac, pc, mv, group, bank, tmp, gn, eps, tag):
    mean_ps = bank[:, 0:KC * NB].rearrange("p (k b) -> p k b", k=KC)
    var_ps = bank[:, KC * NB:2 * KC * NB].rearrange("p (k b) -> p k b", k=KC)
    if pe is not None:
        for src, dst, mark in ((mv[:, :, :, 0], mean_ps, "mean"), (tmp, var_ps, "var")):
            pe.wait_ge(*dv[tag + (" mv" if mark == "mean" else " sq")])
            for m in range(KC):
                for k in range(KC):
                    mm = pe.matmul(dst[:, m, :], group[:, k, m * P:(m + 1) * P], src[:, k, :],
                                   start=(k == 0), stop=(k == KC - 1))
            mm.then_inc(pc[0], 1)
    if dve is not None:
        dve.wait_ge(pc[0], pc[1] + 1)
        dv.add(dve.tensor_copy(gn[:, :, :, 0], mean_ps))
        dv.own(dve)
        dv.add(dve.tensor_tensor(tmp, mv[:, :, :, 0], gn[:, :, :, 0], ALU.subtract))
        dv.own(dve)
        dv.add(dve.tensor_tensor(tmp, tmp, tmp, ALU.mult))
        dv.own(dve)
        dv.add(dve.tensor_tensor(tmp, tmp, mv[:, :, :, 1], ALU.add), tag + " sq")
        dve.wait_ge(ac[0], ac[1] + 1)
        dv.add(dve.reciprocal(gn[:, :, :, 1], gn[:, :, :, 1]), tag + " done")
    if act is not None:
        act.wait_ge(pc[0], pc[1] + 2)
        act.activation(gn[:, :, :, 1], var_ps, ACT.Sqrt, bias=eps[:, 0:1]).then_inc(ac[0], 1)


def layer0(nc, outer, a, sem, psum, ident, st1, gn0, eps, x_d, x1_d, b_d):
    with ExitStack() as ctx:
        def sb(name, shape):
            return ctx.enter_context(nc.sbuf_tensor(name, shape, F32))

        w_in = sb("w_in", [P, KC, 2 * DI])
        w_xp = sb("w_xp", [P, KD, NX])
        w_dt = sb("w_dt", [P, DI])
        w_out = sb("w_out", [P, KD, C])
        conv_w = sb("conv_w", [P, KD, 3])
        conv_b = sb("conv_b", [P, KD])
        dt_b = sb("dt_b", [P, KD])
        d_sk = sb("d_sk", [P, KD])
        a_neg = sb("a_neg", [P, KD, NS])
        ln_w = sb("ln_w", [P, KC])
        ln_b = sb("ln_b", [P, KC])
        b_in = sb("b_in", [P, 2 * KD])
        b1 = sb("b1", [P, KH])
        b2 = sb("b2", [P, KC])
        mean_w = sb("mean_w", [P, P])
        wring = sb("wring", [P, 3, 768])
        xn = sb("xn", [P, 2, KC, T])
        xc = sb("xc", [P, 2, KD, T])
        hr = sb("hr", [P, 3, T])
        xr = sb("xr", [P, KC, T])
        xm = sb("xm", [P, 3, T + 2])
        tt = xm[:, :, 0:T]
        halo = sb("halo", [P, KD, 2])
        rstd = sb("rstd", [P, T])
        dbc = sb("dbc", [P, T])
        dt = sb("dt", [P, 2, KD, T])
        wu = sb("wu", [P, 2, KD, T])
        ct = sb("ct", [P, 2, CH, NS])
        bb = sb("bb", [P, 4, T])
        da = sb("da", [P, 2, G3, T])
        vv = sb("vv", [P, 2, G3, T])
        hh = sb("hh", [P, 2, G3, T])
        hl = sb("hl", [P, NS, KD])
        yy = sb("yy", [P, CH, DI])
        group = vv[:, :, :, :].rearrange("p a g t -> p (a g t)")[:, 0:KC * C].rearrange(
            "p (k c) -> p k c", k=KC)
        st0 = da[:, 0, 0, 0:KC * NB * HALVES * 6].rearrange(
            "p (k b h s) -> p k b h s", k=KC, b=NB, h=HALVES)
        mv0 = da[:, 1, 0, 0:KC * NB * 2].rearrange("p (k b s) -> p k b s", k=KC, b=NB)
        tmp0 = da[:, 1, 1, 0:KC * NB].rearrange("p (k b) -> p k b", k=KC)
        xs = [xn[:, 0, :, :], xn[:, 1, :, :], hr[:, :, :], xr[:, :, :]]

        small = [(conv_w, "conv_w"), (conv_b, "conv_b"), (dt_b, "dt_b"), (d_sk, "D"),
                 (a_neg, "A_log"), (ln_w, "ln_w"), (ln_b, "ln_b"), (b1, "mlp_b1"),
                 (b2, "mlp_b2")]

        s_small, s_group, s_big = sem("small"), sem("group"), sem("big")
        s_xs = [sem(f"stat_x{i}") for i in range(4)]
        s_in = sem("w_in_loaded")
        dv = Chain(sem("b1_dve"))
        s_bact, s_bpe = sem("b1_act"), sem("b1_pe")
        with nc.Block() as block:
            @block.vector
            def _(eng):
                dv.add(eng.memset(w_dt[:, :], 0.0), "w_dt zero")
                dv.add(eng.memset(dbc[:, :], 0.0))
                dv.add(eng.memset(eps[:, :], GN_EPS), "eps")
                for n in range(NU):
                    eng.wait_ge(s_xs[n % 4], 16 * (n // 4 + 1))
                    for k in range(KC):
                        dv.add(eng.bn_stats(st0[:, k, n // 2, n % 2, :], xs[n % 4][:, k, :]),
                               ("stats", n))
                dv.own(eng)
                for k in range(KC):
                    for b in range(NB):
                        dv.add(eng.bn_aggr(mv0[:, k, b, :], st0[:, k, b, :, :].rearrange(
                            "p h s -> p (h s)")), "gn0 mv")
                eng.wait_ge(s_small, 16 * len(small))
                eng.wait_ge(s_bact, 1)
                dv.add(eng.tensor_scalar(a_neg[:, :, :], a_neg[:, :, :], -1.0, None, ALU.mult))
                eng.wait_ge(s_bpe, 1)
                dv.add(eng.tensor_copy(b_in[:, :], psum[1][:, 0:2 * KD]))
                for k in range(KC):
                    dv.add(eng.tensor_scalar(w_in[:, k, :], w_in[:, k, :], ln_w[:, k:k + 1],
                                             None, ALU.mult))
                group_stats(eng, None, None, dv, (s_bact, 1), (s_bpe, 1), mv0, group, psum[0],
                            tmp0, gn0, eps, "gn0")

            marks = {k: (dv.sem, v) for k, v in dv.at.items()}

            @block.sync
            def _(eng):
                for n in range(NU):
                    if n >= 4:
                        eng.wait_ge(*marks[("stats", n - 4)])
                    eng.dma_start(xs[n % 4], x_d[n // 2, :, :, n % 2 * T:(n % 2 + 1) * T])\
                       .then_inc(s_xs[n % 4], 16)

            @block.scalar
            def _(eng):
                for tile, name in small:
                    view = tile[:, :, :] if len(tile.shape) == 3 else tile[:, :]
                    eng.dma_start(view, a[name]).then_inc(s_small, 16)
                eng.dma_start(w_in[:, :, :], a["w_in"]).then_inc(s_in, 16)
                eng.dma_start(group, a["group"]).then_inc(s_group, 16)
                eng.dma_start(ident[:, :], a["ident"]).then_inc(s_big, 16)
                eng.dma_start(mean_w[:, :], a["mean_w"]).then_inc(s_big, 16)
                eng.dma_start(w_xp[:, :, :], a["w_xp"]).then_inc(s_big, 16)
                eng.dma_start(w_out[:, :, :], a["w_out"]).then_inc(s_big, 16)
                eng.wait_ge(*marks["w_dt zero"])
                eng.dma_start(w_dt[0:RANK, :], a["w_dt"]).then_inc(s_big, 16)
                eng.wait_ge(s_small, 16 * len(small))
                eng.activation(a_neg[:, :, :], a_neg[:, :, :], ACT.Exp).then_inc(s_bact, 1)
                eng.wait_ge(*marks["eps"])
                group_stats(None, eng, None, marks, (s_bact, 1), (s_bpe, 1), mv0, group,
                            psum[0], tmp0, gn0, eps, "gn0")
                eng.wait_ge(s_big, 16 * 5)

            @block.tensor
            def _(eng):
                eng.wait_ge(s_in, 16)
                eng.wait_ge(s_small, 16 * len(small))
                for m in range(2 * KD):
                    for k in range(KC):
                        mm = eng.matmul(psum[1][:, m:m + 1], w_in[:, k, m * P:(m + 1) * P],
                                        ln_b[:, k:k + 1], start=(k == 0), stop=(k == KC - 1))
                mm.then_inc(s_bpe, 1)
                eng.wait_ge(s_group, 16)
                group_stats(None, None, eng, marks, None, (s_bpe, 1), mv0, group, psum[0],
                            tmp0, gn0, eps, "gn0")

        def ev(name, per_unit, step=1, primed=False):
            return Event(sem(name), per_unit, step, primed)
        e_bb = [ev(f"b_row{i}", NS // 4, 16) for i in range(4)]
        e_da, e_v, e_scan = ev("dA", SLOTS), ev("v", SLOTS), ev("scanned", SLOTS)
        e_ht, e_mac, e_hl = ev("hT", SLOTS * CH), ev("mac", SLOTS * CH), ev("h_last", SLOTS)
        e_yt, e_yz = ev("yT", KD), ev("y_skip", KD)
        e_zp, e_sz, e_gt = ev("z_proj", KD), ev("silu_z", KD), ev("gated", KD)
        e_op, e_t = ev("out_proj", KC), ev("t_copied", KC)
        e_m1, e_ge, e_m2 = (
            ev("mlp1", KH, primed=True), ev("gelu", KH), ev("mlp2", 2 * KC, primed=True))
        e_x1, e_bn = ev("x1", 2 * KC), ev("x1_stats", KC, primed=True)
        e_xr, e_st = ev("xr_loaded", 1, 16), ev("x1_stored", 1, 16, primed=True)
        e_ws = [ev(f"mlp_w{i}", 4, 16) for i in range(3)]
        e_xin = ev("x_loaded", 1, 16)
        e_gn, e_mu, e_ce = ev("gn_applied", KC), ev("ln_mean", 1), ev("centred", KC)
        e_sq, e_var, e_rs = ev("squares", KC), ev("ln_var", 1), ev("ln_rstd", 2)
        e_xh = ev("xhat", KC)
        e_xm, e_xe, e_hi = ev("xm_proj", KD), ev("xm_copied", KD), ev("halo_in", 2)
        e_cv, e_hs, e_xc = ev("conv", 3 * KD), ev("halo_saved", 2), ev("xc", KD)
        e_xp, e_db, e_bw = ev("x_proj", 1), ev("dbc", 1), ev("b_stored", 1, 16)
        e_ct, e_cc = ev("C_T", 1), ev("C_copied", 1)
        e_dp, e_sp = ev("dt_proj", KD), ev("softplus", 4 * KD)
        e_dt, e_w = ev("dt", KD), ev("dt_x", KD)

        order = ([("post", "Y", j, (e_yz, j)) for j in range(KD)]
                 + [("post", "Z", j, (e_sz, j)) for j in range(KD)]
                 + [("post", "O", m, (e_t, m)) for m in range(KC)]
                 + [("post", "M1", m, (e_ge, m)) for m in (0, 1)]
                 + [("pre", "MU", 0, (e_ce, KC - 1))]
                 + [("post", "M1", m, (e_ge, m)) for m in (2, 3)]
                 + [("pre", "VAR", 0, (e_rs, 0))]
                 + [("post", "M1", m, (e_ge, m)) for m in (4, 5)]
                 + [("post", "M2", m, (e_x1, m)) for m in range(KC)]
                 + [("post", "M1", m, (e_ge, m)) for m in range(HH, KH)]
                 + [("post", "M2", m, (e_x1, m)) for m in range(KC, 2 * KC)]
                 + [("pre", "XM", j, (e_xe, j)) for j in range(KD)]
                 + [("pre", "XP", 0, (e_db, 0)), ("pre", "CT", 0, (e_cc, 0))]
                 + [("pre", "DT", j, (e_sp, 4 * j + 1)) for j in range(KD)])
        NDB = 4
        place = {(s[1], s[2]): i for i, s in enumerate(order)}
        dense, ht = psum[4:8], psum[0:4]

        def bank(name, i):
            return dense[place[(name, i)] % NDB]

        def bank_free(eng, units, name, i):
            pos = place[(name, i)]
            same = [s for q, s in enumerate(order[:pos]) if q % NDB == pos % NDB and s[0] in units]
            if same:
                kind, _, _, (event, at) = same[-1]
                event.wait(eng, units[kind], at)
                return
            if "pre" in units:
                kind, unit, back = "pre", units["pre"], 1
            elif units["post"].n + 1 < NU:
                kind, unit, back = "pre", units["post"], -1
            else:
                kind, unit, back = "post", units["post"], 1
            same = [s for q, s in enumerate(order) if q % NDB == pos % NDB and s[0] == kind]
            event, at = same[-1][3]
            event.wait(eng, unit, at, back=back)

        def scan_sync(eng, u, k):
            if k % NG:
                return
            n = k // NG
            if n == 0:
                e_bw.wait(eng, u)
            if n >= 4:
                e_v.wait(eng, u, NG * (n - 4) + NG - 1)
            else:
                e_v.wait(eng, u, NG * (n + NS - 4) + NG - 1, back=1)
            e_bb[n % 4].inc_by(eng.dma_start(
                bb[:, n % 4, :], b_d[u.half, n:n + 1, :].to_broadcast([P, T])))

        def scan_pool(eng, u, k):
            n, g = k // NG, k % NG
            if n == 0:
                e_w.wait(eng, u, G3 * g + G3 - 1)
            if g == 0:
                e_bb[n % 4].wait(eng, u, n // 4)
            if k >= 2:
                e_scan.wait(eng, u, k - 2)
            else:
                e_scan.wait(eng, u, SLOTS - 2 + k, back=1)
            e_v.inc_by(eng.tensor_tensor(
                vv[:, k % 2, :, :], wu[:, u.half, G3 * g:G3 * g + G3, :],
                bb[:, n % 4:n % 4 + 1, :].to_broadcast([P, G3, T]), ALU.mult))

        def scan_act(eng, u, k):
            n, g = k // NG, k % NG
            if n == 0:
                e_dt.wait(eng, u, G3 * g + G3 - 1)
            if k >= 2:
                e_scan.wait(eng, u, k - 2)
            else:
                e_scan.wait(eng, u, SLOTS - 2 + k, back=1)
            for i in range(G3):
                j = G3 * g + i
                ins = eng.activation(da[:, k % 2, i, :], dt[:, u.half, j, :], ACT.Exp,
                                     scale=a_neg[:, j, n:n + 1])
            e_da.inc_by(ins)

        def scan_dve(eng, u, k):
            n, g = k // NG, k % NG
            e_da.wait(eng, u, k)
            e_v.wait(eng, u, k)
            if k >= 2:
                e_ht.wait(eng, u, CH * (k - 2) + CH - 1)
                e_hl.wait(eng, u, k - 2)
            else:
                e_ht.wait(eng, u, CH * (SLOTS - 2 + k) + CH - 1, back=1)
                e_hl.wait(eng, u, SLOTS - 2 + k, back=1)
            for i in range(G3):
                j = G3 * g + i
                start = hl[:, n, j:j + 1] if u.half else 0.0
                ins = eng.tensor_tensor_scan(hh[:, k % 2, i, :], da[:, k % 2, i, :],
                                             vv[:, k % 2, i, :], start, ALU.mult, ALU.add)
            e_scan.inc_by(ins)

        def mac_dve(eng, u, k):
            n, g = k // NG, k % NG
            if k == 0:
                e_cc.wait(eng, u)
                e_yt.wait(eng, u, back=1)
            if k >= NG:
                e_mac.wait(eng, u, CH * (k - NG) + CH - 1)
            for c in range(CH):
                e_ht.wait(eng, u, CH * k + c)
                y = yy[:, c, G3 * P * g:G3 * P * (g + 1)]
                scale = ct[:, u.half, c, n:n + 1]
                if n == 0:
                    ins = eng.tensor_scalar(y, ht[c][:, 0:G3 * P], scale, None, ALU.mult)
                else:
                    ins = eng.scalar_tensor_tensor(out=y, in0=ht[c][:, 0:G3 * P], scalar=scale,
                                                   in1=y, op0=ALU.mult, op1=ALU.add)
                e_mac.inc_by(ins)

        def last_dve(eng, u, k):
            n, g = k // NG, k % NG
            e_scan.wait(eng, u, k)
            e_hl.inc_by(eng.tensor_copy(hl[:, n, G3 * g:G3 * g + G3], hh[:, k % 2, :, T - 1]))

        def scan_pe(eng, u, k):
            e_scan.wait(eng, u, k)
            for c in range(CH):
                if k >= 1:
                    e_mac.wait(eng, u, CH * (k - 1) + c)
                else:
                    e_mac.wait(eng, u, CH * (SLOTS - 1) + c, back=1)
                for i in range(G3):
                    ins = eng.transpose(ht[c][:, i * P:(i + 1) * P],
                                        hh[:, k % 2, i, c * P:(c + 1) * P], ident[:, :])
                e_ht.inc_by(ins)

        def hid(u, m):
            return hr[:, m - HH, :] if HH <= m < HH + 3 else xc[:, u.half, m % 9, :]

        def stream(q):
            h, r = q // 6, q % 6
            return a["w_m1"][3 * h + r] if r < 3 else a["w_m2"][2 * (r - 3) + h]

        def stream_sync(eng, u, q):
            h, r = (q - 3) // 6, (q - 3) % 6
            if q < 3:
                e_m2.wait(eng, u, KC + q, back=1)
            elif r < 3:
                e_m1.wait(eng, u, HH * h + 2 * r + 1)
            else:
                e_m2.wait(eng, u, KC * h + r - 3)
            e_ws[q % 3].inc_by(eng.dma_start(wring[:, q % 3, :], stream(q)))

        def stages_of(units):
            st = {}
            u, v = units.get("post"), units.get("pre")

            def y_stage(j):
                def pe(eng):
                    if j == 0:
                        e_mac.wait(eng, u)
                    bank_free(eng, units, "Y", j)
                    for c in range(CH):
                        ins = eng.transpose(bank("Y", j)[:, c * P:(c + 1) * P],
                                            yy[:, c, j * P:(j + 1) * P], ident[:, :])
                    e_yt.inc_by(ins)
                    yield 0.5

                def dve(eng):
                    e_yt.wait(eng, u, j)
                    e_yz.inc_by(eng.scalar_tensor_tensor(
                        out=xc[:, u.half, j, :], in0=xc[:, u.half, j, :],
                        scalar=d_sk[:, j:j + 1], in1=bank("Y", j)[:, :],
                        op0=ALU.mult, op1=ALU.add))
                st[("Y", j)] = (0.5, {"pe": (0, pe), "dve": (1, dve)})

            def z_stage(j):
                def pe(eng):
                    bank_free(eng, units, "Z", j)
                    for k in range(KC):
                        ins = eng.matmul(bank("Z", j)[:, :], w_in[:, k, DI + j * P:DI + (j + 1) * P],
                                         xn[:, u.half, k, :], start=(k == 0), stop=(k == KC - 1))
                        if k == KC - 1:
                            e_zp.inc_by(ins)
                        yield 1

                def act(eng):
                    if j == 2:
                        last_pre(eng)
                    for q in range(j - 2, j + 1):
                        if q >= 3:
                            e_gt.wait(eng, u, q - 3)
                        e_zp.wait(eng, u, q)
                        e_sz.inc_by(eng.activation(hr[:, q % 3, :], bank("Z", q)[:, :], ACT.Silu,
                                                   bias=b_in[:, KD + q:KD + q + 1]))

                def dve(eng):
                    for q in range(j - 2, j + 1):
                        e_sz.wait(eng, u, q)
                        e_yz.wait(eng, u, q)
                        e_gt.inc_by(eng.tensor_tensor(xc[:, u.half, q, :], xc[:, u.half, q, :],
                                                      hr[:, q % 3, :], ALU.mult))
                st[("Z", j)] = (3, {"pe": (0, pe)}
                                | ({"act": (1, act), "dve": (1, dve)} if j % 3 == 2 else {}))

            def last_pre(eng):
                if not (u.static and u.n >= NU - 1):
                    e_dt.wait(eng, u, back=-1)

            def o_stage(m):
                def pe(eng):
                    bank_free(eng, units, "O", m)
                    e_gt.wait(eng, u)
                    for k in range(KD):
                        ins = eng.matmul(bank("O", m)[:, :], w_out[:, k, m * P:(m + 1) * P],
                                         xc[:, u.half, k, :], start=(k == 0), stop=(k == KD - 1))
                        if k == KD - 1:
                            e_op.inc_by(ins)
                        yield 1

                def act(eng):
                    if m == 0:
                        e_m1.wait(eng, u, back=1)
                    e_op.wait(eng, u, m)
                    e_t.inc_by(eng.activation(tt[:, m, :], bank("O", m)[:, :], ACT.Copy))
                st[("O", m)] = (6, {"pe": (0, pe), "act": (1, act)})

            def m1_stage(m):
                q = m // 2 + (3 if m >= HH else 0)

                def pe(eng):
                    bank_free(eng, units, "M1", m)
                    if m == 0:
                        e_t.wait(eng, u)
                    if m % 2 == 0:
                        e_ws[q % 3].wait(eng, u, q // 3)
                    w = wring[:, q % 3, :].rearrange("p (m k c) -> p m k c", m=2, k=KC)
                    for k in range(KC):
                        ins = eng.matmul(bank("M1", m)[:, :], w[:, m % 2, k, :], tt[:, k, :],
                                         start=(k == 0), stop=(k == KC - 1))
                        if k == KC - 1:
                            e_m1.inc_by(ins)
                        yield 1

                def act(eng):
                    if m == HH + 2 and v:
                        e_var.wait(eng, v)
                    if m == KH - 1:
                        e_m2.wait(eng, u, KC - 1)
                    for i in range(m - 2, m + 1):
                        e_m1.wait(eng, u, i)
                        e_ge.inc_by(eng.activation(hid(u, i), bank("M1", i)[:, :], ACT.Gelu,
                                                   bias=b1[:, i:i + 1]))
                st[("M1", m)] = (3, {"pe": (0, pe)} | ({"act": (1, act)} if m % 3 == 2 else {}))

            def m2_stage(i):
                h, m = i // KC, i % KC
                q = 3 + 6 * h + m

                def pe(eng):
                    bank_free(eng, units, "M2", i)
                    e_ws[q % 3].wait(eng, u, q // 3)
                    w = wring[:, q % 3, :].rearrange("p (k c) -> p k c", k=HH)
                    for k in range(HH):
                        if m == 0:
                            e_ge.wait(eng, u, HH * h + k)
                        ins = eng.matmul(bank("M2", i)[:, :], w[:, k, :], hid(u, HH * h + k),
                                         start=(k == 0), stop=(k == HH - 1))
                        if k == HH - 1:
                            e_m2.inc_by(ins)
                        yield 1

                def dve(eng):
                    if i == 0:
                        e_xr.wait(eng, u)
                    e_m2.wait(eng, u, i)
                    if h == 0:
                        e_x1.inc_by(eng.scalar_tensor_tensor(
                            out=xr[:, m, :], in0=bank("M2", i)[:, :], scalar=b2[:, m:m + 1],
                            in1=xr[:, m, :], op0=ALU.add, op1=ALU.add))
                        return
                    e_x1.wait(eng, u, m)
                    e_x1.inc_by(eng.tensor_tensor(xr[:, m, :], xr[:, m, :], bank("M2", i)[:, :],
                                                  ALU.add))
                    e_x1.wait(eng, u, i)
                    e_bn.inc_by(eng.bn_stats(
                        st1[:, u.ds(), u.half, m, :].rearrange("p o s -> p (o s)"), xr[:, m, :]))
                st[("M2", i)] = (HH, {"pe": (0, pe), "dve": (1, dve)})

            def load_x():
                def sync(eng):
                    e_zp.wait(eng, v, back=2)
                    e_xin.inc_by(eng.dma_start(xn[:, v.half, :, :], x_half(x_d, v)))

                def dve(eng):
                    e_xin.wait(eng, v)
                    for k in range(KC):
                        s = [gn0[:, k, v.ds(), i] for i in range(2)]
                        e_gn.inc_by(eng.tensor_scalar(
                            xn[:, v.half, k, :], xn[:, v.half, k, :], s[0], s[1],
                            ALU.subtract, ALU.mult))
                return sync, dve

            def mu_stage():
                def pe(eng):
                    bank_free(eng, units, "MU", 0)
                    e_gn.wait(eng, v)
                    for k in range(KC):
                        ins = eng.matmul(bank("MU", 0)[:, :], mean_w[:, :], xn[:, v.half, k, :],
                                         start=(k == 0), stop=(k == KC - 1))
                    e_mu.inc_by(ins)
                    yield 3

                def dve(eng):
                    e_mu.wait(eng, v)
                    for k in range(KC):
                        e_ce.inc_by(eng.tensor_tensor(xn[:, v.half, k, :], xn[:, v.half, k, :],
                                                      bank("MU", 0)[:, :], ALU.subtract))

                def act(eng):
                    e_gt.wait(eng, v, back=2)
                    for k in range(KC):
                        e_ce.wait(eng, v, k)
                        e_sq.inc_by(eng.activation(hr[:, k, :], xn[:, v.half, k, :], ACT.Square))
                st[("MU", 0)] = (3, {"pe": (0, pe), "dve": (1, dve), "act": (1, act)})

            def var_stage():
                def pe(eng):
                    bank_free(eng, units, "VAR", 0)
                    for k in range(KC):
                        e_sq.wait(eng, v, k)
                        ins = eng.matmul(bank("VAR", 0)[:, :], mean_w[:, :], hr[:, k, :],
                                         start=(k == 0), stop=(k == KC - 1))
                    e_var.inc_by(ins)
                    yield 3

                def act(eng):
                    e_xh.wait(eng, v, back=1)
                    e_var.wait(eng, v)
                    e_rs.inc_by(eng.activation(rstd[:, :], bank("VAR", 0)[:, :], ACT.Ln,
                                               bias=eps[:, 0:1]))
                    e_rs.wait(eng, v, 0)
                    e_rs.inc_by(eng.activation(rstd[:, :], rstd[:, :], ACT.Exp, scale=-0.5))

                def dve(eng):
                    e_rs.wait(eng, v)
                    for k in range(KC):
                        e_xh.inc_by(eng.tensor_tensor(xn[:, v.half, k, :], xn[:, v.half, k, :],
                                                      rstd[:, :], ALU.mult))
                st[("VAR", 0)] = (3, {"pe": (0, pe), "act": (1, act), "dve": (2, dve)})

            def xm_stage(j):
                q = j // 3

                def pe(eng):
                    bank_free(eng, units, "XM", j)
                    e_xh.wait(eng, v)
                    for k in range(KC):
                        ins = eng.matmul(bank("XM", j)[:, :], w_in[:, k, j * P:(j + 1) * P],
                                         xn[:, v.half, k, :], start=(k == 0), stop=(k == KC - 1))
                        if k == KC - 1:
                            e_xm.inc_by(ins)
                        yield 1

                def act(eng):
                    if q:
                        e_hs.wait(eng, v, 0)
                        e_cv.wait(eng, v, 8)
                    elif j == 0:
                        e_hs.wait(eng, v, back=1)
                        e_cv.wait(eng, v, back=1)
                        e_dt.wait(eng, v, back=1)
                        e_m1.wait(eng, v, back=2)
                    e_xm.wait(eng, v, j)
                    e_xe.inc_by(eng.activation(xm[:, j % 3, 2:T + 2], bank("XM", j)[:, :],
                                               ACT.Identity, bias=b_in[:, j:j + 1]))

                def dve(eng):
                    edge = xm[:, :, 0:2]
                    if q:
                        e_cv.wait(eng, v, 8)
                    else:
                        e_cv.wait(eng, v, back=1)
                        e_m1.wait(eng, v, back=2)
                    if v.half:
                        e_hs.wait(eng, v, q, back=1)
                        ins = eng.tensor_copy(edge, halo[:, 3 * q:3 * q + 3, :])
                    else:
                        ins = eng.memset(edge, 0.0)
                    e_hi.inc_by(ins)
                    e_xe.wait(eng, v, j)
                    e_hi.wait(eng, v, q)
                    e_hs.inc_by(eng.tensor_copy(halo[:, 3 * q:3 * q + 3, :], xm[:, :, T:T + 2]))
                    if q:
                        e_xc.wait(eng, v, 2)
                    else:
                        e_m2.wait(eng, v, back=2)
                    for tap in range(3):
                        for i in range(3 * q, 3 * q + 3):
                            src = xm[:, i % 3, 2 - tap:T + 2 - tap]
                            w = conv_w[:, i, 2 - tap:3 - tap]
                            if tap == 0:
                                ins = eng.tensor_scalar(hr[:, i % 3, :], src, w, None, ALU.mult)
                            else:
                                e_cv.wait(eng, v, 9 * q + 3 * (tap - 1) + i % 3)
                                ins = eng.scalar_tensor_tensor(
                                    out=hr[:, i % 3, :], in0=src, scalar=w, in1=hr[:, i % 3, :],
                                    op0=ALU.mult, op1=ALU.add)
                            e_cv.inc_by(ins)

                def silu(eng):
                    if q == 0:
                        e_m2.wait(eng, v, back=2)
                    for i in range(3 * q, 3 * q + 3):
                        e_cv.wait(eng, v, 9 * q + 6 + i % 3)
                        e_xc.inc_by(eng.activation(xc[:, v.half, i, :], hr[:, i % 3, :], ACT.Silu,
                                                   bias=conv_b[:, i:i + 1]))
                st[("XM", j)] = (3, {"pe": (0, pe), "act": (1, act)}
                                 | ({"dve": (1, dve), "act2": (2, silu)} if j % 3 == 2 else {}))

            def xp_stage():
                def pe(eng):
                    bank_free(eng, units, "XP", 0)
                    for k in range(KD):
                        e_xc.wait(eng, v, k)
                        ins = eng.matmul(bank("XP", 0)[0:NX, :], w_xp[:, k, :],
                                         xc[:, v.half, k, :], start=(k == 0), stop=(k == KD - 1))
                        if k == KD - 1:
                            e_xp.inc_by(ins)
                        yield 1

                def act(eng):
                    e_bw.wait(eng, v, back=1)
                    e_dp.wait(eng, v, back=1)
                    e_ct.wait(eng, v, back=1)
                    e_xp.wait(eng, v)
                    e_db.inc_by(eng.activation(dbc[0:NX, :], bank("XP", 0)[0:NX, :], ACT.Copy))

                def sync(eng):
                    e_db.wait(eng, v)
                    e_bw.inc_by(eng.dma_start(b_d[v.half, :, :], dbc[RANK:RANK + NS, :]))
                st[("XP", 0)] = (6, {"pe": (0, pe), "act": (0, act), "sync": (1, sync)})

            def ct_stage():
                def pe(eng):
                    e_db.wait(eng, v)
                    bank_free(eng, units, "CT", 0)
                    for c in range(CH):
                        ins = eng.transpose(bank("CT", 0)[:, c * P:(c + 1) * P],
                                            dbc[:, c * P:(c + 1) * P], ident[:, :])
                    e_ct.inc_by(ins)
                    yield 0.5

                def dve(eng):
                    e_ct.wait(eng, v)
                    c_t = bank("CT", 0)[:, :].rearrange("p (c r) -> p c r", c=CH)
                    e_cc.inc_by(eng.tensor_copy(ct[:, v.half, :, :], c_t[:, :, RANK + NS:NX]))
                st[("CT", 0)] = (0.5, {"pe": (0, pe), "dve": (1, dve)})

            def dt_stage(j):
                def pe(eng):
                    bank_free(eng, units, "DT", j)
                    e_dp.inc_by(eng.matmul(bank("DT", j)[:, :], w_dt[:, j * P:(j + 1) * P],
                                           dbc[:, :], start=True, stop=True))
                    yield 1

                sa, sb_ = tt[:, j % 3, :], hr[:, j % 3, :]

                def act(eng):
                    if j >= 3:
                        e_dt.wait(eng, v, j - 3)
                    e_dp.wait(eng, v, j)
                    ps = bank("DT", j)[:, :]
                    e_sp.inc_by(eng.activation(sb_, ps, ACT.Abs, bias=dt_b[:, j:j + 1]))
                    e_sp.inc_by(eng.activation(sa, ps, ACT.Identity, bias=dt_b[:, j:j + 1]))
                    e_sp.wait(eng, v, 4 * j)
                    e_sp.inc_by(eng.activation(sb_, sb_, ACT.Exp, scale=-1.0))
                    e_sp.wait(eng, v, 4 * j + 2)
                    e_sp.inc_by(eng.activation(sb_, sb_, ACT.Ln, bias=1.0))

                def dve(eng):
                    if j == 0:
                        e_da.wait(eng, v, back=2)
                        e_v.wait(eng, v, back=2)
                    e_sp.wait(eng, v, 4 * j + 3)
                    e_dt.inc_by(eng.scalar_tensor_tensor(
                        out=dt[:, v.half, j, :], in0=sa, scalar=0.0, in1=sb_,
                        op0=ALU.max, op1=ALU.add))
                    e_dt.wait(eng, v, j)
                    e_w.inc_by(eng.tensor_tensor(wu[:, v.half, j, :], dt[:, v.half, j, :],
                                                 xc[:, v.half, j, :], ALU.mult))
                st[("DT", j)] = (1, {"pe": (0, pe), "act": (j // 3, act), "dve": (1 + j // 3, dve)})

            def load_xr(eng):
                e_st.wait(eng, u, back=1)
                e_bn.wait(eng, u, back=1)
                e_xr.inc_by(eng.dma_start(xr[:, :, :], x_half(x_d, u)))

            def store_x1(eng):
                e_x1.wait(eng, u)
                e_st.inc_by(eng.dma_start(x_half(x1_d, u), xr[:, :, :]))

            loads = {}
            if u:
                for j in range(KD):
                    y_stage(j)
                    z_stage(j)
                for m in range(KC):
                    o_stage(m)
                for m in range(KH):
                    m1_stage(m)
                for i in range(2 * KC):
                    m2_stage(i)
                loads[("Y", 0)] = [load_xr] + [lambda eng, q=q: stream_sync(eng, u, q)
                                               for q in range(3)]
                for q in range(3, 12):
                    h, r = (q - 3) // 6, (q - 3) % 6
                    at = ("M1", HH * h + 2 * r + 1) if r < 3 else ("M2", KC * h + r - 3)
                    loads[at] = [lambda eng, q=q: stream_sync(eng, u, q)]
                loads[("M2", 2 * KC - 1)] = [store_x1]
            if v:
                sync, gn = load_x()
                mu_stage()
                var_stage()
                for j in range(KD):
                    xm_stage(j)
                xp_stage()
                ct_stage()
                for j in range(KD):
                    dt_stage(j)
                before = ("O", 0) if u else ("MU", 0)
                loads.setdefault(before, []).append(sync)
                st[before][1]["dve0"] = (0 if u else -1, gn)
            return st, loads

        def x_half(d, u):
            s = slice(u.half * T, (u.half + 1) * T)
            if u.static:
                return d[u.b, :, :, s]
            return d[u.ds(), :, :, s].rearrange("o p k l -> (o p) k l")

        def step(eng, name, scan=None, posts=None, pres=None):
            units = {k: x for k, x in (("post", posts), ("pre", pres)) if x}
            st, loads = stages_of(units)
            total = sum(s[0] for s in st.values())
            per = total / DENSE_SLOTS
            end = SLOTS + 6
            at = [[] for _ in range(end)]
            pe_parts, done, latest = [], 0.0, 0
            for _, sname, i, _ in order:
                if (sname, i) not in st:
                    continue
                work, parts = st[(sname, i)]
                done += work
                slot = min(int((done - 1e-6) / per), SLOTS - 1)
                if name == "pe":
                    pe_parts.append(parts["pe"][1])
                for e, (lag, f) in sorted(parts.items(), key=lambda x: x[0][-1] != "0"):
                    if e.rstrip("02") == name and e != "pe":
                        latest = max(slot + lag, latest)
                        at[latest].append(f)
                if name == "sync":
                    for f in loads.get((sname, i), []):
                        at[slot].append(f)
            if name == "pe":
                def run():
                    for f in pe_parts:
                        yield from f(eng)
                work_left, spent = run(), 0.0
            for k in range(end):
                if scan and k < SLOTS:
                    if name == "sync":
                        if k == 0:
                            for q in range(0, 2 * NG, NG):
                                scan_sync(eng, scan, q)
                        if k + 2 * NG < SLOTS and k % NG == 0:
                            scan_sync(eng, scan, k + 2 * NG)
                    if name == "pool":
                        scan_pool(eng, scan, k)
                    if name == "act":
                        scan_act(eng, scan, k)
                    if name == "dve":
                        scan_dve(eng, scan, k)
                    if name == "pe":
                        scan_pe(eng, scan, k)
                for f in at[k]:
                    f(eng)
                if name == "pe":
                    while spent < (k + 1) * per or k == end - 1:
                        w = next(work_left, None)
                        if w is None:
                            break
                        spent += w
                if scan and name == "dve" and k < SLOTS:
                    if k >= 1:
                        mac_dve(eng, scan, k - 1)
                    last_dve(eng, scan, k)
                    if k == SLOTS - 1:
                        mac_dve(eng, scan, k)

        def program(eng, name):
            step(eng, name, pres=Unit(0, 0))
            step(eng, name, scan=Unit(0, 0), pres=Unit(0, 1))
            with eng.Fori(0, NB - 1) as i:
                step(eng, name, scan=Unit(i, 1), posts=Unit(i, 0), pres=Unit(i + 1, 0))
                step(eng, name, scan=Unit(i + 1, 0), posts=Unit(i, 1), pres=Unit(i + 1, 1))
            step(eng, name, scan=Unit(NB - 1, 1), posts=Unit(NB - 1, 0))
            step(eng, name, posts=Unit(NB - 1, 1))

        with nc.Block() as block:
            @block.sync
            def _(eng):
                for event in (e_m1, e_m2, e_bn, e_st):
                    event.prime(eng)
                program(eng, "sync")
                e_st.wait(eng, Unit(NB - 1, 1))

            @block.gpsimd
            def _(eng):
                program(eng, "pool")

            @block.scalar
            def _(eng):
                program(eng, "act")

            @block.vector
            def _(eng):
                program(eng, "dve")

            @block.tensor
            def _(eng):
                program(eng, "pe")


def layer1(nc, outer, a, sem, psum, ident, st1, eps, x1_d, w_d, out_d):
    with ExitStack() as ctx:
        def sb(name, shape):
            return ctx.enter_context(nc.sbuf_tensor(name, shape, F32))

        w1 = sb("w1e", [P, E, KC, C])
        w2 = sb("w2e", [P, E, KC, C])
        b1 = sb("b1e", [P, E, KC])
        gn1 = sb("gn1", [P, KC, NB, 2])
        sel = sb("sel", [P, E, P])
        b2r = sb("b2r", [P, C])
        xb = sb("xb", [P, 2, KC, T])
        xg = sb("xg", [P, 2, KC, T])
        cw = sb("cw", [P, 2, T])
        cf = sb("cf", [P, E, T])
        hb = sb("hb", [P, 2, KC, T])
        ob = sb("ob", [P, 2, KC, T])
        group = sb("group1", [P, KC, C])
        mv = sb("mv1", [P, KC, NB, 2])
        tmp = sb("tmp1", [P, KC, NB])
        gate_w = sb("gate_w", [P, KC, E])
        gate_b = sb("gate_b", [P, E])
        rows = sb("rows", [P, KTOP])
        ones = sb("ones", [P, P])
        gs = sb("gs", [P, KC, NB, E])
        gm = sb("gm", [P, KC, NB, E])
        b2b = sb("b2b", [P, E, C])
        NT = NB * L // P
        lg = sb("lg", [P, NT, E])
        off = sb("off", [P, NB, E])
        mx = sb("mx", [P, NT])
        sm = sb("sm", [P, NT])
        ge = sb("ge", [P, 6, NT])
        rk = sb("rk", [P, NT, E])
        top = sb("top", [P, KTOP, NT, E])
        pf = sb("pf", [P, KTOP, E])
        pres = sb("pres", [P, KTOP, E])
        tw = sb("tw", [P, KTOP, NT])
        twt = sb("twt", [P, P])
        se = sb("se", [P, E])

        s_c, s_w = sem("b3_small"), sem("b3_weights")
        s_x = [sem(f"gate_x{i}") for i in range(HALVES)]
        s_pe, s_act, s_tw = sem("b3_pe"), sem("b3_act"), sem("b3_tw")
        s_lg = sem("b3_logits")
        dv = Chain(sem("b3_dve"))
        small = [(group, "group"), (gate_w, "gate_w"), (rows, "rows"), (ones, "ones"), (b1, "b1e")]
        n_small = len(small) + 2
        pairs = [(i, j) for i in range(E) for j in range(i + 1, E)]
        with nc.Block() as block:
            @block.vector
            def _(eng):
                for h in range(2):
                    dv.add(eng.memset(cw[:, h, :], 0.0))
                for k in range(KC):
                    for b in range(NB):
                        dv.add(eng.bn_aggr(mv[:, k, b, :], st1[:, b, :, k, :]), "gn1 mv")
                group_stats(eng, None, None, dv, (s_act, 0), (s_pe, 0), mv, group, psum[0], tmp[:, :, :],
                            gn1, eps, "gn1")
                dv.own(eng)
                eng.wait_ge(s_c, 16 * n_small)
                for k in range(KC):
                    dv.add(eng.tensor_tensor(
                        gs[:, k, :, :], gate_w[:, k:k + 1, :].to_broadcast([P, NB, E]),
                        gn1[:, k, :, 1:2].to_broadcast([P, NB, E]), ALU.mult))
                dv.own(eng)
                dv.at["gs"] = dv.n
                for k in range(KC):
                    dv.add(eng.tensor_tensor(gm[:, k, :, :], gs[:, k, :, :],
                                             gn1[:, k, :, 0:1].to_broadcast([P, NB, E]),
                                             ALU.mult), "gm")
                eng.wait_ge(s_pe, 3)
                offp = psum[2][:, 0:NB * E].rearrange("p (b e) -> p b e", b=NB)
                dv.add(eng.tensor_tensor(off[:, :, :], gate_b[:, None, :].to_broadcast([P, NB, E]),
                                         offp, ALU.subtract))
                dv.own(eng)
                eng.wait_ge(s_lg, NB + 1)
                lgp = psum[1][:, 0:NT * E].rearrange("p (b t e) -> p b t e", b=NB, e=E)
                dv.add(eng.tensor_tensor(
                    lg[:, :, :].rearrange("p (b t) e -> p b t e", b=NB), lgp,
                    off[:, :, None, :].to_broadcast([P, NB, NT // NB, E]), ALU.add))
                dv.own(eng)
                dv.add(eng.tensor_reduce(mx[:, :], lg[:, :, :], AX.X, ALU.max))
                dv.own(eng)
                dv.add(eng.tensor_tensor(lg[:, :, :], lg[:, :, :],
                                         mx[:, :, None].to_broadcast([P, NT, E]), ALU.subtract),
                       "shifted")
                eng.wait_ge(s_act, 2)
                dv.add(eng.tensor_reduce(sm[:, :], lg[:, :, :], AX.X, ALU.add))
                dv.own(eng)
                dv.add(eng.reciprocal(sm[:, :], sm[:, :]))
                dv.own(eng)
                dv.add(eng.tensor_tensor(lg[:, :, :], lg[:, :, :],
                                         sm[:, :, None].to_broadcast([P, NT, E]), ALU.mult))
                dv.own(eng)
                for q, (i, j) in enumerate(pairs):
                    dv.add(eng.tensor_tensor(ge[:, q, :], lg[:, :, i], lg[:, :, j], ALU.is_ge))
                for i in range(E):
                    dv.add(eng.memset(rk[:, :, i], float(E - 1 - i)))
                dv.own(eng)
                for q, (i, j) in enumerate(pairs):
                    dv.add(eng.tensor_tensor(rk[:, :, i], rk[:, :, i], ge[:, q, :], ALU.subtract))
                    dv.own(eng)
                    dv.add(eng.tensor_tensor(rk[:, :, j], rk[:, :, j], ge[:, q, :], ALU.add))
                    dv.own(eng)
                for k in range(KTOP):
                    dv.add(eng.tensor_scalar(top[:, k, :, :], rk[:, :, :], float(k), None,
                                             ALU.is_equal))
                dv.own(eng)
                for k in range(KTOP):
                    dv.add(eng.tensor_reduce(pf[:, k, :], top[:, k, :, :].rearrange(
                        "p t e -> p e t"), AX.X, ALU.max), "chosen")
                dv.own(eng)
                for k in range(KTOP):
                    dv.add(eng.tensor_tensor(top[:, k, :, :], top[:, k, :, :], lg[:, :, :],
                                             ALU.mult))
                dv.own(eng)
                for k in range(KTOP):
                    dv.add(eng.tensor_reduce(tw[:, k, :], top[:, k, :, :], AX.X, ALU.add))
                dv.own(eng)
                dv.add(eng.tensor_tensor(tw[:, 1, :], tw[:, 1, :], tw[:, 0, :], ALU.subtract),
                       "second - first")
                eng.wait_ge(s_act, 3)
                dv.add(eng.tensor_scalar(tw[:, 0, :], tw[:, 1, :], 1.0, None, ALU.add))
                dv.own(eng)
                dv.add(eng.reciprocal(tw[:, 0, :], tw[:, 0, :]))
                dv.own(eng)
                dv.add(eng.tensor_tensor(tw[:, 1, :], tw[:, 1, :], tw[:, 0, :], ALU.mult),
                       "weights")
                eng.wait_ge(s_pe, 4)
                dv.add(eng.tensor_scalar(
                    pres[:, :, :], psum[3][:, 0:KTOP * E].rearrange("p (k e) -> p k e", k=KTOP),
                    0.0, None, ALU.is_gt))
                dv.own(eng)
                dv.add(eng.tensor_scalar(se[:, :], pres[:, 0, :], rows[:, 0:1], None, ALU.mult))
                dv.own(eng)
                dv.add(eng.scalar_tensor_tensor(out=se[:, :], in0=pres[:, 1, :],
                                                scalar=rows[:, 1:2], in1=se[:, :],
                                                op0=ALU.mult, op1=ALU.add))
                dv.own(eng)
                for e in range(E):
                    dv.add(eng.tensor_scalar(sel[:, e, :], ones[:, :], se[:, e:e + 1], None,
                                             ALU.mult))
                    if e == 0:
                        ins = eng.tensor_scalar(b2r[:, :], b2b[:, e, :], se[:, e:e + 1], None,
                                                ALU.mult)
                    else:
                        ins = eng.scalar_tensor_tensor(out=b2r[:, :], in0=b2b[:, e, :],
                                                       scalar=se[:, e:e + 1], in1=b2r[:, :],
                                                       op0=ALU.mult, op1=ALU.add)
                    dv.add(ins)
                    dv.own(eng)
                eng.wait_ge(s_pe, 5)
                dv.add(eng.tensor_copy(twt[:, :], psum[4][:, 0:P]), "twt")

            marks = {k: (dv.sem, v) for k, v in dv.at.items()}

            @block.sync
            def _(eng):
                for tile, name in small:
                    view = tile[:, :, :] if len(tile.shape) == 3 else tile[:, :]
                    eng.dma_start(view, a[name]).then_inc(s_c, 16)
                eng.dma_start(gate_b[:, :], a["gate_b"].to_broadcast([P, E])).then_inc(s_c, 16)
                eng.dma_start(b2b[:, :, :], a["b2e"].to_broadcast([P, E, C])).then_inc(s_c, 16)
                eng.sem_inc(s_lg, 1)
                with eng.Fori(0, NB) as b:
                    for h in range(HALVES):
                        eng.wait_ge(s_lg, b + 1)
                        eng.dma_start(xb[:, h, :, :],
                                      x1_d[bass.ds(b, 1), :, :, h * T:(h + 1) * T].rearrange(
                                          "o p k l -> (o p) k l")).then_inc(s_x[h], 16)
                eng.wait_ge(*marks["twt"])
                eng.dma_start(w_d.rearrange("k b (c l) -> (k b c) l", l=P), twt[:, :])\
                   .then_inc(s_tw, 16)
                eng.wait_ge(s_tw, 16)

            @block.scalar
            def _(eng):
                eng.dma_start(w1[:, :, :, :], a["w1e"]).then_inc(s_w, 16)
                eng.dma_start(w2[:, :, :, :], a["w2e"]).then_inc(s_w, 16)
                group_stats(None, eng, None, marks, (s_act, 0), (s_pe, 0), mv, group, psum[0],
                            tmp[:, :, :], gn1, eps, "gn1")
                eng.wait_ge(*marks["shifted"])
                eng.activation(lg[:, :, :], lg[:, :, :], ACT.Exp).then_inc(s_act, 1)
                eng.wait_ge(*marks["second - first"])
                eng.activation(tw[:, 1, :], tw[:, 1, :], ACT.Exp).then_inc(s_act, 1)
                eng.wait_ge(s_w, 32)

            @block.tensor
            def _(eng):
                eng.wait_ge(s_c, 16 * n_small)
                group_stats(None, None, eng, marks, None, (s_pe, 0), mv, group, psum[0], tmp[:, :, :],
                            gn1, eps, "gn1")
                eng.wait_ge(*marks["gm"])
                for k in range(KC):
                    mm = eng.matmul(psum[2][:, 0:NB * E], ones[:, :], gm[:, k, :, :].rearrange(
                        "p b e -> p (b e)"), start=(k == 0), stop=(k == KC - 1))
                mm.then_inc(s_pe, 1)
                with eng.Fori(0, NB) as b:
                    for h in range(HALVES):
                        eng.wait_ge(s_x[h], 16 * b + 16)
                        for c in range(CH):
                            at = (h * CH + c) * E
                            for k in range(KC):
                                mm = eng.matmul(
                                    psum[1][:, bass.ds(b * (HALVES * CH * E) + at, E)],
                                    xb[:, h, k, c * P:(c + 1) * P],
                                    gs[:, k, bass.ds(b, 1), :].rearrange("p o e -> p (o e)"),
                                    start=(k == 0), stop=(k == KC - 1))
                    mm.then_inc(s_lg, 1)
                eng.wait_ge(*marks["chosen"])
                eng.matmul(psum[3][:, 0:KTOP * E], ones[:, :], pf[:, :, :].rearrange(
                    "p k e -> p (k e)"), start=True, stop=True).then_inc(s_pe, 1)
                eng.wait_ge(*marks["weights"])
                eng.transpose(psum[4][:, 0:P], tw[:, :, :].rearrange("p k t -> p (k t)"),
                              ident[:, :]).then_inc(s_pe, 1)

        def ev(name, per_unit, step=1):
            return Event(sem(name), per_unit, step)
        e_lx = [ev(f"x1_load{h}", 1, 16) for h in range(2)]
        e_lw = [ev(f"tw_load{h}", 1, 16) for h in range(2)]
        e_so = [ev(f"out_store{h}", 1, 16) for h in range(2)]
        e_ng, e_cp, e_cf = ev("normed", KC), ev("coef_mm", E), ev("coef", E)
        e_w1, e_rl, e_hc = ev("w1_mm", E * KC), ev("relu", E * KC), ev("h_coef", E * KC)
        e_w2, e_o = ev("w2_mm", E), ev("result", KC)
        hbank, cbank, acc = psum[0:3], psum[3:5], psum[5:8]

        class Image:
            def __init__(self, b):
                self.n, self.static = b, isinstance(b, int)

        def wait_image(event, eng, b, back=0):
            eng.wait_ge(event.sem, b * 16 + (16 - 16 * back))

        def body(eng, name, b, first):
            for h in range(HALVES):
                u = Unit(b, h)
                u.static = False
                begin = first and h == 0
                if name == "sync":
                    if not first:
                        e_o_b(eng, b, h)
                    src = slice(h * T, (h + 1) * T)
                    e_lx[h].inc_by(eng.dma_start(xb[:, h, :, :], x1_d[bass.ds(b, 1), :, :, src]
                                                 .rearrange("o p k l -> (o p) k l")))
                    e_lw[h].inc_by(eng.dma_start(cw[0:KTOP, h, :],
                                                 w_d[:, bass.ds(b, 1), src].rearrange(
                                                     "k o l -> k (o l)")))
                if name == "pe":
                    wait_image(e_lw[h], eng, b)
                    for e in range(E):
                        if e >= 2:
                            e_cf.wait(eng, u, e - 2)
                        elif not begin:
                            e_cf.wait(eng, u, E - 2 + e, back=1)
                        e_cp.inc_by(eng.matmul(cbank[e % 2][:, :], sel[:, e, :], cw[:, h, :],
                                               start=True, stop=True))
                    e_ng.wait(eng, u)
                    for e in range(E + 1):
                        if e < E:
                            for m in range(KC):
                                q = KC * e + m
                                if e:
                                    e_rl.wait(eng, u, q - KC)
                                elif not begin:
                                    e_rl.wait(eng, u, (E - 1) * KC + m, back=1)
                                for k in range(KC):
                                    mm = eng.matmul(hbank[m][:, :], w1[:, e, k, m * P:(m + 1) * P],
                                                    xg[:, h, k, :], start=(k == 0),
                                                    stop=(k == KC - 1))
                                e_w1.inc_by(mm)
                        if e == 0:
                            if not begin:
                                e_o.wait(eng, u, back=1)
                            for o in range(KC):
                                eng.matmul(acc[o][:, :], b2r[:, o * P:(o + 1) * P], cw[:, h, :],
                                           start=True, stop=False)
                        if e >= 1:
                            for k in range(KC):
                                e_hc.wait(eng, u, KC * (e - 1) + k)
                                for o in range(KC):
                                    mm = eng.matmul(acc[o][:, :],
                                                    w2[:, e - 1, k, o * P:(o + 1) * P],
                                                    hb[:, (e - 1) % 2, k, :], start=False,
                                                    stop=(e == E and k == KC - 1))
                            e_w2.inc_by(mm)
                if name == "act":
                    for e in range(E):
                        if not begin:
                            e_hc.wait(eng, u, KC * e + KC - 1, back=1)
                        e_cp.wait(eng, u, e)
                        e_cf.inc_by(eng.activation(cf[:, e, :], cbank[e % 2][:, :], ACT.Copy))
                    for e in range(E):
                        if e >= 2:
                            e_w2.wait(eng, u, e - 2)
                        elif not begin:
                            e_w2.wait(eng, u, E - 2 + e, back=1)
                        for m in range(KC):
                            e_w1.wait(eng, u, KC * e + m)
                            e_rl.inc_by(eng.activation(hb[:, e % 2, m, :], hbank[m][:, :],
                                                       ACT.Relu, bias=b1[:, e, m:m + 1]))
                if name == "dve":
                    wait_image(e_lx[h], eng, b)
                    if not first:
                        e_w1.wait(eng, u, back=2)
                    for k in range(KC):
                        s = [gn1[:, k, bass.ds(b, 1), i] for i in range(2)]
                        e_ng.inc_by(eng.tensor_scalar(xg[:, h, k, :], xb[:, h, k, :], s[0], s[1],
                                                      ALU.subtract, ALU.mult))
                    for e in range(E):
                        e_cf.wait(eng, u, e)
                        for m in range(KC):
                            e_rl.wait(eng, u, KC * e + m)
                            e_hc.inc_by(eng.tensor_tensor(hb[:, e % 2, m, :], hb[:, e % 2, m, :],
                                                          cf[:, e, :], ALU.mult))
                    if not first:
                        wait_image(e_so[h], eng, b, back=1)
                    e_w2.wait(eng, u)
                    for k in range(KC):
                        e_o.inc_by(eng.tensor_tensor(ob[:, h, k, :], xb[:, h, k, :], acc[k][:, :],
                                                     ALU.add))
                if name == "store":
                    e_o.wait(eng, u)
                    dst = slice(h * T, (h + 1) * T)
                    e_so[h].inc_by(eng.dma_start(out_d[bass.ds(b, 1), :, :, dst].rearrange(
                        "o p k l -> (o p) k l"), ob[:, h, :, :]))

        def e_o_b(eng, b, h):
            u = Unit(b, h)
            u.static = False
            e_o.wait(eng, u, back=2)

        def program(eng, name):
            body(eng, name, 0, True)
            with eng.Fori(1, NB) as b:
                body(eng, name, b, False)

        with nc.Block() as block:
            @block.sync
            def _(eng):
                program(eng, "sync")

            @block.gpsimd
            def _(eng):
                program(eng, "store")
                for h in range(HALVES):
                    eng.wait_ge(e_so[h].sem, 16 * NB)

            @block.scalar
            def _(eng):
                program(eng, "act")

            @block.vector
            def _(eng):
                program(eng, "dve")

            @block.tensor
            def _(eng):
                program(eng, "pe")


def constants():
    c = np.arange(C)
    group = (c[:, None] // GN_CH == c[None, :] // GN_CH).astype(np.float32) / np.float32(GN_CH)
    rows = np.zeros((P, KTOP), np.float32)
    rows[np.arange(KTOP), np.arange(KTOP)] = 1
    return {
        "ident": np.eye(P, dtype=np.float32),
        "mean_w": np.full((P, P), 1.0 / C, np.float32),
        "ones": np.ones((P, P), np.float32),
        "group": group.reshape(KC, P, C).transpose(1, 0, 2),
        "rows": rows,
    }


def kernel(**inputs):
    import numpy as _np
    import concourse.bacc as _bacc
    from concourse.bass_utils import run_bass_kernel_spmd as _run

    v = {k: _np.asarray(x) for k, x in inputs.items()}

    def l0(name):
        return v["L0_conv_" + name]

    def l1(name):
        return v["L1_conv_" + name]

    def cols(x, k):
        return x.reshape(k, P, *x.shape[1:]).swapaxes(0, 1)
    w_m1 = l0("mlp_w1").reshape(KH // 2, 2, P, KC, P).transpose(0, 4, 1, 3, 2)
    w_m2 = l0("mlp_w2").reshape(KC, P, 2, KH // 2, P).transpose(0, 2, 4, 3, 1)
    arrays = {
        "x": v["x"].reshape(NB, C, L),
        "w_in": cols(l0("in_proj_w").T, KC),
        "w_xp": cols(l0("x_proj_w").T, KD),
        "w_dt": l0("dt_proj_w").T,
        "w_out": cols(l0("out_proj_w").T, KD),
        "w_m1": w_m1.reshape(KH // 2, P, 2 * KC * P),
        "w_m2": w_m2.reshape(2 * KC, P, KH // 2 * P),
        "conv_w": cols(l0("conv_w"), KD),
        "conv_b": cols(l0("conv_b"), KD),
        "dt_b": cols(l0("dt_proj_b"), KD),
        "D": cols(l0("D"), KD),
        "A_log": cols(l0("A_log"), KD),
        "ln_w": cols(l0("ln_w"), KC),
        "ln_b": cols(l0("ln_b"), KC),
        "mlp_b1": cols(l0("mlp_b1"), KH),
        "mlp_b2": cols(l0("mlp_b2"), KC),
        "w1e": l1("w1").reshape(E, C, KC, P).transpose(3, 0, 2, 1),
        "w2e": l1("w2").reshape(E, C, KC, P).transpose(3, 0, 2, 1),
        "b1e": l1("b1").reshape(E, KC, P).transpose(2, 0, 1),
        "b2e": l1("b2").reshape(1, E, C),
        "gate_w": cols(l1("gate_w"), KC),
        "gate_b": l1("gate_b").reshape(1, E),
    }
    arrays.update(constants())
    nc = _bacc.Bacc("TRN2", target_bir_lowering=False, num_devices=1)
    feed, args = {}, {}
    for name, x in arrays.items():
        x = _np.ascontiguousarray(x)
        feed[f"in_{name}"] = x
        args[name] = nc.dram_tensor(f"in_{name}", x.shape, F32, kind="ExternalInput").ap()
    out = nc.dram_tensor("out_0", (NB, C, L), F32, kind="ExternalOutput").ap()
    build(nc, args, out)
    r = _run(nc, [feed], core_ids=[0])
    return r.results[0]["out_0"].reshape(v["x"].shape)
```

```python
from contextlib import ExitStack

import numpy as np

import concourse.bass as bass
from concourse import mybir

F32 = mybir.dt.float32
F32R = mybir.dt.float32r
ALU = mybir.AluOpType
ACT = mybir.ActivationFunctionType
AX = mybir.AxisListType

P = 128
NB, C, L = 8, 384, 1024
T = 512
HALVES = L // T
NU = NB * HALVES
DI, NS, RANK = 768, 16, 24
NX = RANK + 2 * NS
HID = 4 * C
E, KTOP = 4, 2
KC, KD, KH = C // P, DI // P, HID // P
CH = T // P
G3 = 3
NG = KD // G3
SLOTS = NS * NG
GN_EPS, LN_EPS = 1e-5, 1e-5
GN_CH = C // 32
NBB = 3
HH = KH // 2
DVE_QUOTA = 3
SOFTPLUS_LAG = 1
DT_LAG = 2
SILU_Z_LAG = 1
GATE_LAG = 2
XHAT_LAG = 2
X1_LAG = 1
XM_COPY_LAG = 0
CONV_LAG = 1
SILU_LAG = 3
DENSE_SLOTS = SLOTS - 1
BANK = 512


class Unit:

    def __init__(self, b, half):
        self.b, self.half, self.n = b, half, b * HALVES + half
        self.static = isinstance(b, int)

    def ds(self):
        return bass.ds(self.b, 1)


class Event:

    def __init__(self, sem, per_unit, step=1, primed=False):
        self.sem, self.per_unit, self.step = sem, per_unit, step
        self.base = per_unit * step if primed else 0

    def prime(self, eng):
        eng.sem_inc(self.sem, self.base)

    def inc_by(self, instruction):
        instruction.then_inc(self.sem, self.step)

    def wait(self, eng, unit, i=None, back=0):
        i = self.per_unit - 1 if i is None else i
        if unit.static and unit.n < back:
            return
        eng.wait_ge(self.sem, unit.n * (self.per_unit * self.step)
                    + (self.base + (i + 1 - back * self.per_unit) * self.step))


def build(nc, a, out):
    with ExitStack() as ctx:
        def sem(name):
            return ctx.enter_context(nc.semaphore(name))

        x_d = a["x"].rearrange("b (k p) l -> b p k l", p=P)
        out_d = out.rearrange("b (k p) l -> b p k l", p=P)
        x1_t = nc.dram_tensor("x1_scratch", (NB, C, L), F32).ap()
        x1_d = x1_t.rearrange("b (k p) l -> b p k l", p=P)
        b_d = nc.dram_tensor("b_rows", (2, NS, T), F32).ap()
        w_d = nc.dram_tensor("top_weights", (KTOP, NB, L), F32).ap()

        def keep(name, shape):
            return ctx.enter_context(nc.sbuf_tensor(name, shape, F32))
        ident = keep("ident", [P, P])
        st1 = keep("st1", [P, NB, HALVES, KC, 6])
        gn0 = keep("gn0", [P, KC, NB, 2])
        eps = keep("eps", [P, 2])
        psum = [ctx.enter_context(nc.psum_tensor(f"bank{i}", [P, BANK], F32)) for i in range(8)]

        dt = keep("dt", [P, 2, KD, T])
        wu = keep("wu", [P, 2, KD, T])
        vv = keep("vv", [P, 2, G3, T])
        consts = Experts(a, dt, wu, vv)

        layer0(nc, a, sem, psum, ident, st1, gn0, eps, x_d, x1_d, b_d, dt, wu, vv, consts)
        layer1(nc, a, sem, psum, ident, st1, eps, x1_d, w_d, out_d, consts, dt, wu)


class Experts:

    def __init__(self, a, dt, wu, vv):
        def flat(t):
            return t[:, :, :, :].rearrange("p a j t -> p (a j t)")

        def weights(t):
            return flat(t)[:, 0:E * KC * C].rearrange("p (e k c) -> p e k c", e=E, k=KC)
        self.w1, self.w2 = weights(dt), weights(wu)
        at = 0
        views = {}
        for name, width in (("group", KC * C), ("ones", P), ("b1", E * KC), ("b2", KC * E),
                            ("gate_w", KC * E), ("gate_b", E)):
            views[name] = flat(vv)[:, at:at + width]
            at += width
        self.spare = flat(vv)[:, at:]
        self.group = views["group"].rearrange("p (k c) -> p k c", k=KC)
        self.ones, self.gate_b = views["ones"], views["gate_b"]
        self.b1 = views["b1"].rearrange("p (e k) -> p e k", e=E)
        self.b2 = views["b2"].rearrange("p (k e) -> p k e", k=KC)
        self.gate_w = views["gate_w"].rearrange("p (k e) -> p k e", k=KC)
        self.loads = [(self.group, a["group"]), (self.ones, a["ones"]),
                      (self.gate_w, a["gate_w"]), (self.gate_b, a["gate_b"].to_broadcast([P, E])),
                      (self.b1, a["b1e"]), (self.b2, a["b2e"]),
                      (self.w1, a["w1e"]), (self.w2, a["w2e"])]


class Spare:

    def __init__(self, consts):
        self.left = consts.spare

    def take(self, width):
        part, self.left = self.left[:, 0:width], self.left[:, width:]
        return part


class Chain:

    def __init__(self, sem):
        self.sem, self.n, self.at = sem, 0, {}

    def add(self, instruction, mark=None):
        instruction.then_inc(self.sem, 1)
        self.n += 1
        if mark is not None:
            self.at[mark] = self.n

    def own(self, eng):
        eng.wait_ge(self.sem, self.n)


def group_stats(dve, act, pe, dv, ac, pc, mv, group, bank, tmp, gn, eps, tag):
    mean_ps = bank[:, 0:KC * NB].rearrange("p (k b) -> p k b", k=KC)
    var_ps = bank[:, KC * NB:2 * KC * NB].rearrange("p (k b) -> p k b", k=KC)
    if pe is not None:
        for src, dst, mark in ((mv[:, :, :, 0], mean_ps, "mean"), (tmp, var_ps, "var")):
            pe.wait_ge(*dv[tag + (" mv" if mark == "mean" else " sq")])
            for m in range(KC):
                for k in range(KC):
                    mm = pe.matmul(dst[:, m, :], group[:, k, m * P:(m + 1) * P], src[:, k, :],
                                   start=(k == 0), stop=(k == KC - 1))
            mm.then_inc(pc[0], 1)
    if dve is not None:
        dve.wait_ge(pc[0], pc[1] + 1)
        dv.add(dve.tensor_copy(gn[:, :, :, 0], mean_ps))
        dv.own(dve)
        dv.add(dve.tensor_tensor(tmp, mv[:, :, :, 0], gn[:, :, :, 0], ALU.subtract))
        dv.own(dve)
        dv.add(dve.tensor_tensor(tmp, tmp, tmp, ALU.mult))
        dv.own(dve)
        dv.add(dve.tensor_tensor(tmp, tmp, mv[:, :, :, 1], ALU.add), tag + " sq")
        dve.wait_ge(ac[0], ac[1] + 1)
        dv.add(dve.reciprocal(gn[:, :, :, 1], gn[:, :, :, 1]), tag + " done")
    if act is not None:
        act.wait_ge(pc[0], pc[1] + 2)
        act.activation(gn[:, :, :, 1], var_ps, ACT.Sqrt, bias=eps[:, 0:1]).then_inc(ac[0], 1)


def layer0(nc, a, sem, psum, ident, st1, gn0, eps, x_d, x1_d, b_d, dt, wu, vv, consts):
    with ExitStack() as ctx:
        def sb(name, shape):
            return ctx.enter_context(nc.sbuf_tensor(name, shape, F32))

        w_in = sb("w_in", [P, KC, 2 * DI])
        w_xp = sb("w_xp", [P, KD, NX])
        w_dt = sb("w_dt", [P, DI])
        w_out = sb("w_out", [P, KD, C])
        conv_w = sb("conv_w", [P, KD, 3])
        conv_b = sb("conv_b", [P, KD])
        dt_b = sb("dt_b", [P, KD])
        d_sk = sb("d_sk", [P, KD])
        a_neg = sb("a_neg", [P, KD, NS])
        b_in = sb("b_in", [P, 2 * KD])
        b1 = sb("b1", [P, KH])
        b2 = sb("b2", [P, KC])
        mean_w = eps[:, 1:2].to_broadcast([P, P])
        wring = sb("wring", [P, 3, 768])
        xn = sb("xn", [P, 2, KC, T])
        xc = sb("xc", [P, 2, KD, T])
        hr = sb("hr", [P, 3, T])
        xr = sb("xr", [P, KC, T])
        xm = sb("xm", [P, 3, T + 2])
        tt = xm[:, :, 0:T]
        halo = sb("halo", [P, KD, 2])
        hx = sb("hx", [P, 3, T])
        rstd = hx[:, 0, :]
        dbc = sb("dbc", [P, T])
        ct = sb("ct", [P, 2, CH, NS])
        bb = sb("bb", [P, NBB, T])
        da = sb("da", [P, 2, G3, T])
        hh = sb("hh", [P, 2, G3, T])
        hl = sb("hl", [P, NS, KD])
        yy = sb("yy", [P, CH, DI])
        group = vv[:, :, :, :].rearrange("p a g t -> p (a g t)")[:, 0:KC * C].rearrange(
            "p (k c) -> p k c", k=KC)
        st0 = da[:, 0, 0, 0:KC * NB * HALVES * 6].rearrange(
            "p (k b h s) -> p k b h s", k=KC, b=NB, h=HALVES)
        mv0 = da[:, 1, 0, 0:KC * NB * 2].rearrange("p (k b s) -> p k b s", k=KC, b=NB)
        ln_w, ln_b = da[:, 1, 2, 0:KC], da[:, 1, 2, KC:2 * KC]
        tmp0 = da[:, 1, 1, 0:KC * NB].rearrange("p (k b) -> p k b", k=KC)
        xs = [xn[:, 0, :, :], xn[:, 1, :, :], hr[:, :, :], xr[:, :, :]]

        small = [(conv_w, "conv_w"), (conv_b, "conv_b"), (dt_b, "dt_b"), (d_sk, "D"),
                 (a_neg, "A_log"), (ln_w, "ln_w"), (ln_b, "ln_b"), (b1, "mlp_b1"),
                 (b2, "mlp_b2")]

        s_small, s_group, s_big = sem("small"), sem("group"), sem("big")
        s_xs = [sem(f"stat_x{i}") for i in range(4)]
        s_in = sem("w_in_loaded")
        dv = Chain(sem("b1_dve"))
        s_bact, s_bpe = sem("b1_act"), sem("b1_pe")
        with nc.Block() as block:
            @block.vector
            def _(eng):
                dv.add(eng.memset(w_dt[:, :], 0.0), "w_dt zero")
                dv.add(eng.memset(dbc[:, :], 0.0))
                dv.add(eng.memset(eps[:, 0:1], GN_EPS), "eps")
                dv.add(eng.memset(eps[:, 1:2], 1.0 / C))
                for n in range(NU):
                    eng.wait_ge(s_xs[n % 4], 16 * (n // 4 + 1))
                    for k in range(KC):
                        dv.add(eng.bn_stats(st0[:, k, n // 2, n % 2, :], xs[n % 4][:, k, :]),
                               ("stats", n))
                dv.own(eng)
                for k in range(KC):
                    for b in range(NB):
                        dv.add(eng.bn_aggr(mv0[:, k, b, :], st0[:, k, b, :, :].rearrange(
                            "p h s -> p (h s)")), "gn0 mv")
                eng.wait_ge(s_small, 16 * len(small))
                eng.wait_ge(s_bact, 1)
                dv.add(eng.tensor_scalar(a_neg[:, :, :], a_neg[:, :, :], -1.0, None, ALU.mult))
                eng.wait_ge(s_bpe, 1)
                dv.add(eng.tensor_copy(b_in[:, :], psum[1][:, 0:2 * KD]))
                for k in range(KC):
                    dv.add(eng.tensor_scalar(w_in[:, k, :], w_in[:, k, :], ln_w[:, k:k + 1],
                                             None, ALU.mult))
                group_stats(eng, None, None, dv, (s_bact, 1), (s_bpe, 1), mv0, group, psum[0],
                            tmp0, gn0, eps, "gn0")

            marks = {k: (dv.sem, v) for k, v in dv.at.items()}

            @block.sync
            def _(eng):
                for n in range(NU):
                    if n >= 4:
                        eng.wait_ge(*marks[("stats", n - 4)])
                    eng.dma_start(xs[n % 4], x_d[n // 2, :, :, n % 2 * T:(n % 2 + 1) * T])\
                       .then_inc(s_xs[n % 4], 16)

            @block.scalar
            def _(eng):
                for tile, name in small:
                    view = tile[:, :, :] if len(tile.shape) == 3 else tile[:, :]
                    eng.dma_start(view, a[name]).then_inc(s_small, 16)
                eng.dma_start(w_in[:, :, :], a["w_in"]).then_inc(s_in, 16)
                eng.dma_start(group, a["group"]).then_inc(s_group, 16)
                eng.dma_start(ident[:, :], a["ident"]).then_inc(s_big, 16)
                eng.dma_start(w_xp[:, :, :], a["w_xp"]).then_inc(s_big, 16)
                eng.dma_start(w_out[:, :, :], a["w_out"]).then_inc(s_big, 16)
                eng.wait_ge(*marks["w_dt zero"])
                eng.dma_start(w_dt[0:RANK, :], a["w_dt"]).then_inc(s_big, 16)
                eng.wait_ge(s_small, 16 * len(small))
                eng.activation(a_neg[:, :, :], a_neg[:, :, :], ACT.Exp).then_inc(s_bact, 1)
                eng.wait_ge(*marks["eps"])
                group_stats(None, eng, None, marks, (s_bact, 1), (s_bpe, 1), mv0, group,
                            psum[0], tmp0, gn0, eps, "gn0")
                eng.wait_ge(s_big, 16 * 4)

            @block.tensor
            def _(eng):
                eng.wait_ge(s_in, 16)
                eng.wait_ge(s_small, 16 * len(small))
                for m in range(2 * KD):
                    for k in range(KC):
                        mm = eng.matmul(psum[1][:, m:m + 1], w_in[:, k, m * P:(m + 1) * P],
                                        ln_b[:, k:k + 1], start=(k == 0), stop=(k == KC - 1))
                mm.then_inc(s_bpe, 1)
                eng.wait_ge(s_group, 16)
                group_stats(None, None, eng, marks, None, (s_bpe, 1), mv0, group, psum[0],
                            tmp0, gn0, eps, "gn0")

        def ev(name, per_unit, step=1, primed=False):
            return Event(sem(name), per_unit, step, primed)
        e_bb = [ev(f"b_row{i}", len(range(i, NS, NBB)), 16) for i in range(NBB)]
        e_da, e_v, e_scan = ev("dA", SLOTS), ev("v", SLOTS), ev("scanned", SLOTS)
        e_ht, e_mac, e_hl = ev("hT", SLOTS * CH), ev("mac", SLOTS * CH), ev("h_last", SLOTS)
        e_yt, e_yz = ev("yT", KD), ev("y_skip", KD, primed=True)
        e_zp, e_sz, e_gt = ev("z_proj", KD), ev("silu_z", KD, primed=True), ev("gated", KD)
        e_op, e_t = ev("out_proj", KC), ev("t_copied", KC, primed=True)
        e_m1, e_ge, e_m2 = (
            ev("mlp1", KH, primed=True), ev("gelu", KH, primed=True),
            ev("mlp2", 2 * KC, primed=True))
        e_x1, e_bn = ev("x1", 2 * KC, primed=True), ev("x1_stats", KC, primed=True)
        e_xr, e_st = ev("xr_loaded", 1, 16), ev("x1_stored", 1, 16, primed=True)
        e_ws = [ev(f"mlp_w{i}", 4, 16) for i in range(3)]
        e_xin = ev("x_loaded", 1, 16)
        e_gn, e_mu, e_ce = ev("gn_applied", KC), ev("ln_mean", 1), ev("centred", KC)
        e_sq, e_var, e_rs = ev("squares", KC), ev("ln_var", 1), ev("ln_rstd", 2)
        e_xh = ev("xhat", KC)
        e_xm, e_xe, e_hi = ev("xm_proj", KD), ev("xm_copied", KD), ev("halo_in", KD)
        e_cv, e_hs, e_xc = ev("conv", 3 * KD), ev("halo_saved", KD), ev("xc", KD)
        e_xp, e_db, e_bw = ev("x_proj", 1), ev("dbc", 1), ev("b_stored", 1, 16)
        e_ct, e_cc = ev("C_T", 1), ev("C_copied", 1)
        e_dp, e_sp = ev("dt_proj", KD), ev("softplus", 4 * KD)
        e_dt, e_w = ev("dt", KD), ev("dt_x", KD)

        order = ([("post", "Y", j, (e_yz, j)) for j in range(KD)]
                 + [("post", "Z", j, (e_sz, j)) for j in range(KD)]
                 + [("post", "O", m, (e_t, m)) for m in range(KC)]
                 + [("post", "M1", m, (e_ge, m)) for m in (0, 1)]
                 + [("pre", "MU", 0, (e_ce, KC - 1))]
                 + [("post", "M1", m, (e_ge, m)) for m in (2, 3)]
                 + [("pre", "VAR", 0, (e_rs, 0))]
                 + [("post", "M1", m, (e_ge, m)) for m in (4, 5)]
                 + [("post", "M2", m, (e_x1, m)) for m in range(KC)]
                 + [("post", "M1", m, (e_ge, m)) for m in range(HH, KH)]
                 + [("pre", "XM", 0, (e_xe, 0)),
                    ("pre", "XM", 1, (e_xe, 1)),
                    ("pre", "XM", 2, (e_xe, 2)),
                    ("pre", "XM", 3, (e_xe, 3)),
                    ("pre", "XM", 4, (e_xe, 4)),
                    ("pre", "XM", 5, (e_xe, 5)),
                    ("post", "M2", KC + 0, (e_x1, KC + 0)),
                    ("pre", "XP", 0, (e_db, 0)),
                    ("post", "M2", KC + 1, (e_x1, KC + 1)),
                    ("pre", "CT", 0, (e_cc, 0)),
                    ("pre", "DT", 0, (e_sp, 4 * 0 + 1)),
                    ("pre", "DT", 1, (e_sp, 4 * 1 + 1)),
                    ("pre", "DT", 2, (e_sp, 4 * 2 + 1)),
                    ("post", "M2", KC + 2, (e_x1, KC + 2)),
                    ("pre", "DT", 3, (e_sp, 4 * 3 + 1)),
                    ("pre", "DT", 4, (e_sp, 4 * 4 + 1)),
                    ("pre", "DT", 5, (e_sp, 4 * 5 + 1))])
        NDB = 4
        place = {(s[1], s[2]): i for i, s in enumerate(order)}
        dense, ht = psum[4:8], psum[0:4]

        def bank(name, i):
            return dense[place[(name, i)] % NDB]

        def bank_free(eng, units, name, i):
            pos = place[(name, i)]
            same = [s for q, s in enumerate(order[:pos]) if q % NDB == pos % NDB and s[0] in units]
            if same:
                kind, _, _, (event, at) = same[-1]
                event.wait(eng, units[kind], at)
                return
            post, pre = units.get("post"), units.get("pre")
            before = [("pre", pre, 1) if pre else ("pre", post, -1),
                      ("post", post, 1) if post else ("post", pre, 3)]
            for kind, unit, back in before:
                same = [s for q, s in enumerate(order) if q % NDB == pos % NDB and s[0] == kind]
                if same and not (unit.static and unit.n - back >= NU):
                    event, at = same[-1][3]
                    event.wait(eng, unit, at, back=back)

        def scan_sync(eng, u, k):
            if k % NG:
                return
            n = k // NG
            if n >= NBB:
                e_v.wait(eng, u, NG * (n - NBB) + NG - 1)
            else:
                e_v.wait(eng, u, NG * range(n, NS, NBB)[-1] + NG - 1, back=1)
            if n == 0:
                e_bw.wait(eng, u)
            e_bb[n % NBB].inc_by(eng.dma_start(
                bb[:, n % NBB, :], b_d[u.half, n:n + 1, :].to_broadcast([P, T])))

        def scan_pool(eng, u, k):
            n, g = k // NG, k % NG
            if n == 0:
                e_w.wait(eng, u, G3 * g + G3 - 1)
            if g == 0:
                e_bb[n % NBB].wait(eng, u, n // NBB)
            if k >= 2:
                e_scan.wait(eng, u, k - 2)
            else:
                e_scan.wait(eng, u, SLOTS - 2 + k, back=1)
            e_v.inc_by(eng.tensor_tensor(
                vv[:, k % 2, :, :], wu[:, u.half, G3 * g:G3 * g + G3, :],
                bb[:, n % NBB:n % NBB + 1, :].to_broadcast([P, G3, T]), ALU.mult))

        def scan_act(eng, u, k):
            n, g = k // NG, k % NG
            if n == 0:
                e_dt.wait(eng, u, G3 * g + G3 - 1)
            if k >= 2:
                e_scan.wait(eng, u, k - 2)
            else:
                e_scan.wait(eng, u, SLOTS - 2 + k, back=1)
            for i in range(G3):
                j = G3 * g + i
                ins = eng.activation(da[:, k % 2, i, :], dt[:, u.half, j, :], ACT.Exp,
                                     scale=a_neg[:, j, n:n + 1])
            e_da.inc_by(ins)

        def scan_dve(eng, u, k):
            n, g = k // NG, k % NG
            e_da.wait(eng, u, k)
            e_v.wait(eng, u, k)
            if k >= 2:
                e_ht.wait(eng, u, CH * (k - 2) + CH - 1)
                e_hl.wait(eng, u, k - 2)
            else:
                e_ht.wait(eng, u, CH * (SLOTS - 2 + k) + CH - 1, back=1)
                e_hl.wait(eng, u, SLOTS - 2 + k, back=1)
            for i in range(G3):
                j = G3 * g + i
                start = hl[:, n, j:j + 1] if u.half else 0.0
                ins = eng.tensor_tensor_scan(hh[:, k % 2, i, :], da[:, k % 2, i, :],
                                             vv[:, k % 2, i, :], start, ALU.mult, ALU.add)
            e_scan.inc_by(ins)

        def mac_dve(eng, u, k):
            n, g = k // NG, k % NG
            if k == 0:
                e_cc.wait(eng, u)
                e_yt.wait(eng, u, back=1)
            if k >= NG:
                e_mac.wait(eng, u, CH * (k - NG) + CH - 1)
            for c in range(CH):
                e_ht.wait(eng, u, CH * k + c)
                y = yy[:, c, G3 * P * g:G3 * P * (g + 1)]
                scale = ct[:, u.half, c, n:n + 1]
                if n == 0:
                    ins = eng.tensor_scalar(y, ht[c][:, 0:G3 * P], scale, None, ALU.mult)
                else:
                    ins = eng.scalar_tensor_tensor(out=y, in0=ht[c][:, 0:G3 * P], scalar=scale,
                                                   in1=y, op0=ALU.mult, op1=ALU.add)
                e_mac.inc_by(ins)

        def last_dve(eng, u, k):
            n, g = k // NG, k % NG
            e_scan.wait(eng, u, k)
            e_hl.inc_by(eng.tensor_copy(hl[:, n, G3 * g:G3 * g + G3], hh[:, k % 2, :, T - 1]))

        def scan_pe(eng, u, k):
            e_scan.wait(eng, u, k)
            for c in range(CH):
                if k >= 1:
                    e_mac.wait(eng, u, CH * (k - 1) + c)
                else:
                    e_mac.wait(eng, u, CH * (SLOTS - 1) + c, back=1)
                for i in range(G3):
                    ins = eng.transpose(ht[c][:, i * P:(i + 1) * P],
                                        hh[:, k % 2, i, c * P:(c + 1) * P], ident[:, :])
                e_ht.inc_by(ins)

        def exp_table(eng):
            eng.preload_act_table_set("natural_log_exp_and_others")

        def hid(u, m):
            if m < HH:
                return xc[:, u.half, m, :]
            return hr[:, m - HH, :] if m < HH + 3 else hx[:, m - HH - 3, :]

        def stream(q):
            h, r = q // 6, q % 6
            return a["w_m1"][3 * h + r] if r < 3 else a["w_m2"][2 * (r - 3) + h]

        def stream_sync(eng, u, q):
            h, r = (q - 3) // 6, (q - 3) % 6
            if q < 3:
                e_m2.wait(eng, u, KC + q, back=1)
            elif r < 3:
                e_m1.wait(eng, u, HH * h + 2 * r + 1)
            else:
                e_m2.wait(eng, u, KC * h + r - 3)
            e_ws[q % 3].inc_by(eng.dma_start(wring[:, q % 3, :], stream(q)))

        def stages_of(units):
            st = {}
            u, v = units.get("post"), units.get("pre")

            def y_stage(j):
                def pe(eng):
                    if j == 0:
                        e_mac.wait(eng, u)
                    bank_free(eng, units, "Y", j)
                    for c in range(CH):
                        ins = eng.transpose(bank("Y", j)[:, c * P:(c + 1) * P],
                                            yy[:, c, j * P:(j + 1) * P], ident[:, :])
                    e_yt.inc_by(ins)
                    yield 0.5

                def dve(eng):
                    e_yt.wait(eng, u, j)
                    e_yz.inc_by(eng.scalar_tensor_tensor(
                        out=xc[:, u.half, j, :], in0=xc[:, u.half, j, :],
                        scalar=d_sk[:, j:j + 1], in1=bank("Y", j)[:, :],
                        op0=ALU.mult, op1=ALU.add))
                st[("Y", j)] = (0.5, {"pe": (0, pe), "dve": (1, dve)})

            def z_stage(j):
                def pe(eng):
                    bank_free(eng, units, "Z", j)
                    for k in range(KC):
                        w = w_in[:, k, DI + j * P:DI + (j + 1) * P]
                        ins = eng.matmul(bank("Z", j)[:, :], w,
                                         xn[:, u.half, k, :], start=(k == 0), stop=(k == KC - 1))
                        if k == KC - 1:
                            e_zp.inc_by(ins)
                        yield 1

                def act(eng):
                    if j == 2:
                        last_pre(eng)
                    for q in range(j - 2, j + 1):
                        if q >= 3:
                            e_gt.wait(eng, u, q - 3)
                        e_zp.wait(eng, u, q)
                        e_sz.inc_by(eng.activation(hr[:, q % 3, :], bank("Z", q)[:, :], ACT.Silu,
                                                   bias=b_in[:, KD + q:KD + q + 1]))
                    exp_table(eng)

                def dve(eng):
                    for q in range(j - 2, j + 1):
                        e_sz.wait(eng, u, q)
                        e_yz.wait(eng, u, q)
                        e_gt.inc_by(eng.tensor_tensor(xc[:, u.half, q, :], xc[:, u.half, q, :],
                                                      hr[:, q % 3, :], ALU.mult))
                        yield
                st[("Z", j)] = (3, {"pe": (0, pe)}
                                | ({"act": (SILU_Z_LAG, act), "dve": (GATE_LAG, dve)}
                                   if j % 3 == 2 else {}))

            def last_pre(eng):
                if not (u.static and u.n >= NU - 1):
                    e_dt.wait(eng, u, back=-1)

            def o_stage(m):
                def pe(eng):
                    bank_free(eng, units, "O", m)
                    for k in range(KD):
                        if m == 0:
                            e_gt.wait(eng, u, k)
                        ins = eng.matmul(bank("O", m)[:, :], w_out[:, k, m * P:(m + 1) * P],
                                         xc[:, u.half, k, :], start=(k == 0), stop=(k == KD - 1))
                        if k == KD - 1:
                            e_op.inc_by(ins)
                        yield 1

                def act(eng):
                    if m == 0:
                        e_m1.wait(eng, u, back=1)
                    e_op.wait(eng, u, m)
                    e_t.inc_by(eng.activation(tt[:, m, :], bank("O", m)[:, :], ACT.Copy))
                st[("O", m)] = (6, {"pe": (0, pe), "act": (1, act)})

            def m1_stage(m):
                q = m // 2 + (3 if m >= HH else 0)

                def pe(eng):
                    bank_free(eng, units, "M1", m)
                    if m == 0:
                        e_t.wait(eng, u)
                    if m % 2 == 0:
                        e_ws[q % 3].wait(eng, u, q // 3)
                    w = wring[:, q % 3, :].rearrange("p (m k c) -> p m k c", m=2, k=KC)
                    for k in range(KC):
                        ins = eng.matmul(bank("M1", m)[:, :], w[:, m % 2, k, :], tt[:, k, :],
                                         start=(k == 0), stop=(k == KC - 1))
                        if k == KC - 1:
                            e_m1.inc_by(ins)
                        yield 1

                def act(eng):
                    if m == HH + 2 and v:
                        e_var.wait(eng, v)
                    if m == KH - 1:
                        e_m2.wait(eng, u, back=1)
                        if v:
                            e_xh.wait(eng, v)
                    for i in range(m - 2, m + 1):
                        e_m1.wait(eng, u, i)
                        e_ge.inc_by(eng.activation(hid(u, i), bank("M1", i)[:, :], ACT.Gelu,
                                                   bias=b1[:, i:i + 1]))
                    exp_table(eng)
                st[("M1", m)] = (3, {"pe": (0, pe)} | ({"act": (1, act)} if m % 3 == 2 else {}))

            def m2_stage(i):
                h, m = i // KC, i % KC
                q = 3 + 6 * h + m

                def pe(eng):
                    bank_free(eng, units, "M2", i)
                    e_ws[q % 3].wait(eng, u, q // 3)
                    w = wring[:, q % 3, :].rearrange("p (k c) -> p k c", k=HH)
                    for k in range(HH):
                        if m == 0:
                            e_ge.wait(eng, u, HH * h + k)
                        ins = eng.matmul(bank("M2", i)[:, :], w[:, k, :], hid(u, HH * h + k),
                                         start=(k == 0), stop=(k == HH - 1))
                        if k == HH - 1:
                            e_m2.inc_by(ins)
                        yield 1

                def dve(eng):
                    if i == 0:
                        e_xr.wait(eng, u)
                    e_m2.wait(eng, u, i)
                    if h == 0:
                        e_x1.inc_by(eng.scalar_tensor_tensor(
                            out=xr[:, m, :], in0=bank("M2", i)[:, :], scalar=b2[:, m:m + 1],
                            in1=xr[:, m, :], op0=ALU.add, op1=ALU.add))
                        return
                    e_x1.wait(eng, u, m)
                    e_x1.inc_by(eng.tensor_tensor(xr[:, m, :], xr[:, m, :], bank("M2", i)[:, :],
                                                  ALU.add))
                    yield
                    e_x1.wait(eng, u, i)
                    e_bn.inc_by(eng.bn_stats(
                        st1[:, u.ds(), u.half, m, :].rearrange("p o s -> p (o s)"), xr[:, m, :]))
                st[("M2", i)] = (HH, {"pe": (0, pe), "dve": (X1_LAG, dve)})

            def load_x():
                def sync(eng):
                    e_zp.wait(eng, v, back=2)
                    e_xin.inc_by(eng.dma_start(xn[:, v.half, :, :], x_half(x_d, v)))

                def dve(eng):
                    e_xin.wait(eng, v)
                    for k in range(KC):
                        s = [gn0[:, k, v.ds(), i] for i in range(2)]
                        e_gn.inc_by(eng.tensor_scalar(
                            xn[:, v.half, k, :], xn[:, v.half, k, :], s[0], s[1],
                            ALU.subtract, ALU.mult))
                        yield
                return sync, dve

            def mu_stage():
                def pe(eng):
                    bank_free(eng, units, "MU", 0)
                    e_gn.wait(eng, v)
                    for k in range(KC):
                        ins = eng.matmul(bank("MU", 0)[:, :], mean_w, xn[:, v.half, k, :],
                                         start=(k == 0), stop=(k == KC - 1))
                    e_mu.inc_by(ins)
                    yield 3

                def dve(eng):
                    e_mu.wait(eng, v)
                    for k in range(KC):
                        e_ce.inc_by(eng.tensor_tensor(xn[:, v.half, k, :], xn[:, v.half, k, :],
                                                      bank("MU", 0)[:, :], ALU.subtract))
                        yield

                def act(eng):
                    e_gt.wait(eng, v, back=2)
                    for k in range(KC):
                        e_ce.wait(eng, v, k)
                        e_sq.inc_by(eng.activation(hr[:, k, :], xn[:, v.half, k, :], ACT.Square))
                st[("MU", 0)] = (3, {"pe": (0, pe), "dve": (1, dve), "act": (1, act)})

            def var_stage():
                def pe(eng):
                    bank_free(eng, units, "VAR", 0)
                    for k in range(KC):
                        e_sq.wait(eng, v, k)
                        ins = eng.matmul(bank("VAR", 0)[:, :], mean_w, hr[:, k, :],
                                         start=(k == 0), stop=(k == KC - 1))
                    e_var.inc_by(ins)
                    yield 3

                def act(eng):
                    e_xh.wait(eng, v, back=1)
                    e_m2.wait(eng, v, back=3)
                    e_var.wait(eng, v)
                    e_rs.inc_by(eng.activation(rstd, bank("VAR", 0)[:, :], ACT.Ln,
                                               bias=eps[:, 0:1]))
                    e_rs.wait(eng, v, 0)
                    e_rs.inc_by(eng.activation(rstd, rstd, ACT.Exp, scale=-0.5))

                def dve(eng):
                    e_rs.wait(eng, v)
                    for k in range(KC):
                        e_xh.inc_by(eng.tensor_tensor(xn[:, v.half, k, :], xn[:, v.half, k, :],
                                                      rstd, ALU.mult))
                        yield
                st[("VAR", 0)] = (3, {"pe": (0, pe), "act": (1, act), "dve": (XHAT_LAG, dve)})

            def xm_stage(j):
                q = j // 3

                def pe(eng):
                    bank_free(eng, units, "XM", j)
                    e_xh.wait(eng, v)
                    for k in range(KC):
                        ins = eng.matmul(bank("XM", j)[:, :], w_in[:, k, j * P:(j + 1) * P],
                                         xn[:, v.half, k, :], start=(k == 0), stop=(k == KC - 1))
                        if k == KC - 1:
                            e_xm.inc_by(ins)
                        yield 1

                def place_free(eng):
                    if q:
                        e_hs.wait(eng, v, j - 3)
                        e_cv.wait(eng, v, 3 * (j - 3) + 2)
                    else:
                        e_dt.wait(eng, v, back=1)
                        e_m1.wait(eng, v, back=2)

                def act(eng):
                    place_free(eng)
                    e_xm.wait(eng, v, j)
                    e_xe.inc_by(eng.activation(xm[:, j % 3, 2:T + 2], bank("XM", j)[:, :],
                                               ACT.Identity, bias=b_in[:, j:j + 1]))

                def dve(eng):
                    tile = xm[:, j % 3, :]
                    place_free(eng)
                    if v.half:
                        e_hs.wait(eng, v, j, back=1)
                        ins = eng.tensor_copy(tile[:, 0:2], halo[:, j, :])
                    else:
                        ins = eng.memset(tile[:, 0:2], 0.0)
                    e_hi.inc_by(ins)
                    e_xe.wait(eng, v, j)
                    e_hi.wait(eng, v, j)
                    e_hs.inc_by(eng.tensor_copy(halo[:, j, :], tile[:, T:T + 2]))
                    if j == 0:
                        e_m2.wait(eng, v, KC - 1, back=2)
                    y = xc[:, v.half, j, :]
                    for tap in range(3):
                        src, w = tile[:, 2 - tap:T + 2 - tap], conv_w[:, j, 2 - tap:3 - tap]
                        if tap == 0:
                            ins = eng.tensor_scalar(y, src, w, None, ALU.mult)
                        else:
                            e_cv.wait(eng, v, 3 * j + tap - 1)
                            ins = eng.scalar_tensor_tensor(out=y, in0=src, scalar=w, in1=y,
                                                           op0=ALU.mult, op1=ALU.add)
                        e_cv.inc_by(ins)
                        yield

                def silu(eng):
                    for i in range(3 * q, 3 * q + 3):
                        e_cv.wait(eng, v, 3 * i + 2)
                        y = xc[:, v.half, i, :]
                        e_xc.inc_by(eng.activation(y, y, ACT.Silu, bias=conv_b[:, i:i + 1]))
                    exp_table(eng)
                st[("XM", j)] = (3, {"pe": (0, pe), "act": (XM_COPY_LAG, act),
                                      "dve": (CONV_LAG, dve)}
                                 | ({"act2": (SILU_LAG, silu)} if j % 3 == 2 else {}))

            def xp_stage():
                def pe(eng):
                    bank_free(eng, units, "XP", 0)
                    for k in range(KD):
                        e_xc.wait(eng, v, k)
                        ins = eng.matmul(bank("XP", 0)[0:NX, :], w_xp[:, k, :],
                                         xc[:, v.half, k, :], start=(k == 0), stop=(k == KD - 1))
                        if k == KD - 1:
                            e_xp.inc_by(ins)
                        yield 1

                def act(eng):
                    e_bw.wait(eng, v, back=1)
                    e_dp.wait(eng, v, back=1)
                    e_ct.wait(eng, v, back=1)
                    e_xp.wait(eng, v)
                    e_db.inc_by(eng.activation(dbc[0:NX, :], bank("XP", 0)[0:NX, :], ACT.Copy))

                def sync(eng):
                    e_db.wait(eng, v)
                    e_bw.inc_by(eng.dma_start(b_d[v.half, :, :], dbc[RANK:RANK + NS, :]))
                st[("XP", 0)] = (6, {"pe": (0, pe), "act": (0, act), "sync": (1, sync)})

            def ct_stage():
                def pe(eng):
                    e_db.wait(eng, v)
                    bank_free(eng, units, "CT", 0)
                    for c in range(CH):
                        ins = eng.transpose(bank("CT", 0)[:, c * P:(c + 1) * P],
                                            dbc[:, c * P:(c + 1) * P], ident[:, :])
                    e_ct.inc_by(ins)
                    yield 0.5

                def dve(eng):
                    e_ct.wait(eng, v)
                    c_t = bank("CT", 0)[:, :].rearrange("p (c r) -> p c r", c=CH)
                    e_cc.inc_by(eng.tensor_copy(ct[:, v.half, :, :], c_t[:, :, RANK + NS:NX]))
                st[("CT", 0)] = (0.5, {"pe": (0, pe), "dve": (1, dve)})

            def dt_stage(j):
                def pe(eng):
                    bank_free(eng, units, "DT", j)
                    e_dp.inc_by(eng.matmul(bank("DT", j)[:, :], w_dt[:, j * P:(j + 1) * P],
                                           dbc[:, :], start=True, stop=True))
                    yield 1

                sa, sb_ = dt[:, v.half, j, :], tt[:, j % 3, :]

                def act(eng):
                    if j == 0:
                        e_da.wait(eng, v, back=2)
                        e_w.wait(eng, v, back=2)
                    if j < 3:
                        e_cv.wait(eng, v)
                        e_hs.wait(eng, v)
                    else:
                        e_dt.wait(eng, v, j - 3)
                    e_dp.wait(eng, v, j)
                    ps = bank("DT", j)[:, :]
                    e_sp.inc_by(eng.activation(sb_, ps, ACT.Abs, bias=dt_b[:, j:j + 1]))
                    e_sp.inc_by(eng.activation(sa, ps, ACT.Identity, bias=dt_b[:, j:j + 1]))
                    e_sp.wait(eng, v, 4 * j)
                    e_sp.inc_by(eng.activation(sb_, sb_, ACT.Exp, scale=-1.0))
                    e_sp.wait(eng, v, 4 * j + 2)
                    e_sp.inc_by(eng.activation(sb_, sb_, ACT.Ln, bias=1.0))

                def dve(eng):
                    if j == 0:
                        e_v.wait(eng, v, back=2)
                    e_sp.wait(eng, v, 4 * j + 3)
                    e_dt.inc_by(eng.scalar_tensor_tensor(
                        out=sa, in0=sa, scalar=0.0, in1=sb_,
                        op0=ALU.max, op1=ALU.add))
                    yield
                    e_dt.wait(eng, v, j)
                    e_w.inc_by(eng.tensor_tensor(wu[:, v.half, j, :], dt[:, v.half, j, :],
                                                 xc[:, v.half, j, :], ALU.mult))
                st[("DT", j)] = (1, {"pe": (0, pe), "act": (SOFTPLUS_LAG, act),
                                     "dve": (DT_LAG, dve)})

            def load_xr(eng):
                e_st.wait(eng, u, back=1)
                e_bn.wait(eng, u, back=1)
                e_xr.inc_by(eng.dma_start(xr[:, :, :], x_half(x_d, u)))

            def store_x1(eng):
                e_x1.wait(eng, u)
                e_st.inc_by(eng.dma_start(x_half(x1_d, u), xr[:, :, :]))

            loads = {}
            if u:
                for j in range(KD):
                    y_stage(j)
                    z_stage(j)
                for m in range(KC):
                    o_stage(m)
                for m in range(KH):
                    m1_stage(m)
                for i in range(2 * KC):
                    m2_stage(i)
                loads[("Y", 0)] = [load_xr] + [lambda eng, q=q: stream_sync(eng, u, q)
                                               for q in range(3)]
                for q in range(3, 12):
                    h, r = (q - 3) // 6, (q - 3) % 6
                    at = ("M1", HH * h + 2 * r + 1) if r < 3 else ("M2", KC * h + r - 3)
                    loads[at] = [lambda eng, q=q: stream_sync(eng, u, q)]
                loads[("M2", 2 * KC - 1)] = [store_x1]
            if v:
                sync, gn = load_x()
                mu_stage()
                var_stage()
                for j in range(KD):
                    xm_stage(j)
                xp_stage()
                ct_stage()
                for j in range(KD):
                    dt_stage(j)
                before = ("O", 0) if u else ("MU", 0)
                loads.setdefault(before, []).append(sync)
                st[before][1]["dve0"] = (0 if u else -1, gn)
            return st, loads

        def parts_of(f, eng):
            parts = f(eng)
            if parts is not None:
                yield from parts
            else:
                yield

        def x_half(d, u):
            s = slice(u.half * T, (u.half + 1) * T)
            if u.static:
                return d[u.b, :, :, s]
            return d[u.ds(), :, :, s].rearrange("o p k l -> (o p) k l")

        def step(eng, name, scan=None, posts=None, pres=None):
            units = {k: x for k, x in (("post", posts), ("pre", pres)) if x}
            st, loads = stages_of(units)
            total = sum(s[0] for s in st.values())
            per = total / DENSE_SLOTS
            end = SLOTS + 6
            at = [[] for _ in range(end)]
            pe_parts, done, latest = [], 0.0, 0
            for _, sname, i, _ in order:
                if (sname, i) not in st:
                    continue
                work, parts = st[(sname, i)]
                done += work
                slot = min(int((done - 1e-6) / per), SLOTS - 1)
                if name == "pe":
                    pe_parts.append(parts["pe"][1])
                for e, (lag, f) in sorted(parts.items(), key=lambda x: x[0][-1] != "0"):
                    if e.rstrip("02") == name and e != "pe":
                        latest = max(slot + lag, latest)
                        at[latest].append(f)
                if name == "sync":
                    for f in loads.get((sname, i), []):
                        at[slot].append(f)
            if name == "pe":
                def run():
                    for f in pe_parts:
                        yield from f(eng)
                work_left, spent = run(), 0.0
            queue = []
            for k in range(end):
                if scan and k < SLOTS:
                    if name == "sync":
                        if k == 0:
                            for q in range(0, 2 * NG, NG):
                                scan_sync(eng, scan, q)
                        if k + 2 * NG < SLOTS and k % NG == 0:
                            scan_sync(eng, scan, k + 2 * NG)
                    if name == "pool":
                        scan_pool(eng, scan, k)
                    if name == "act":
                        if k == 0:
                            scan_act(eng, scan, k)
                        if k + 1 < SLOTS:
                            scan_act(eng, scan, k + 1)
                    if name == "dve":
                        scan_dve(eng, scan, k)
                    if name == "pe":
                        scan_pe(eng, scan, k)
                for f in at[k]:
                    if name == "dve":
                        queue.append(parts_of(f, eng))
                    else:
                        f(eng)
                given = 0
                while queue and (given < DVE_QUOTA or not scan or k >= SLOTS - 1):
                    if next(queue[0], StopIteration) is StopIteration:
                        queue.pop(0)
                    else:
                        given += 1
                if name == "pe":
                    while spent < (k + 1) * per or k == end - 1:
                        w = next(work_left, None)
                        if w is None:
                            break
                        spent += w
                if scan and name == "dve" and k < SLOTS:
                    if k >= 1:
                        mac_dve(eng, scan, k - 1)
                    last_dve(eng, scan, k)
                    if k == SLOTS - 1:
                        mac_dve(eng, scan, k)

        def program(eng, name):
            if name == "act":
                exp_table(eng)
            step(eng, name, pres=Unit(0, 0))
            step(eng, name, scan=Unit(0, 0), pres=Unit(0, 1))
            with eng.Fori(0, NB - 1) as i:
                step(eng, name, scan=Unit(i, 1), posts=Unit(i, 0), pres=Unit(i + 1, 0))
                step(eng, name, scan=Unit(i + 1, 0), posts=Unit(i, 1), pres=Unit(i + 1, 1))
            step(eng, name, scan=Unit(NB - 1, 1), posts=Unit(NB - 1, 0))
            step(eng, name, posts=Unit(NB - 1, 1))

        s_const = sem("layer1_constants")
        with nc.Block() as block:
            @block.sync
            def _(eng):
                for event in (e_m1, e_m2, e_bn, e_st, e_yz, e_sz, e_t, e_ge, e_x1):
                    event.prime(eng)
                program(eng, "sync")
                e_st.wait(eng, Unit(NB - 1, 1))

            @block.gpsimd
            def _(eng):
                program(eng, "pool")
                last = Unit(NB - 1, 1)
                e_v.wait(eng, last)
                e_scan.wait(eng, last)
                for tile, src in consts.loads:
                    eng.dma_start(tile, src).then_inc(s_const, 16)
                eng.wait_ge(s_const, 16 * len(consts.loads))

            @block.scalar
            def _(eng):
                program(eng, "act")

            @block.vector
            def _(eng):
                program(eng, "dve")

            @block.tensor
            def _(eng):
                program(eng, "pe")


def layer1(nc, a, sem, psum, ident, st1, eps, x1_d, w_d, out_d, consts, dt, wu):
    with ExitStack() as ctx:
        def sb(name, shape, dtype=F32):
            return ctx.enter_context(nc.sbuf_tensor(name, shape, dtype))

        w_raw = [consts.w1, consts.w2]
        w_hi = [sb(f"we{i}_hi", [P, E, KC, C], F32R) for i in range(2)]
        w_lo = [sb(f"we{i}_lo", [P, E, KC, C], F32R) for i in range(2)]
        xg_hi = sb("xg_hi", [P, 2, KC, T], F32R)
        xg_lo = sb("xg_lo", [P, 2, KC, T], F32R)
        hb_hi = sb("hb_hi", [P, 2, KC, T], F32R)
        hb_lo = sb("hb_lo", [P, 2, KC, T], F32R)
        xb = sb("xb", [P, 2, KC, T])
        gn1 = sb("gn1", [P, KC, NB, 2])

        flat_dt = dt[:, :, :, :].rearrange("p a j t -> p (a j t)")
        flat_wu = wu[:, :, :, :].rearrange("p a j t -> p (a j t)")
        half, nw = 2 * KC * T, E * KC * C
        xg = flat_dt[:, 0:half].rearrange("p (h k t) -> p h k t", h=2, k=KC)
        hb = flat_dt[:, half:2 * half].rearrange("p (h k t) -> p h k t", h=2, k=KC)
        cf = flat_wu[:, 0:E * T].rearrange("p (e t) -> p e t", e=E)
        wb = flat_wu[:, E * T:(E + 2 * KTOP) * T].rearrange(
            "p (h k t) -> p h k t", h=2, k=KTOP)
        behind = [f[:, nw:nw + KC * T].rearrange("p (k t) -> p k t", k=KC)
                  for f in (flat_dt, flat_wu)]
        EP = 32
        spare = Spare(consts)
        mv = spare.take(KC * NB * 2).rearrange("p (k b s) -> p k b s", k=KC, b=NB)
        tmp = spare.take(KC * NB).rearrange("p (k b) -> p k b", k=KC)
        gs = spare.take(KC * NB * EP).rearrange("p (k b e) -> p k b e", k=KC, b=NB)
        glt = spare.take(2 * P).rearrange("p (h c) -> p h c", h=2)
        gsb = sb("gsb", [P, 2, KC, EP])
        gm = sb("gm", [P, KC, NB, E])
        NT = NB * L // P
        lg = sb("lg", [P, NT, E])
        off = sb("off", [P, NB, E])
        mx = sb("mx", [P, NT])
        sm = sb("sm", [P, NT])
        ge = sb("ge", [P, 6, NT])
        rk = sb("rk", [P, NT, E])
        top = sb("top", [P, KTOP, NT, E])
        pf = sb("pf", [P, KTOP, E])
        pres = sb("pres", [P, KTOP, E])
        b2t = sb("b2t", [P, KTOP, KC, E])
        b2k = sb("b2k", [P, KTOP, KC])
        tw = sb("tw", [P, KTOP, NT])
        twt = sb("twt", [P, P])

        s_x = [sem(f"gate_x{i}") for i in range(4)]
        s_pe, s_act, s_tw, s_split = sem("b3_pe"), sem("b3_act"), sem("b3_tw"), sem("b3_split")
        ahead = 4
        s_gsb, s_gm, s_gc, s_gt, s_lg = (
            sem("gate_weights"), sem("gate_mm"), sem("gate_copied"), sem("gate_T"),
            sem("gate_logits"))
        dv = Chain(sem("b3_dve"))
        pairs = [(i, j) for i in range(E) for j in range(i + 1, E)]
        places = [xb[:, 0, :, :], xb[:, 1, :, :], *behind]
        offp = psum[2][:, 0:NB * E].rearrange("p (b e) -> p b e", b=NB)
        glp, gtp = psum[4:6], psum[6:8]
        with nc.Block() as block:
            @block.vector
            def _(eng):
                dv.add(eng.memset(gs, 0.0))
                for k in range(KC):
                    for b in range(NB):
                        dv.add(eng.bn_aggr(mv[:, k, b, :], st1[:, b, :, k, :]), "gn1 mv")
                group_stats(eng, None, None, dv, (s_act, 0), (s_pe, 0), mv, consts.group, psum[0],
                            tmp, gn1, eps, "gn1")
                dv.own(eng)
                for k in range(KC):
                    dv.add(eng.tensor_tensor(
                        gs[:, k, :, 0:E], consts.gate_w[:, k:k + 1, :].to_broadcast([P, NB, E]),
                        gn1[:, k, :, 1:2].to_broadcast([P, NB, E]), ALU.mult), "gs")
                dv.own(eng)
                for k in range(KC):
                    dv.add(eng.tensor_tensor(gm[:, k, :, :], gs[:, k, :, 0:E],
                                             gn1[:, k, :, 0:1].to_broadcast([P, NB, E]),
                                             ALU.mult), "gm")
                eng.wait_ge(s_pe, 3)
                dv.add(eng.tensor_tensor(off[:, :, :],
                                         consts.gate_b[:, None, :].to_broadcast([P, NB, E]),
                                         offp, ALU.subtract))
                dv.own(eng)
                with eng.Fori(0, NU // 4) as p:
                    for j in range(2):
                        eng.wait_ge(s_gm, p * 4 + (2 * j - 2 + ahead))
                        eng.tensor_copy(gsb[:, j, :, :], gs[:, :, bass.ds(p * 2 + j, 1), :]
                                        .rearrange("p k o e -> p (k o) e")).then_inc(s_gsb, 1)
                    for i in range(4):
                        h, j = i % HALVES, i // HALVES
                        eng.wait_ge(s_gt, p * 4 + (i + 1 + ahead))
                        src = gtp[h][:, 0:P].rearrange("p (c e) -> p c e", c=CH)[:, :, 0:E]
                        eng.tensor_tensor(
                            lg[:, bass.ds(p * (4 * CH) + i * CH, CH), :], src,
                            off[:, bass.ds(p * 2 + j, 1), :].to_broadcast([P, CH, E]),
                            ALU.add).then_inc(s_lg, 1)
                eng.wait_ge(s_lg, NU + ahead)
                dv.add(eng.tensor_reduce(mx[:, :], lg[:, :, :], AX.X, ALU.max))
                dv.own(eng)
                dv.add(eng.tensor_tensor(lg[:, :, :], lg[:, :, :],
                                         mx[:, :, None].to_broadcast([P, NT, E]), ALU.subtract),
                       "shifted")
                eng.wait_ge(s_act, 2)
                dv.add(eng.tensor_reduce(sm[:, :], lg[:, :, :], AX.X, ALU.add))
                dv.own(eng)
                dv.add(eng.reciprocal(sm[:, :], sm[:, :]))
                dv.own(eng)
                dv.add(eng.tensor_tensor(lg[:, :, :], lg[:, :, :],
                                         sm[:, :, None].to_broadcast([P, NT, E]), ALU.mult))
                dv.own(eng)
                for q, (i, j) in enumerate(pairs):
                    dv.add(eng.tensor_tensor(ge[:, q, :], lg[:, :, i], lg[:, :, j], ALU.is_ge))
                for i in range(E):
                    dv.add(eng.memset(rk[:, :, i], float(E - 1 - i)))
                dv.own(eng)
                for q, (i, j) in enumerate(pairs):
                    dv.add(eng.tensor_tensor(rk[:, :, i], rk[:, :, i], ge[:, q, :], ALU.subtract))
                    dv.own(eng)
                    dv.add(eng.tensor_tensor(rk[:, :, j], rk[:, :, j], ge[:, q, :], ALU.add))
                    dv.own(eng)
                for k in range(KTOP):
                    dv.add(eng.tensor_scalar(top[:, k, :, :], rk[:, :, :], float(k), None,
                                             ALU.is_equal))
                dv.own(eng)
                for k in range(KTOP):
                    dv.add(eng.tensor_reduce(pf[:, k, :], top[:, k, :, :].rearrange(
                        "p t e -> p e t"), AX.X, ALU.max), "chosen")
                dv.own(eng)
                for k in range(KTOP):
                    dv.add(eng.tensor_tensor(top[:, k, :, :], top[:, k, :, :], lg[:, :, :],
                                             ALU.mult))
                dv.own(eng)
                for k in range(KTOP):
                    dv.add(eng.tensor_reduce(tw[:, k, :], top[:, k, :, :], AX.X, ALU.add))
                dv.own(eng)
                dv.add(eng.tensor_tensor(tw[:, 1, :], tw[:, 1, :], tw[:, 0, :], ALU.subtract),
                       "second - first")
                eng.wait_ge(s_act, 3)
                dv.add(eng.tensor_scalar(tw[:, 0, :], tw[:, 1, :], 1.0, None, ALU.add))
                dv.own(eng)
                dv.add(eng.reciprocal(tw[:, 0, :], tw[:, 0, :]))
                dv.own(eng)
                dv.add(eng.tensor_tensor(tw[:, 1, :], tw[:, 1, :], tw[:, 0, :], ALU.mult),
                       "weights")
                eng.wait_ge(s_pe, 5)
                dv.add(eng.tensor_copy(twt[:, :], psum[1][:, 0:P]), "twt")
                eng.wait_ge(s_pe, 4)
                dv.add(eng.tensor_scalar(
                    pres[:, :, :], psum[3][:, 0:KTOP * E].rearrange("p (k e) -> p k e", k=KTOP),
                    0.0, None, ALU.is_gt))
                dv.own(eng)
                for k in range(KTOP):
                    dv.add(eng.tensor_tensor(b2t[:, k, :, :], consts.b2,
                                             pres[:, k:k + 1, :].to_broadcast([P, KC, E]),
                                             ALU.mult))
                dv.own(eng)
                for k in range(KTOP):
                    dv.add(eng.tensor_reduce(b2k[:, k, :], b2t[:, k, :, :], AX.X, ALU.add))

            marks = {k: (dv.sem, v) for k, v in dv.at.items()}

            @block.sync
            def _(eng):
                for s in (s_gm, s_gc, s_gt, s_lg):
                    eng.sem_inc(s, ahead)
                with eng.Fori(0, NU // 4) as p:
                    for i in range(4):
                        eng.wait_ge(s_gm, p * 4 + (i + 1))
                        h = i % HALVES
                        eng.dma_start(places[i], x1_d[bass.ds(p * 2 + i // HALVES, 1), :, :,
                                                      h * T:(h + 1) * T].rearrange(
                                          "o p k l -> (o p) k l")).then_inc(s_x[i], 16)
                eng.wait_ge(*marks["twt"])
                eng.dma_start(w_d.rearrange("k b (c l) -> (k b c) l", l=P), twt[:, :])\
                   .then_inc(s_tw, 16)
                eng.wait_ge(s_tw, 16)

            @block.gpsimd
            def _(eng):
                for i in range(2):
                    for e in range(E):
                        eng.wait_ge(s_split, E * i + e + 1)
                        eng.tensor_tensor(w_lo[i][:, e, :, :], w_raw[i][:, e, :, :],
                                          w_hi[i][:, e, :, :].bitcast(F32), ALU.subtract)

            @block.scalar
            def _(eng):
                for i in range(2):
                    for e in range(E):
                        eng.activation(w_hi[i][:, e, :, :], w_raw[i][:, e, :, :],
                                       ACT.Copy).then_inc(s_split, 1)
                group_stats(None, eng, None, marks, (s_act, 0), (s_pe, 0), mv, consts.group,
                            psum[0], tmp, gn1, eps, "gn1")
                with eng.Fori(0, NB) as b:
                    for h in range(HALVES):
                        n1 = b * HALVES + (h + 1)
                        eng.wait_ge(s_gt, n1 + (ahead - 2))
                        eng.wait_ge(s_gm, n1 + ahead)
                        eng.activation(glt[:, h, :], glp[h][:, 0:P], ACT.Copy).then_inc(s_gc, 1)
                eng.wait_ge(*marks["shifted"])
                eng.activation(lg[:, :, :], lg[:, :, :], ACT.Exp).then_inc(s_act, 1)
                eng.wait_ge(*marks["second - first"])
                eng.activation(tw[:, 1, :], tw[:, 1, :], ACT.Exp).then_inc(s_act, 1)

            @block.tensor
            def _(eng):
                group_stats(None, None, eng, marks, None, (s_pe, 0), mv, consts.group, psum[0],
                            tmp, gn1, eps, "gn1")
                eng.wait_ge(*marks["gm"])
                for k in range(KC):
                    mm = eng.matmul(psum[2][:, 0:NB * E], consts.ones, gm[:, k, :, :].rearrange(
                        "p b e -> p (b e)"), start=(k == 0), stop=(k == KC - 1))
                mm.then_inc(s_pe, 1)
                with eng.Fori(0, NU // 4) as p:
                    for i in range(4):
                        h = i % HALVES
                        n1 = p * 4 + (i + 1)
                        eng.wait_ge(s_x[i], p * 16 + 16)
                        eng.wait_ge(s_gsb, p * 2 + (i // HALVES + 1))
                        eng.wait_ge(s_gc, n1 + (ahead - 2))
                        for k in range(KC):
                            for c in range(CH):
                                mm = eng.matmul(
                                    glp[h][EP * c:EP * (c + 1), 0:P],
                                    gsb[:, i // HALVES, k, :],
                                    places[i][:, k, c * P:(c + 1) * P],
                                    start=(k == 0), stop=(k == KC - 1))
                        mm.then_inc(s_gm, 1)
                        eng.wait_ge(s_gc, n1 + ahead)
                        eng.wait_ge(s_lg, n1 + (ahead - 2))
                        eng.transpose(gtp[h][:, 0:P], glt[:, h, :], ident[:, :])\
                           .then_inc(s_gt, 1)
                eng.wait_ge(*marks["chosen"])
                eng.matmul(psum[3][:, 0:KTOP * E], consts.ones, pf[:, :, :].rearrange(
                    "p k e -> p (k e)"), start=True, stop=True).then_inc(s_pe, 1)
                eng.wait_ge(*marks["weights"])
                eng.transpose(psum[1][:, 0:P], tw[:, :, :].rearrange("p k t -> p (k t)"),
                              ident[:, :]).then_inc(s_pe, 1)

        def ev(name, per_unit, step=1):
            return Event(sem(name), per_unit, step)
        e_lx = [ev(f"x1_load{h}", 1, 16) for h in range(2)]
        e_lw = [ev(f"tw_load{h}", 1, 16) for h in range(2)]
        e_so = [ev(f"out_store{h}", 1, 16) for h in range(2)]
        e_ng, e_nh, e_nl = ev("normed", KC), ev("normed_hi", KC), ev("normed_lo", KC)
        e_cb, e_cf, e_xs = ev("coef_first", E), ev("coef", E), ev("x_bias", 2 * KC)
        e_w1, e_rl, e_hc = ev("w1_mm", E * KC), ev("relu", E * KC), ev("h_coef", E * KC)
        e_hh, e_hl = ev("h_hi", E * KC), ev("h_lo", E * KC)
        e_w2, e_o = ev("w2_mm", E), ev("result", KC)
        hbank, acc = psum[0:4], psum[4:4 + KC]

        def wait_image(event, eng, b, back=0):
            eng.wait_ge(event.sem, b * 16 + (16 - 16 * back))

        def product(eng, bank, which, e, k, m, hi, lo, start, stop):
            w = [t[which][:, e, k, m * P:(m + 1) * P] for t in (w_hi, w_lo)]
            eng.matmul(bank, w[0], hi, start=start, stop=False)
            eng.matmul(bank, w[0], lo, start=False, stop=False)
            return eng.matmul(bank, w[1], hi, start=False, stop=stop)

        def normalise(eng, name, b, h):
            u = Unit(b, h)
            if name == "dve":
                wait_image(e_lx[h], eng, b)
                e_w1.wait(eng, u, back=2)
                for k in range(KC):
                    s = [gn1[:, k, bass.ds(b, 1), i] for i in range(2)]
                    e_ng.inc_by(eng.tensor_scalar(xg[:, h, k, :], xb[:, h, k, :], s[0], s[1],
                                                  ALU.subtract, ALU.mult))
                for k in range(KC):
                    e_nh.wait(eng, u, k)
                    e_nl.inc_by(eng.tensor_tensor(xg_lo[:, h, k, :], xg[:, h, k, :],
                                                  xg_hi[:, h, k, :].bitcast(F32), ALU.subtract))
            if name == "act":
                e_w1.wait(eng, u, back=2)
                for k in range(KC):
                    e_ng.wait(eng, u, k)
                    e_nh.inc_by(eng.activation(xg_hi[:, h, k, :], xg[:, h, k, :], ACT.Copy))

        def body(eng, name, b, first=False, last=False):
            for h in range(HALVES):
                u = Unit(b, h)
                following = (b, 1) if h == 0 else (b + 1, 0)
                if last and h:
                    following = None
                if name == "sync":
                    if not first:
                        wait_image(e_so[h], eng, b, back=1)
                    src = slice(h * T, (h + 1) * T)
                    e_lx[h].inc_by(eng.dma_start(xb[:, h, :, :], x1_d[bass.ds(b, 1), :, :, src]
                                                 .rearrange("o p k l -> (o p) k l")))
                    for k in range(KTOP):
                        eng.dma_start(wb[:, h, k, :], w_d[k, bass.ds(b, 1), src].to_broadcast(
                            [P, T])).then_inc(e_lw[h].sem, 16)
                if name == "pe":
                    for e in range(E + 1):
                        if e < E:
                            for m in range(KC):
                                q = KC * e + m
                                if q >= len(hbank):
                                    e_rl.wait(eng, u, q - len(hbank))
                                else:
                                    e_rl.wait(eng, u, E * KC + q - len(hbank), back=1)
                                for k in range(KC):
                                    if q == 0:
                                        e_nl.wait(eng, u, k)
                                    mm = product(eng, hbank[q % 4][:, :], 0, e, k, m,
                                                 xg_hi[:, h, k, :], xg_lo[:, h, k, :],
                                                 k == 0, k == KC - 1)
                                e_w1.inc_by(mm)
                        if e == 1:
                            e_o.wait(eng, u, back=1)
                        if e >= 1:
                            for k in range(KC):
                                e_hl.wait(eng, u, KC * (e - 1) + k)
                                for o in range(KC):
                                    mm = product(eng, acc[o][:, :], 1, e - 1, k, o,
                                                 hb_hi[:, (e - 1) % 2, k, :],
                                                 hb_lo[:, (e - 1) % 2, k, :],
                                                 e == 1 and k == 0, e == E and k == KC - 1)
                            e_w2.inc_by(mm)
                if name == "act":
                    eng.wait_ge(e_lw[h].sem, b * (16 * KTOP) + 16 * KTOP)
                    for e in range(E):
                        e_hc.wait(eng, u, KC * e + KC - 1, back=1)
                        e_cb.inc_by(eng.activation(cf[:, e, :], wb[:, h, 0, :], ACT.Copy,
                                                   scale=pres[:, 0, e:e + 1]))
                    for e in range(E):
                        if e >= 2:
                            e_w2.wait(eng, u, e - 2)
                        else:
                            e_w2.wait(eng, u, E - 2 + e, back=1)
                        for m in range(KC + 1):
                            if m < KC:
                                q = KC * e + m
                                e_w1.wait(eng, u, q)
                                e_rl.inc_by(eng.activation(hb[:, e % 2, m, :], hbank[q % 4][:, :],
                                                           ACT.Relu, bias=consts.b1[:, e, m:m + 1]))
                            if m:
                                e_hc.wait(eng, u, KC * e + m - 1)
                                e_hh.inc_by(eng.activation(hb_hi[:, e % 2, m - 1, :],
                                                           hb[:, e % 2, m - 1, :], ACT.Copy))
                        if e == 2 and following:
                            normalise(eng, name, *following)
                if name == "dve":
                    for e in range(E):
                        e_cb.wait(eng, u, e)
                        e_cf.inc_by(eng.scalar_tensor_tensor(
                            out=cf[:, e, :], in0=wb[:, h, 1, :], scalar=pres[:, 1, e:e + 1],
                            in1=cf[:, e, :], op0=ALU.mult, op1=ALU.add))
                    for e in range(E):
                        e_cf.wait(eng, u, e)
                        for m in range(KC + 1):
                            if m < KC:
                                e_rl.wait(eng, u, KC * e + m)
                                e_hc.inc_by(eng.tensor_tensor(
                                    hb[:, e % 2, m, :], hb[:, e % 2, m, :], cf[:, e, :],
                                    ALU.mult))
                            if m:
                                e_hh.wait(eng, u, KC * e + m - 1)
                                hi = hb_hi[:, e % 2, m - 1, :].bitcast(F32)
                                e_hl.inc_by(eng.tensor_tensor(
                                    hb_lo[:, e % 2, m - 1, :], hb[:, e % 2, m - 1, :],
                                    hi, ALU.subtract))
                        if e == 0:
                            for k in range(KTOP):
                                for m in range(KC):
                                    if k:
                                        e_xs.wait(eng, u, m)
                                    else:
                                        e_ng.wait(eng, u, m)
                                    e_xs.inc_by(eng.scalar_tensor_tensor(
                                        out=xb[:, h, m, :], in0=wb[:, h, k, :],
                                        scalar=b2k[:, k, m:m + 1],
                                        in1=xb[:, h, m, :],
                                        op0=ALU.mult, op1=ALU.add))
                        if e == 2 and following:
                            normalise(eng, name, *following)
                    e_w2.wait(eng, u)
                    for k in range(KC):
                        e_xs.wait(eng, u, KC + k)
                        e_o.inc_by(eng.tensor_tensor(xb[:, h, k, :], xb[:, h, k, :], acc[k][:, :],
                                                     ALU.add))
                if name == "store":
                    e_o.wait(eng, u)
                    dst = slice(h * T, (h + 1) * T)
                    e_so[h].inc_by(eng.dma_start(out_d[bass.ds(b, 1), :, :, dst].rearrange(
                        "o p k l -> (o p) k l"), xb[:, h, :, :]))

        def program(eng, name):
            normalise(eng, name, 0, 0)
            body(eng, name, 0, first=True)
            with eng.Fori(1, NB - 1) as b:
                body(eng, name, b)
            body(eng, name, NB - 1, last=True)

        with nc.Block() as block:
            @block.sync
            def _(eng):
                program(eng, "sync")

            @block.gpsimd
            def _(eng):
                program(eng, "store")
                for h in range(HALVES):
                    eng.wait_ge(e_so[h].sem, 16 * NB)

            @block.scalar
            def _(eng):
                program(eng, "act")

            @block.vector
            def _(eng):
                program(eng, "dve")

            @block.tensor
            def _(eng):
                program(eng, "pe")


def constants():
    c = np.arange(C)
    group = (c[:, None] // GN_CH == c[None, :] // GN_CH).astype(np.float32) / np.float32(GN_CH)
    return {
        "ident": np.eye(P, dtype=np.float32),
        "ones": np.ones((P, P), np.float32),
        "group": group.reshape(KC, P, C).transpose(1, 0, 2),
    }


def kernel(**inputs):
    import numpy as _np
    import concourse.bacc as _bacc
    from concourse.bass_utils import run_bass_kernel_spmd as _run

    v = {k: _np.asarray(x) for k, x in inputs.items()}

    def l0(name):
        return v["L0_conv_" + name]

    def l1(name):
        return v["L1_conv_" + name]

    def cols(x, k):
        return x.reshape(k, P, *x.shape[1:]).swapaxes(0, 1)
    w_m1 = l0("mlp_w1").reshape(KH // 2, 2, P, KC, P).transpose(0, 4, 1, 3, 2)
    w_m2 = l0("mlp_w2").reshape(KC, P, 2, KH // 2, P).transpose(0, 2, 4, 3, 1)
    arrays = {
        "x": v["x"].reshape(NB, C, L),
        "w_in": cols(l0("in_proj_w").T, KC),
        "w_xp": cols(l0("x_proj_w").T, KD),
        "w_dt": l0("dt_proj_w").T,
        "w_out": cols(l0("out_proj_w").T, KD),
        "w_m1": w_m1.reshape(KH // 2, P, 2 * KC * P),
        "w_m2": w_m2.reshape(2 * KC, P, KH // 2 * P),
        "conv_w": cols(l0("conv_w"), KD),
        "conv_b": cols(l0("conv_b"), KD),
        "dt_b": cols(l0("dt_proj_b"), KD),
        "D": cols(l0("D"), KD),
        "A_log": cols(l0("A_log"), KD),
        "ln_w": cols(l0("ln_w"), KC),
        "ln_b": cols(l0("ln_b"), KC),
        "mlp_b1": cols(l0("mlp_b1"), KH),
        "mlp_b2": cols(l0("mlp_b2"), KC),
        "w1e": l1("w1").reshape(E, C, KC, P).transpose(3, 0, 2, 1),
        "w2e": l1("w2").reshape(E, C, KC, P).transpose(3, 0, 2, 1),
        "b1e": l1("b1").reshape(E, KC, P).transpose(2, 0, 1),
        "b2e": l1("b2").reshape(E, KC, P).transpose(2, 1, 0),
        "gate_w": cols(l1("gate_w"), KC),
        "gate_b": l1("gate_b").reshape(1, E),
    }
    arrays.update(constants())
    nc = _bacc.Bacc("TRN2", target_bir_lowering=False, num_devices=1)
    feed, args = {}, {}
    for name, x in arrays.items():
        x = _np.ascontiguousarray(x)
        feed[f"in_{name}"] = x
        args[name] = nc.dram_tensor(f"in_{name}", x.shape, F32, kind="ExternalInput").ap()
    out = nc.dram_tensor("out_0", (NB, C, L), F32, kind="ExternalOutput").ap()
    build(nc, args, out)
    r = _run(nc, [feed], core_ids=[0])
    return r.results[0]["out_0"].reshape(v["x"].shape)
```
